# Optimizing a Trainium2 kernel written in Bass

```python
import numpy as np
import jax
import jax.numpy as jnp

def _softmax(x, axis=-1):
    return jax.nn.softmax(x, axis=axis)

def _gelu(x):
    return jax.nn.gelu(x, approximate=True)

def _silu(x):
    return jax.nn.silu(x)

def _sigmoid(x):
    return jax.nn.sigmoid(x)

def _layernorm(x, axis=-1, eps=1e-05):
    m = jnp.mean(x, axis=axis, keepdims=True)
    v = jnp.var(x, axis=axis, keepdims=True)
    return (x - m) / jnp.sqrt(v + eps)

def _scatter_add(tgt, idx, src, axis=0):
    return tgt.at[idx].add(src)

def _segment_sum(src, seg, n):
    return jax.ops.segment_sum(src, seg, n)
kernel_name = 'mk_recurrent_d2_jaxref_r8_1caeed'

def setup_inputs(seed: int=0):
    np.random.seed(seed)
    _w = jnp.asarray

    def _L0_attn_setup():
        import jax, jax.numpy as jnp
        import numpy as np
        D_MODEL = 128
        NUM_HEADS = 16
        HEAD_DIM = D_MODEL // NUM_HEADS
        key = jax.random.key(seed)
        ks = jax.random.split(key, 7)
        B, T, C = (4, 256, D_MODEL)
        s = 1.0 / np.sqrt(C)
        return {'x': jax.random.normal(ks[0], (B, T, C), dtype=jnp.float32), 'ln_gamma': jnp.ones((C,), dtype=jnp.float32), 'ln_beta': jnp.zeros((C,), dtype=jnp.float32), 'w_qkv': jax.random.normal(ks[1], (C, 3 * C), dtype=jnp.float32) * s, 'b_qkv': jnp.zeros((3 * C,), dtype=jnp.float32), 'w_out': jax.random.normal(ks[2], (C, C), dtype=jnp.float32) * s, 'b_out': jnp.zeros((C,), dtype=jnp.float32)}
    _L0_attn_in = _L0_attn_setup()

    def _L0_ffn_setup():
        import jax, jax.numpy as jnp
        import numpy as np
        import math
        BETA = 0.9
        THRESHOLD = 1.0
        NUM_STEPS = 5
        ALPHA = 2.0

        @jax.custom_vjp
        def spike_fn(u):
            return (u > 0).astype(u.dtype)

        def _spike_fwd(u):
            return (spike_fn(u), u)

        def _spike_bwd(u, g):
            s = jnp.pi / 2.0 * ALPHA * u
            return (g * (ALPHA / 2.0) / (1.0 + s * s),)
        spike_fn.defvjp(_spike_fwd, _spike_bwd)
        key = jax.random.key(seed)
        k1, k2, k3 = jax.random.split(key, 3)
        n_embd = 128
        x = jax.random.normal(k1, (4, 256, n_embd), dtype=jnp.float32)
        W_fc = jax.random.normal(k2, (4 * n_embd, n_embd), dtype=jnp.float32) / math.sqrt(n_embd)
        W_proj = jax.random.normal(k3, (n_embd, 4 * n_embd), dtype=jnp.float32) / math.sqrt(4 * n_embd)
        return {'x': x, 'W_fc': W_fc, 'W_proj': W_proj}
    _L0_ffn_in = _L0_ffn_setup()

    def _L1_attn_setup():
        import math
        import jax, jax.numpy as jnp
        import numpy as np
        B, T, C, H = (1, 512, 128, 16)
        HD = C // H

        def get_slopes(n):

            def pow2(n):
                start = 2 ** (-2 ** (-(math.log2(n) - 3)))
                return [start * start ** i for i in range(n)]
            if math.log2(n).is_integer():
                return pow2(n)
            cp2 = 2 ** math.floor(math.log2(n))
            return pow2(cp2) + get_slopes(2 * cp2)[0::2][:n - cp2]
        key = jax.random.key(seed)
        ks = jax.random.split(key, 5)
        x = jax.random.normal(ks[0], (B, T, C), dtype=jnp.float32)
        mk = lambda k: 0.02 * jax.random.normal(k, (C, C), dtype=jnp.float32)
        return {'x': x, 'Wq': mk(ks[1]), 'bq': jnp.zeros((C,), jnp.float32), 'Wk': mk(ks[2]), 'bk': jnp.zeros((C,), jnp.float32), 'Wv': mk(ks[3]), 'bv': jnp.zeros((C,), jnp.float32), 'Wo': 0.02 / math.sqrt(24) * jax.random.normal(ks[4], (C, C), dtype=jnp.float32), 'bo': jnp.zeros((C,), jnp.float32)}
    _L1_attn_in = _L1_attn_setup()

    def _L1_ffn_setup():
        import jax, jax.numpy as jnp
        import numpy as np
        B, S, DIM = (4, 512, 128)
        BASE_COUPLING = 0.1
        NUM_CYCLES = 3

        def _gelu(x):
            return jax.nn.gelu(x, approximate=False)

        def _coupling_net(h, w1, b1, w2, b2, w3, b3, w4, b4):
            h = _gelu(h @ w1 + b1)
            h = _gelu(h @ w2 + b2)
            h = _gelu(h @ w3 + b3)
            return jax.nn.sigmoid(h @ w4 + b4)

        def _global_net(h, w1, b1, w2, b2, w3, b3):
            h = _gelu(h @ w1 + b1)
            h = _gelu(h @ w2 + b2)
            return jax.nn.sigmoid(h @ w3 + b3)

        def _twist(x):
            o_r, o_i, p_r, p_i = jnp.split(x, 4, axis=-1)
            return jnp.concatenate([p_r, -p_i, -o_r, o_i], axis=-1)
        key = jax.random.key(seed)
        ks = jax.random.split(key, 9)
        d = DIM

        def w(k, fan_in, fan_out):
            return jax.random.normal(k, (fan_in, fan_out), dtype=jnp.float32) / np.sqrt(fan_in).astype(np.float32)
        inp = {'x': jax.random.normal(ks[0], (B, S, d), dtype=jnp.float32)}
        cn_dims = [(d, d), (d, d // 2), (d // 2, d // 4), (d // 4, 1)]
        for i, (a, b) in enumerate(cn_dims):
            inp[f'cn_w{i + 1}'] = w(ks[1 + i], a, b)
            inp[f'cn_b{i + 1}'] = jnp.zeros((b,), dtype=jnp.float32)
        gc_dims = [(d, d // 2), (d // 2, d // 4), (d // 4, 1)]
        for i, (a, b) in enumerate(gc_dims):
            inp[f'gc_w{i + 1}'] = w(ks[5 + i], a, b)
            inp[f'gc_b{i + 1}'] = jnp.zeros((b,), dtype=jnp.float32)
        inp['adaptive_range'] = jnp.full((1,), 0.2, dtype=jnp.float32)
        return inp
    _L1_ffn_in = _L1_ffn_setup()
    _d = {'L0_attn_x': _L0_attn_in['x'], 'L0_attn_ln_gamma': _L0_attn_in['ln_gamma'], 'L0_attn_ln_beta': _L0_attn_in['ln_beta'], 'L0_attn_w_qkv': _L0_attn_in['w_qkv'], 'L0_attn_b_qkv': _L0_attn_in['b_qkv'], 'L0_attn_w_out': _L0_attn_in['w_out'], 'L0_attn_b_out': _L0_attn_in['b_out'], 'L0_ffn_W_fc': _L0_ffn_in['W_fc'], 'L0_ffn_W_proj': _L0_ffn_in['W_proj'], 'L1_attn_Wq': _L1_attn_in['Wq'], 'L1_attn_bq': _L1_attn_in['bq'], 'L1_attn_Wk': _L1_attn_in['Wk'], 'L1_attn_bk': _L1_attn_in['bk'], 'L1_attn_Wv': _L1_attn_in['Wv'], 'L1_attn_bv': _L1_attn_in['bv'], 'L1_attn_Wo': _L1_attn_in['Wo'], 'L1_attn_bo': _L1_attn_in['bo'], 'L1_ffn_cn_w1': _L1_ffn_in['cn_w1'], 'L1_ffn_cn_b1': _L1_ffn_in['cn_b1'], 'L1_ffn_cn_w2': _L1_ffn_in['cn_w2'], 'L1_ffn_cn_b2': _L1_ffn_in['cn_b2'], 'L1_ffn_cn_w3': _L1_ffn_in['cn_w3'], 'L1_ffn_cn_b3': _L1_ffn_in['cn_b3'], 'L1_ffn_cn_w4': _L1_ffn_in['cn_w4'], 'L1_ffn_cn_b4': _L1_ffn_in['cn_b4'], 'L1_ffn_gc_w1': _L1_ffn_in['gc_w1'], 'L1_ffn_gc_b1': _L1_ffn_in['gc_b1'], 'L1_ffn_gc_w2': _L1_ffn_in['gc_w2'], 'L1_ffn_gc_b2': _L1_ffn_in['gc_b2'], 'L1_ffn_gc_w3': _L1_ffn_in['gc_w3'], 'L1_ffn_gc_b3': _L1_ffn_in['gc_b3'], 'L1_ffn_adaptive_range': _L1_ffn_in['adaptive_range']}
    _x0 = _d['L0_attn_x']
    _d['L0_attn_x'] = jax.random.normal(jax.random.fold_in(jax.random.key(seed), 1), (4, 1024, 128), dtype=_x0.dtype)
    del _x0
    return _d

def reference(L0_attn_x, L0_attn_ln_gamma, L0_attn_ln_beta, L0_attn_w_qkv, L0_attn_b_qkv, L0_attn_w_out, L0_attn_b_out, L0_ffn_W_fc, L0_ffn_W_proj, L1_attn_Wq, L1_attn_bq, L1_attn_Wk, L1_attn_bk, L1_attn_Wv, L1_attn_bv, L1_attn_Wo, L1_attn_bo, L1_ffn_cn_w1, L1_ffn_cn_b1, L1_ffn_cn_w2, L1_ffn_cn_b2, L1_ffn_cn_w3, L1_ffn_cn_b3, L1_ffn_cn_w4, L1_ffn_cn_b4, L1_ffn_gc_w1, L1_ffn_gc_b1, L1_ffn_gc_w2, L1_ffn_gc_b2, L1_ffn_gc_w3, L1_ffn_gc_b3, L1_ffn_adaptive_range):

    def _L0_attn_ref(x, ln_gamma, ln_beta, w_qkv, b_qkv, w_out, b_out):
        import jax, jax.numpy as jnp
        import numpy as np
        D_MODEL = 128
        NUM_HEADS = 16
        HEAD_DIM = D_MODEL // NUM_HEADS
        B, T, C = x.shape
        residual = x
        mu = jnp.mean(x, axis=-1, keepdims=True)
        var = jnp.var(x, axis=-1, keepdims=True)
        h = (x - mu) * jax.lax.rsqrt(var + 1e-05) * ln_gamma + ln_beta
        qkv = (h @ w_qkv + b_qkv).reshape(B, T, 3, NUM_HEADS, HEAD_DIM)
        qkv = jnp.transpose(qkv, (2, 0, 3, 1, 4))
        q, k, v = (qkv[0], qkv[1], qkv[2])
        scores = jnp.einsum('bhqd,bhkd->bhqk', q, k) / np.sqrt(HEAD_DIM)
        attn = jax.nn.softmax(scores, axis=-1)
        out = jnp.einsum('bhqk,bhkd->bhqd', attn, v)
        out = jnp.transpose(out, (0, 2, 1, 3)).reshape(B, T, C)
        out = out @ w_out + b_out
        return residual + out

    def _L0_ffn_ref(x, W_fc, W_proj):
        import jax, jax.numpy as jnp
        import numpy as np
        import math
        BETA = 0.9
        THRESHOLD = 1.0
        NUM_STEPS = 5
        ALPHA = 2.0

        @jax.custom_vjp
        def spike_fn(u):
            return (u > 0).astype(u.dtype)

        def _spike_fwd(u):
            return (spike_fn(u), u)

        def _spike_bwd(u, g):
            s = jnp.pi / 2.0 * ALPHA * u
            return (g * (ALPHA / 2.0) / (1.0 + s * s),)
        spike_fn.defvjp(_spike_fwd, _spike_bwd)
        h = jnp.square(jax.nn.relu(jnp.einsum('bsd,fd->bsf', x, W_fc)))
        y = jnp.einsum('bsf,df->bsd', h, W_proj)

        def step(mem, _):
            reset = jax.lax.stop_gradient(spike_fn(mem - THRESHOLD))
            mem_new = BETA * mem + y - reset * THRESHOLD
            spk = spike_fn(mem_new - THRESHOLD)
            return (mem_new, spk)
        mem0 = jnp.zeros_like(y)
        _, spks = jax.lax.scan(step, mem0, None, length=NUM_STEPS)
        return jnp.sum(spks, axis=0) / NUM_STEPS

    def _L1_attn_ref(x, Wq, bq, Wk, bk, Wv, bv, Wo, bo):
        import math
        import jax, jax.numpy as jnp
        import numpy as np
        B, T, C, H = (1, 512, 128, 16)
        HD = C // H

        def get_slopes(n):

            def pow2(n):
                start = 2 ** (-2 ** (-(math.log2(n) - 3)))
                return [start * start ** i for i in range(n)]
            if math.log2(n).is_integer():
                return pow2(n)
            cp2 = 2 ** math.floor(math.log2(n))
            return pow2(cp2) + get_slopes(2 * cp2)[0::2][:n - cp2]
        b, t, c = x.shape
        proj = lambda W, bias: (x @ W + bias).reshape(b, t, H, HD).transpose(0, 2, 1, 3)
        q, k, v = (proj(Wq, bq), proj(Wk, bk), proj(Wv, bv))
        scale = 1.0 / jnp.sqrt(jnp.asarray(HD, x.dtype))
        attn = jnp.einsum('bhqd,bhkd->bhqk', q, k) * scale
        slopes = jnp.asarray(get_slopes(H), dtype=x.dtype)
        alibi = -slopes[:, None, None] * (t - 1 - jnp.arange(t, dtype=x.dtype))[None, None, :]
        attn = attn + alibi
        causal = jnp.tril(jnp.ones((t, t), dtype=bool))[None, None]
        attn = jnp.where(causal, attn, jnp.finfo(x.dtype).min)
        p = jax.nn.softmax(attn, axis=-1)
        out = jnp.einsum('bhqk,bhkd->bhqd', p, v).transpose(0, 2, 1, 3).reshape(b, t, c)
        return out @ Wo + bo

    def _L1_ffn_ref(x, cn_w1, cn_b1, cn_w2, cn_b2, cn_w3, cn_b3, cn_w4, cn_b4, gc_w1, gc_b1, gc_w2, gc_b2, gc_w3, gc_b3, adaptive_range):
        import jax, jax.numpy as jnp
        import numpy as np
        B, S, DIM = (4, 512, 128)
        BASE_COUPLING = 0.1
        NUM_CYCLES = 3

        def _gelu(x):
            return jax.nn.gelu(x, approximate=False)

        def _coupling_net(h, w1, b1, w2, b2, w3, b3, w4, b4):
            h = _gelu(h @ w1 + b1)
            h = _gelu(h @ w2 + b2)
            h = _gelu(h @ w3 + b3)
            return jax.nn.sigmoid(h @ w4 + b4)

        def _global_net(h, w1, b1, w2, b2, w3, b3):
            h = _gelu(h @ w1 + b1)
            h = _gelu(h @ w2 + b2)
            return jax.nn.sigmoid(h @ w3 + b3)

        def _twist(x):
            o_r, o_i, p_r, p_i = jnp.split(x, 4, axis=-1)
            return jnp.concatenate([p_r, -p_i, -o_r, o_i], axis=-1)
        global_context = x.mean(axis=1, keepdims=True)
        gf = _global_net(global_context, gc_w1, gc_b1, gc_w2, gc_b2, gc_w3, gc_b3)
        out = x
        for _ in range(NUM_CYCLES):
            tf = _coupling_net(out, cn_w1, cn_b1, cn_w2, cn_b2, cn_w3, cn_b3, cn_w4, cn_b4)
            combined = 0.7 * gf + 0.3 * tf
            coupling = BASE_COUPLING + adaptive_range * (combined - 0.5) * 2.0
            out = out + coupling * _twist(out)
        return out
    x = L0_attn_x
    xn = _layernorm(x, axis=-1)
    s = _L0_attn_ref(xn, L0_attn_ln_gamma, L0_attn_ln_beta, L0_attn_w_qkv, L0_attn_b_qkv, L0_attn_w_out, L0_attn_b_out)
    g = _silu(_L0_ffn_ref(xn, L0_ffn_W_fc, L0_ffn_W_proj))
    x = x + s * g
    xn = _layernorm(x, axis=-1)
    s = _L1_attn_ref(xn, L1_attn_Wq, L1_attn_bq, L1_attn_Wk, L1_attn_bk, L1_attn_Wv, L1_attn_bv, L1_attn_Wo, L1_attn_bo)
    g = _silu(_L1_ffn_ref(xn, L1_ffn_cn_w1, L1_ffn_cn_b1, L1_ffn_cn_w2, L1_ffn_cn_b2, L1_ffn_cn_w3, L1_ffn_cn_b3, L1_ffn_cn_w4, L1_ffn_cn_b4, L1_ffn_gc_w1, L1_ffn_gc_b1, L1_ffn_gc_w2, L1_ffn_gc_b2, L1_ffn_gc_w3, L1_ffn_gc_b3, L1_ffn_adaptive_range))
    x = x + s * g
    return x

_drawn_inputs = setup_inputs


def setup_inputs(seed=0):
    import zlib

    import numpy as np

    out = dict(_drawn_inputs(seed))
    spreads = {'L0_attn_ln_gamma': (1.0, 0.6),
     'L0_attn_ln_beta': (0.0, 0.291),
     'L0_attn_b_qkv': (0.0, 0.279),
     'L0_attn_b_out': (0.0, 0.296),
     'L1_attn_bq': (0.0, 0.8),
     'L1_attn_bk': (0.0, 2.0),
     'L1_attn_bv': (0.0, 0.8),
     'L1_attn_bo': (0.0, 0.1),
     'L1_ffn_cn_b1': (0.0, 2.0),
     'L1_ffn_cn_b2': (0.0, 2.0),
     'L1_ffn_cn_b3': (0.0, 2.0),
     'L1_ffn_gc_b1': (0.0, 0.8),
     'L1_ffn_gc_b2': (0.0, 0.8)}
    factors = {'L1_attn_Wq': 8.0,
     'L1_attn_Wk': 8.0,
     'L1_attn_Wv': 8.0,
     'L1_attn_Wo': 8.0,
     'L1_ffn_cn_w1': 8.0,
     'L1_ffn_cn_w2': 8.0,
     'L1_ffn_cn_w3': 8.0,
     'L1_ffn_cn_w4': 8.0,
     'L1_ffn_gc_w1': 8.0,
     'L1_ffn_gc_w2': 8.0,
     'L1_ffn_gc_w3': 64.0}
    for name, (base, spread) in spreads.items():
        noise = np.random.default_rng([zlib.crc32(name.encode()), seed]).standard_normal(out[name].shape)
        drawn = base * np.exp(spread * noise) if base else spread * noise
        out[name] = jnp.asarray(drawn.astype(out[name].dtype))
    for name, factor in factors.items():
        out[name] = (out[name] * factor).astype(out[name].dtype)
    return out
```

```python
from contextlib import ExitStack

import numpy as np

import concourse.bass as bass
from concourse import mybir

F32 = mybir.dt.float32
BF16 = mybir.dt.bfloat16
I32 = mybir.dt.int32
ALU = mybir.AluOpType
ACT = mybir.ActivationFunctionType
AX = mybir.AxisListType

P = 128
B, T, C = 4, 1024, 128
H, D = 16, 8
N = B * T
NT = N // P
BT = T // P
HALF = 512
HT = HALF // P
G = 4
NG = H // G
FF = 512
FC = FF // P
SCALE = float(D) ** -0.5
EPS = 1e-5
Q_PARTS = (0, 0, 0, 1, 1, 2)
K_PARTS = (0, 1, 2, 0, 1, 0)
SPLIT_ROWS = D * len(Q_PARTS)
ROWS = 64
VW = 16
BOUND = 60.0
STEPS = 5
BETA = 0.9
MASK = -1.0e30
CYCLES = 3


class Semaphores:

    def __init__(self, nc, ctx, prefix):
        self.nc, self.ctx, self.prefix, self.all = nc, ctx, prefix, []

    def __call__(self, name):
        self.all.append(self.ctx.enter_context(self.nc.semaphore(f"{self.prefix}{name}")))
        return self.all[-1]

    def pair(self, name):
        return self.many(name, 2)

    def many(self, name, n):
        return [self(f"{name}{k}") for k in range(n)]

    def wiped(self):
        ids = sorted(h.num for h in self.all)
        firsts = [n for n in ids if n - 1 not in ids]
        with self.nc.Block() as block:
            @block.sync
            def _(sp):
                for n in firsts:
                    end = next(m for m in range(n, n + len(ids) + 1) if m not in ids)
                    sp.sem_clear(range(n, end))


def now(eng, sem, i, hf, m=1):
    eng.wait_ge(sem[hf], m * i + m)


def before(eng, sem, i, hf, m=1):
    eng.wait_ge(sem[1 - hf], m * i + m * hf)


def last_trip(eng, sem, i, hf, m=1):
    eng.wait_ge(sem[hf], m * i)


class Chain:

    def __init__(self, eng, sem, base=0):
        self.eng, self.sem, self.base, self.n = eng, sem, base, 0

    def mark(self, ins):
        self.n += 1
        ins.then_inc(self.sem, 1)

    def wait(self):
        self.eng.wait_ge(self.sem, self.base + self.n)

    def after(self, ins):
        self.mark(ins)
        self.wait()


def build(nc, a):
    x_t = a["L0_attn_x"].rearrange("b (t p) c -> p (b t) c", p=P)
    out_t = a["out"].rearrange("b (t p) c -> p (b t) c", p=P)
    q_rows = [nc.dram_tensor(f"q_rows{n}", [ROWS, H, N], BF16).ap() for n in range(2)]
    k_rows = [nc.dram_tensor(f"k_rows{n}", [ROWS, H, N], BF16).ap() for n in range(2)]
    sums = nc.dram_tensor("head_sums", [2 + B * NG, P, T], F32).ap()

    with ExitStack() as ctx:
        def sb(name, shape, dt=F32):
            return ctx.enter_context(nc.sbuf_tensor(name, shape, dt))

        s = {
            "ident": sb("ident", [P, P]), "ident_bf": sb("ident_bf", [P, P], BF16),
            "mask_kq": sb("mask_kq", [P, P], BF16),
            "mask_qk": sb("mask_qk", [P, P], BF16),
            "x": sb("x", [P, NT, C]),
            "xn": sb("xn", [P, NT, C]),
            "y": sb("y", [P, NT, C]),
            "v": sb("v", [P, NT, H, VW]),
            "mean": sb("mean", [P, NT]), "rstd": sb("rstd", [P, NT]),
            "flag": sb("flag", [1, 1], I32),
            "wo": sb("wo", [P, 2, C]),
            "bo": sb("bo", [P, 2, C]),
        }
        setup(nc, a, s, q_rows, k_rows)
        layernorm(nc, s, "outer", s["x"], x_t, True)
        layernorm(nc, s, "inner", s["xn"], None, False)
        prepare(nc, a, s, 0, q_rows[0], k_rows[0])
        row_maxima(nc, a, s, 0, q_rows[0], k_rows[0])
        attention(nc, s, 0, q_rows[0], k_rows[0], sums)
        combine(nc, a, s, 0, sums, None)
        layernorm(nc, s, "second", s["x"], None, False)
        prepare(nc, a, s, 1, q_rows[1], k_rows[1])
        coupling(nc, a, s)
        row_maxima(nc, a, s, 1, q_rows[1], k_rows[1])
        attention(nc, s, 1, q_rows[1], k_rows[1], sums)
        combine(nc, a, s, 1, sums, out_t)


def setup(nc, a, s, q_rows, k_rows):
    with ExitStack() as ctx:
        bo_row = ctx.enter_context(nc.sbuf_tensor("bo_row", [1, 2, C], F32))
        ones = ctx.enter_context(nc.sbuf_tensor("su_ones", [1, P], F32))
        ps = ctx.enter_context(nc.psum_tensor("su_ps", [P, 2, C], F32))
        sem = Semaphores(nc, ctx, "su_")
        zero = sem("zero")
        idn = sem("ident")
        load = sem("load")
        rows = sem("rows")
        done = sem("bcast")
        vec = sem("vec")
        with nc.Block() as block:
            @block.sync
            def _(sp):
                sp.dma_start(bo_row[:, 0, :], a["L0_attn_b_out"].rearrange("(o c) -> o c", o=1)).then_inc(load, 16)
                sp.dma_start(bo_row[:, 1, :], a["L1_attn_bo"].rearrange("(o c) -> o c", o=1)).then_inc(load, 16)
                sp.dma_start(s["wo"][:, 0, :], a["L0_attn_w_out"]).then_inc(load, 16)
                sp.dma_start(s["wo"][:, 1, :], a["L1_attn_Wo"]).then_inc(load, 16)
                for n in range(2):
                    for b in range(B):
                        tok = slice(b * T, (b + 1) * T)
                        sp.dma_start(q_rows[n][SPLIT_ROWS:ROWS, :, tok], a["q_extra"][n].bitcast(BF16)).then_inc(rows, 16)
                        sp.dma_start(k_rows[n][SPLIT_ROWS:ROWS, :, tok], a["k_extra"][n].bitcast(BF16)).then_inc(rows, 16)
                sp.wait_ge(load, 64)
                sp.wait_ge(rows, 16 * 2 * B * 2)

            @block.gpsimd
            def _(pool):
                pool.memset(s["ident"][:, :], 0.0).then_inc(zero, 1)
                pool.wait_ge(zero, 1)
                pool.affine_select(out=s["ident"][:, :], in_=s["ident"][:, :], compare_op=ALU.not_equal, fill=1.0,
                                   base=0, pattern=[[-1, P]], channel_multiplier=1).then_inc(idn, 1)
                pool.wait_ge(idn, 1)
                pool.tensor_copy(s["ident_bf"][:, :], s["ident"][:, :]).then_inc(idn, 1)
                for mask, sign in ((s["mask_kq"], 1), (s["mask_qk"], -1)):
                    pool.memset(mask[:, :], 0.0).then_inc(zero, 1)
                pool.wait_ge(zero, 3)
                for mask, sign in ((s["mask_kq"], 1), (s["mask_qk"], -1)):
                    pool.affine_select(out=mask[:, :], in_=mask[:, :], compare_op=ALU.is_ge, fill=MASK, base=0,
                                       pattern=[[sign, P]], channel_multiplier=-sign).then_inc(idn, 1)

            @block.vector
            def _(dve):
                nc.vector.memset(ones[:, :], 1.0).then_inc(vec, 1)
                nc.vector.memset(s["v"][:, :, :, D + 1:VW], 0.0)
                nc.vector.memset(s["v"][:, :, :, D:D + 1], 1.0)
                dve.wait_ge(done, 1)
                nc.vector.tensor_copy(s["bo"][:, :, :], ps[:, :, :]).then_inc(vec, 1)

            @block.tensor
            def _(pe):
                pe.wait_ge(load, 64)
                pe.wait_ge(vec, 1)
                nc.tensor.matmul(ps[:, :, :], ones[:, :], bo_row[:, :, :], start=True, stop=True).then_inc(done, 1)
        sem.wiped()


def layernorm(nc, s, tag, src, x_t, apply):
    with ExitStack() as ctx:
        st = ctx.enter_context(nc.sbuf_tensor(f"{tag}_st", [P, NT, 6], F32))
        mv = ctx.enter_context(nc.sbuf_tensor(f"{tag}_mv", [P, NT, 2], F32))
        tmp = [ctx.enter_context(nc.sbuf_tensor(f"{tag}_t{k}", [P, NT], F32)) for k in range(3)]
        sem = Semaphores(nc, ctx, f"{tag}_")
        load = sem.many("load", B)
        var, root, step = sem("var"), sem("root"), sem("step")
        with nc.Block() as block:
            @block.sync
            def _(sp):
                if x_t is not None:
                    for b in range(B):
                        sp.dma_start(src[:, b * BT:(b + 1) * BT, :], x_t[:, b * BT:(b + 1) * BT, :]).then_inc(load[b], 16)

            @block.scalar
            def _(act):
                act.wait_ge(var, 1)
                nc.scalar.activation(tmp[1][:, :], tmp[0][:, :], ACT.Sqrt).then_inc(root, 1)

            @block.vector
            def _(dve):
                ch = Chain(dve, step)
                for b in range(B):
                    if x_t is not None:
                        dve.wait_ge(load[b], 16)
                    for t in range(b * BT, (b + 1) * BT):
                        ch.mark(nc.vector.bn_stats(st[:, t, :], src[:, t, :]))
                ch.wait()
                for t in range(NT):
                    ch.mark(nc.vector.bn_aggr(mv[:, t, :], st[:, t, :]))
                ch.wait()
                ch.mark(nc.vector.tensor_copy(s["mean"][:, :], mv[:, :, 0]))
                nc.vector.tensor_scalar_add(tmp[0][:, :], mv[:, :, 1], EPS).then_inc(var, 1)
                dve.wait_ge(root, 1)
                ch.after(nc.vector.reciprocal(tmp[1][:, :], tmp[1][:, :]))
                ch.after(nc.vector.tensor_tensor(tmp[2][:, :], tmp[1][:, :], tmp[1][:, :], ALU.mult))
                ch.after(nc.vector.tensor_tensor(tmp[2][:, :], tmp[2][:, :], tmp[0][:, :], ALU.mult))
                ch.after(nc.vector.tensor_scalar(tmp[2][:, :], tmp[2][:, :], -0.5, 1.5, ALU.mult, ALU.add))
                ch.after(nc.vector.tensor_tensor(s["rstd"][:, :], tmp[1][:, :], tmp[2][:, :], ALU.mult))
                if apply:
                    for t in range(NT):
                        ch.mark(nc.vector.tensor_scalar(s["xn"][:, t, :], src[:, t, :], s["mean"][:, t:t + 1],
                                                        s["rstd"][:, t:t + 1], ALU.subtract, ALU.mult))
        sem.wiped()


def prepare(nc, a, s, layer, q_rows, k_rows):
    first = layer == 0
    with ExitStack() as ctx:
        def sb(name, shape, dt=F32):
            return ctx.enter_context(nc.sbuf_tensor(f"p{layer}_{name}", shape, dt))

        def ps(name, shape=(P, HALF)):
            return ctx.enter_context(nc.psum_tensor(f"p{layer}_{name}", list(shape), F32))

        sem = Semaphores(nc, ctx, f"p{layer}_")

        w = sb("w", [P, 3, C])
        wqk = sb("wqk", [P, 2, C])
        b_row = sb("b_row", [1, 3, C])
        bqk_row = sb("bqk_row", [1, 2, C])
        b_col = sb("b_col", [P, 2])
        bv = sb("bv", [P, HT, C])
        norm_col = sb("norm_col", [P, 2])
        ones = sb("ones", [1, P])
        head_of = sb("head_of", [P, H], BF16)
        xs = [sb(f"xs{hf}", [P, HT, C]) for hf in range(2)]
        hs = [sb(f"hs{hf}", [P, HT, C]) for hf in range(2)] if first else xs
        x_ch = [sb(f"x_ch{hf}", [P, HALF]) for hf in range(2)]
        h_ch = [sb(f"h_ch{hf}", [P, HALF]) for hf in range(2)] if first else x_ch
        qk = [sb(f"qk{hf}", [P, 2, HALF]) for hf in range(2)]
        rest = sb("rest", [P, 2, HALF])
        parts = [sb(f"parts{hf}", [P, 2, 3, HALF], BF16) for hf in range(2)]
        square = [sb(f"square{hf}", [P, 2, HALF], BF16) for hf in range(2)]
        norms = sb("norms", [H, 2, 2 * B])
        top = sb("top", [H, 4])
        peak = sb("peak", [1, 1])
        if first:
            fc = sb("fc", [P, FC, C])
            proj = sb("proj", [P, FF])
            fc_t = sb("fc_t", [P, FC, P])
            proj_t = sb("proj_t", [P, FC, C])
            relu = sb("relu", [P, FC, HALF])
            hidden = sb("hidden", [P, FC, HALF])

        tr_x, tr_h, pq, pk, pv = ps("tr_x"), ps("tr_h"), ps("pq"), ps("pk"), ps("pv")
        pf = [ps("pf0"), ps("pf1")]
        py = ps("py")

        w_in, ffn_in, const, perm, bias_ps, wt_ps, wt_in = (sem(x) for x in (
            "w_in", "ffn_in", "const", "perm", "bias_ps", "wt_ps", "wt_in"))
        bias_in, tail, tail_ps, chain = sem("bias_in"), sem("tail"), sem("tail_ps"), sem("chain")
        xs_rdy, hs_rdy, trx_rdy, trh_rdy, xch_rdy, hch_rdy = (sem.pair(x) for x in (
            "xs_rdy", "hs_rdy", "trx_rdy", "trh_rdy", "xch_rdy", "hch_rdy"))
        q_rdy, k_rdy, v_rdy, qk_in, v_in, parts_rdy, stored = (sem.pair(x) for x in (
            "q_rdy", "k_rdy", "v_rdy", "qk_in", "v_in", "parts_rdy", "stored"))
        sq_rdy, norm_ps, norm_in, f_rdy, relu_in, hid_rdy, y_rdy, y_in = (sem.pair(x) for x in (
            "sq_rdy", "norm_ps", "norm_in", "f_rdy", "relu_in", "hid_rdy", "y_rdy", "y_in"))
        if not first:
            hs_rdy, trh_rdy, hch_rdy = xs_rdy, trx_rdy, xch_rdy
        HALF_STEPS = 4

        with nc.Block() as block:
            @block.sync
            def _(sp):
                if first:
                    sp.dma_start(w[:, :, :], a["L0_attn_w_qkv"].rearrange("k (n c) -> k n c", n=3)).then_inc(w_in, 16)
                    sp.dma_start(b_row[:, :, :], a["L0_attn_b_qkv"].rearrange("(o n c) -> o n c", o=1, n=3)).then_inc(w_in, 16)
                    sp.dma_start(norm_col[:, 0:1], a["L0_attn_ln_gamma"].rearrange("(c o) -> c o", o=1)).then_inc(w_in, 16)
                    sp.dma_start(norm_col[:, 1:2], a["L0_attn_ln_beta"].rearrange("(c o) -> c o", o=1)).then_inc(w_in, 16)
                    sp.dma_start(fc[:, :, :], a["L0_ffn_W_fc"].rearrange("(n f) c -> f n c", f=P)).then_inc(ffn_in, 16)
                    sp.dma_start(proj[:, :], a["L0_ffn_W_proj"]).then_inc(ffn_in, 16)
                else:
                    for n, name in enumerate("qkv"):
                        sp.dma_start(w[:, n, :], a[f"L1_attn_W{name}"]).then_inc(w_in, 16)
                        sp.dma_start(b_row[:, n, :], a[f"L1_attn_b{name}"].rearrange("(o c) -> o c", o=1)).then_inc(w_in, 16)
                with sp.Fori(0, B) as i:
                    for hf in range(2):
                        now(sp, parts_rdy, i, hf)
                        tok = bass.ds(T * i + HALF * hf, HALF)
                        for r in range(len(Q_PARTS)):
                            rows = slice(D * r, D * r + D)
                            sp.dma_start(q_rows[rows, :, tok].rearrange("d h t -> (d h) t"),
                                         parts[hf][:, 0, Q_PARTS[r], :]).then_inc(stored[hf], 16)
                            sp.dma_start(k_rows[rows, :, tok].rearrange("d h t -> (d h) t"),
                                         parts[hf][:, 1, K_PARTS[r], :]).then_inc(stored[hf], 16)
                for hf in range(2):
                    sp.wait_ge(stored[hf], 192 * B)

            @block.gpsimd
            def _(pool):
                pool.wait_ge(const, 1)
                for d in range(D):
                    pool.affine_select(out=head_of[:, :], in_=head_of[:, :], compare_op=ALU.not_equal, fill=1.0,
                                       base=-H * d, pattern=[[-1, H]], channel_multiplier=1).then_inc(perm, 1)
                    pool.wait_ge(perm, d + 1)
                with pool.Fori(0, B) as i:
                    for hf in range(2):
                        if first:
                            last_trip(pool, trx_rdy, i, hf)
                            pool.tensor_copy(xs[hf][:, :, :], s["xn"][:, bass.ds(BT * i + HT * hf, HT), :]).then_inc(xs_rdy[hf], 1)
                            last_trip(pool, y_rdy, i, hf)
                            before(pool, y_rdy, i, hf)
                            for f in range(FC):
                                pool.wait_ge(relu_in[hf], FC * i + f + 1)
                                pool.tensor_tensor(hidden[:, f, :], relu[:, f, :], relu[:, f, :], ALU.mult).then_inc(hid_rdy[hf], 1)
                        else:
                            now(pool, xch_rdy, i, hf)
                            pool.tensor_copy(s["y"][:, bass.ds(BT * i + HT * hf, HT), :],
                                             x_ch[hf][:, :].rearrange("p (t c) -> p t c", c=C)).then_inc(y_in[hf], 1)

            @block.scalar
            def _(act):
                with act.Fori(0, B) as i:
                    for hf in range(2):
                        now(act, trx_rdy, i, hf)
                        last_trip(act, v_rdy, i, hf)
                        if first:
                            last_trip(act, f_rdy, i, hf, FC)
                        else:
                            last_trip(act, y_in, i, hf)
                        nc.scalar.copy(x_ch[hf][:, :], tr_x[:, :]).then_inc(xch_rdy[hf], 1)
                        if first:
                            now(act, trh_rdy, i, hf)
                            nc.scalar.activation(h_ch[hf][:, :], tr_h[:, :], ACT.Identity, bias=norm_col[:, 1:2],
                                                 scale=norm_col[:, 0:1]).then_inc(hch_rdy[hf], 1)
                        now(act, q_rdy, i, hf)
                        act.wait_ge(bias_in, 1)
                        last_trip(act, parts_rdy, i, hf)
                        nc.scalar.activation(qk[hf][:, 0, :], pq[:, :], ACT.Identity, bias=b_col[:, 0:1],
                                             scale=SCALE).then_inc(qk_in[hf], 1)
                        now(act, k_rdy, i, hf)
                        nc.scalar.activation(qk[hf][:, 1, :], pk[:, :], ACT.Identity, bias=b_col[:, 1:2]).then_inc(qk_in[hf], 1)
                        last_trip(act, norm_ps, i, hf)
                        now(act, qk_in, i, hf, 2)
                        nc.scalar.activation(square[hf][:, :, :], qk[hf][:, :, :], ACT.Square).then_inc(sq_rdy[hf], 1)
                        if first:
                            for f in range(FC):
                                act.wait_ge(f_rdy[hf], FC * i + f + 1)
                                before(act, hid_rdy, i, hf, FC)
                                nc.scalar.activation(relu[:, f, :], pf[f % 2][:, :], ACT.Relu).then_inc(relu_in[hf], 1)
                            now(act, y_rdy, i, hf)
                            nc.scalar.copy(s["y"][:, bass.ds(BT * i + HT * hf, HT), :],
                                           py[:, :].rearrange("p (t c) -> p t c", c=C)).then_inc(y_in[hf], 1)

            @block.vector
            def _(dve):
                nc.vector.memset(head_of[:, :], 0.0).then_inc(const, 1)
                nc.vector.memset(ones[:, :], 1.0).then_inc(const, 1)
                dve.wait_ge(w_in, 64 if first else 96)
                nc.vector.tensor_copy(wqk[:, :, :].rearrange("p n (d h) -> p n d h", h=H),
                                      w[:, 0:2, :].rearrange("p n (h d) -> p n d h", d=D))
                nc.vector.tensor_copy(bqk_row[:, :, :].rearrange("p n (d h) -> p n d h", h=H),
                                      b_row[:, 0:2, :].rearrange("p n (h d) -> p n d h", d=D)).then_inc(const, 1)
                dve.wait_ge(bias_ps, 1)
                for t in range(HT):
                    nc.vector.tensor_copy(bv[:, t, :], pv[:, 0:C])
                nc.vector.tensor_scalar_mul(b_col[:, 0:1], pq[:, 0:1], SCALE)
                nc.vector.tensor_copy(b_col[:, 1:2], pq[:, 1:2]).then_inc(bias_in, 1)
                if first:
                    dve.wait_ge(wt_ps, 1)
                    nc.vector.tensor_copy(fc_t[:, :, :], pf[0][:, :].rearrange("p (n f) -> p n f", n=FC))
                    nc.vector.tensor_copy(proj_t[:, :, :], pf[1][:, :].rearrange("p (n f) -> p n f", n=FC)).then_inc(wt_in, 1)
                with dve.Fori(0, B) as i:
                    for hf in range(2):
                        ch = Chain(dve, chain, 2 * HALF_STEPS * i + HALF_STEPS * hf)
                        last_trip(dve, trh_rdy, i, hf)
                        src = s["xn"] if first else s["x"]
                        for t in range(HT):
                            tile = bass.ds(BT * i + HT * hf + t, 1)
                            ins = nc.vector.tensor_scalar(
                                hs[hf][:, t, :], src[:, tile, :].rearrange("p o c -> p (o c)"), s["mean"][:, tile],
                                s["rstd"][:, tile], ALU.subtract, ALU.mult)
                        ins.then_inc(hs_rdy[hf], 1)
                        now(dve, qk_in, i, hf, 2)
                        last_trip(dve, stored, i, hf, 192)
                        part = [parts[hf][:, :, n, :] for n in range(3)]
                        ch.after(nc.vector.tensor_copy(part[0], qk[hf][:, :, :]))
                        ch.after(nc.vector.tensor_tensor(rest[:, :, :], qk[hf][:, :, :], part[0], ALU.subtract))
                        ch.after(nc.vector.tensor_copy(part[1], rest[:, :, :]))
                        nc.vector.tensor_tensor(part[2], rest[:, :, :], part[1], ALU.subtract).then_inc(parts_rdy[hf], 1)
                        now(dve, v_rdy, i, hf)
                        nc.vector.tensor_tensor(s["v"][:, bass.ds(BT * i + HT * hf, HT), :, 0:D],
                                                pv[:, :].rearrange("p (t h d) -> p t h d", t=HT, d=D),
                                                bv[:, :, :].rearrange("p t (h d) -> p t h d", d=D), ALU.add).then_inc(v_in[hf], 1)
                        now(dve, norm_ps, i, hf)
                        ch.mark(nc.vector.reduce_max(norms[:, 0, bass.ds(2 * i + hf, 1)], pq[0:H, :], axis=AX.X))
                        nc.vector.reduce_max(norms[:, 1, bass.ds(2 * i + hf, 1)], pk[0:H, :], axis=AX.X).then_inc(norm_in[hf], 1)
                ch = Chain(dve, tail)
                dve.wait_ge(norm_in[0], B)
                dve.wait_ge(norm_in[1], B)
                ch.after(nc.vector.reduce_max(top[:, 0:2], norms[:, :, :], axis=AX.X))
                ch.after(nc.vector.tensor_tensor(top[:, 2:3], top[:, 0:1], top[:, 1:2], ALU.mult))
                dve.wait_ge(tail_ps, 1)
                ch.after(nc.vector.reduce_max(peak[:, :], tr_x[0:1, 0:H], axis=AX.X))
                ch.after(nc.vector.tensor_scalar(s["flag"][:, :], peak[:, :], BOUND * BOUND, None, ALU.is_gt))

            @block.tensor
            def _(pe):
                pe.wait_ge(const, 3)
                for n in range(2):
                    nc.tensor.matmul(pq[:, n:n + 1], bqk_row[:, n, :], ones[:, 0:1], start=True, stop=True)
                nc.tensor.matmul(pv[:, 0:C], ones[:, :], b_row[:, 2, :], start=True, stop=True).then_inc(bias_ps, 1)
                if first:
                    pe.wait_ge(ffn_in, 32)
                    for n in range(FC):
                        nc.tensor.transpose(pf[0][:, n * P:(n + 1) * P], fc[:, n, :], s["ident"][:, :])
                    for n in range(FC):
                        ins = nc.tensor.transpose(pf[1][:, n * P:(n + 1) * P], proj[:, n * P:(n + 1) * P], s["ident"][:, :])
                    ins.then_inc(wt_ps, 1)
                    pe.wait_ge(wt_in, 1)
                pe.wait_ge(bias_in, 1)
                pe.wait_ge(perm, D)
                with pe.Fori(0, B) as i:
                    for hf in range(2):
                        now(pe, xs_rdy, i, hf)
                        before(pe, xch_rdy, i, hf)
                        for t in range(HT):
                            ins = nc.tensor.transpose(tr_x[:, t * P:(t + 1) * P], xs[hf][:, t, :], s["ident"][:, :])
                        ins.then_inc(trx_rdy[hf], 1)
                        if first:
                            now(pe, hs_rdy, i, hf)
                            before(pe, hch_rdy, i, hf)
                            for t in range(HT):
                                ins = nc.tensor.transpose(tr_h[:, t * P:(t + 1) * P], hs[hf][:, t, :], s["ident"][:, :])
                            ins.then_inc(trh_rdy[hf], 1)
                            now(pe, xch_rdy, i, hf)
                            for f in range(2):
                                before(pe, relu_in, i, hf, FC)
                                nc.tensor.matmul(pf[f][:, :], fc_t[:, f, :], x_ch[hf][:, :], start=True, stop=True).then_inc(f_rdy[hf], 1)
                        now(pe, hch_rdy, i, hf)
                        before(pe, norm_in, i, hf)
                        nc.tensor.matmul(pq[:, :], wqk[:, 0, :], h_ch[hf][:, :], start=True, stop=True).then_inc(q_rdy[hf], 1)
                        nc.tensor.matmul(pk[:, :], wqk[:, 1, :], h_ch[hf][:, :], start=True, stop=True).then_inc(k_rdy[hf], 1)
                        before(pe, v_in, i, hf)
                        for t in range(HT):
                            ins = nc.tensor.matmul(pv[:, t * C:(t + 1) * C], h_ch[hf][:, t * P:(t + 1) * P], w[:, 2, :],
                                                   start=True, stop=True)
                        ins.then_inc(v_rdy[hf], 1)
                        if first:
                            for f in range(2, FC):
                                pe.wait_ge(relu_in[hf], FC * i + f - 1)
                                nc.tensor.matmul(pf[f % 2][:, :], fc_t[:, f, :], x_ch[hf][:, :], start=True, stop=True).then_inc(f_rdy[hf], 1)
                        now(pe, sq_rdy, i, hf)
                        nc.tensor.matmul(pq[0:H, :], head_of[:, :], square[hf][:, 0, :], start=True, stop=True)
                        nc.tensor.matmul(pk[0:H, :], head_of[:, :], square[hf][:, 1, :], start=True, stop=True).then_inc(norm_ps[hf], 1)
                        if first:
                            now(pe, hid_rdy, i, hf, FC)
                            before(pe, y_in, i, hf)
                            for t in range(HT):
                                for f in range(FC):
                                    ins = nc.tensor.matmul(py[:, t * C:(t + 1) * C], hidden[:, f, t * P:(t + 1) * P],
                                                           proj_t[:, f, :], start=f == 0, stop=f == FC - 1)
                            ins.then_inc(y_rdy[hf], 1)
                pe.wait_ge(tail, 2)
                nc.tensor.matmul(tr_x[0:1, 0:H], top[:, 2:3], s["ident"][0:H, 0:H], start=True, stop=True).then_inc(tail_ps, 1)
        sem.wiped()


def load_stacks(sp, q_rows, k_rows, q_st, k_st, b, g, sem):
    for rows, st in ((q_rows, q_st), (k_rows, k_st)):
        by_head = rows.rearrange("r (g j i) t -> r g j i t", j=G // 2, i=2)
        for i in range(2):
            sp.dma_start(st[64 * i:64 * i + ROWS, :, :],
                         by_head[:, bass.ds(g, 1), :, i, bass.ds(T * b, T)].rearrange("r o j t -> r (o j) t")).then_inc(sem, 16)


def row_maxima(nc, a, s, layer, q_rows, k_rows):
    causal = layer == 1
    with ExitStack() as ctx:
        def sb(name, shape, dt=F32):
            return ctx.enter_context(nc.sbuf_tensor(f"m{layer}_{name}", shape, dt))

        sem = Semaphores(nc, ctx, f"m{layer}_")

        SLOTS = 4
        UNITS = BT * G
        q_st = [sb(f"q_st{n}", [P, G // 2, T], BF16) for n in range(2)]
        k_st = [sb(f"k_st{n}", [P, G // 2, T], BF16) for n in range(2)]
        maxima = sb("maxima", [P, NT, H])
        base = sb("base", [P, BT, H])
        parts = sb("parts", [P, NT, P // H, H], BF16)
        rows = sb("rows", [3 * H, N], BF16)
        sc = [ctx.enter_context(nc.psum_tensor(f"m{layer}_sc{n}", [P, T], F32)) for n in range(SLOTS)]
        staged = [sem(f"staged{n}") for n in range(2)]
        used = [sem(f"used{n}") for n in range(2)]
        scored, base_in, split, turned, row_in, out = (sem(x) for x in (
            "scored", "base_in", "split", "turned", "row_in", "out"))
        reduced = [sem(f"reduced{n}") for n in range(SLOTS)]

        with nc.Block() as block:
            @block.sync
            def _(sp):
                with sp.If(sp.value_load(s["flag"][0:1, 0:1], min_val=0, max_val=1) > 0):
                    sp.dma_start(base[:, :, :], a["q_shift"][layer]).then_inc(base_in, 16)
                    with sp.Fori(0, B) as b:
                        with sp.Fori(0, NG // 2) as gg:
                            for n in range(2):
                                sp.wait_ge(used[n], 2 * b + gg)
                                load_stacks(sp, q_rows, k_rows, q_st[n], k_st[n], b, 2 * gg + n, staged[n])
                    sp.wait_ge(row_in, NT)
                    sp.dma_start(q_rows[SPLIT_ROWS:SPLIT_ROWS + 3, :, :].rearrange("r h t -> (r h) t"),
                                 rows[:, :]).then_inc(out, 16)
                    sp.wait_ge(out, 16)
                with sp.Else():
                    sp.nop()

            @block.tensor
            def _(pe):
                with pe.If(pe.value_load(s["flag"][0:1, 0:1], min_val=0, max_val=1) > 0):
                    with pe.Fori(0, B) as b:
                        with pe.Fori(0, NG // 2) as gg:
                            trip = 2 * b + gg
                            for n in range(2):
                                pe.wait_ge(staged[n], 64 * trip + 64)
                                for u in range(UNITS):
                                    qt, pair, i = u // G, u % G // 2, u % 2
                                    width = (qt + 1) * P if causal else T
                                    slot = u % SLOTS
                                    per_trip = 2 * UNITS // SLOTS
                                    pe.wait_ge(reduced[slot], per_trip * trip + (n * UNITS + u) // SLOTS)
                                    part = slice(64 * i, 64 * i + ROWS)
                                    for k0 in range(0, width, HALF):
                                        k1 = min(width, k0 + HALF)
                                        diagonal = causal and k1 == width
                                        ins = nc.tensor.matmul(sc[slot][:, k0:k1], q_st[n][part, pair, qt * P:(qt + 1) * P],
                                                               k_st[n][part, pair, k0:k1], start=True, stop=not diagonal)
                                        if diagonal:
                                            ins = nc.tensor.matmul(sc[slot][:, k1 - P:k1], s["ident_bf"][:, :],
                                                                   s["mask_qk"][:, :], start=False, stop=True)
                                    if u == UNITS - 1:
                                        ins.then_inc(used[n], 1)
                                        pe.wait_ge(used[n], trip + 1)
                                        pe.sem_inc(scored, 1)
                                    else:
                                        ins.then_inc(scored, 1)
                    with pe.Fori(0, NT) as t:
                        pe.wait_ge(split, 6)
                        pe.wait_ge(row_in, t)
                        nc.tensor.transpose(sc[0][:, 0:P // 2].bitcast(BF16),
                                            parts[:, bass.ds(t, 1), :, :].rearrange("p o r h -> p (o r h)"),
                                            s["ident_bf"][:, :]).then_inc(turned, 1)
                with pe.Else():
                    pe.nop()

            @block.vector
            def _(dve):
                with dve.If(dve.value_load(s["flag"][0:1, 0:1], min_val=0, max_val=1) > 0):
                    with dve.Fori(0, B) as b:
                        with dve.Fori(0, NG // 2) as gg:
                            for n in range(2):
                                for u in range(UNITS):
                                    qt, head = u // G, u % G
                                    width = (qt + 1) * P if causal else T
                                    dve.wait_ge(scored, 2 * UNITS * (2 * b + gg) + n * UNITS + u + 1)
                                    nc.vector.reduce_max(
                                        maxima[:, bass.ds(BT * b + qt, 1), bass.ds(2 * G * gg + G * n + head, 1)],
                                        sc[u % SLOTS][:, 0:width], axis=AX.X).then_inc(reduced[u % SLOTS], 1)
                    dve.wait_ge(base_in, 16)
                    for n in range(SLOTS):
                        dve.wait_ge(reduced[n], B * NG * UNITS // SLOTS)
                    ch = Chain(dve, split)
                    ch.mark(nc.vector.memset(parts[:, :, 3:, :], 0.0))
                    for b in range(B):
                        tiles = slice(b * BT, (b + 1) * BT)
                        ins = nc.vector.tensor_tensor(maxima[:, tiles, :], base[:, :, :], maxima[:, tiles, :], ALU.subtract)
                    ch.after(ins)
                    ch.after(nc.vector.tensor_copy(parts[:, :, 0, :], maxima[:, :, :]))
                    ch.after(nc.vector.tensor_tensor(maxima[:, :, :], maxima[:, :, :], parts[:, :, 0, :], ALU.subtract))
                    ch.after(nc.vector.tensor_copy(parts[:, :, 1, :], maxima[:, :, :]))
                    ch.after(nc.vector.tensor_tensor(parts[:, :, 2, :], maxima[:, :, :], parts[:, :, 1, :], ALU.subtract))
                    with dve.Fori(0, NT) as t:
                        dve.wait_ge(turned, t + 1)
                        nc.vector.tensor_copy(rows[:, bass.ds(P * t, P)], sc[0][0:3 * H, 0:P // 2].bitcast(BF16)).then_inc(row_in, 1)
                with dve.Else():
                    dve.nop()
        sem.wiped()


def attention(nc, s, layer, q_rows, k_rows, sums):
    causal = layer == 1
    groups = []
    for kt in range(BT):
        for qh in range(2):
            q0 = max(kt * P - qh * HALF, 0) if causal else 0
            if q0 < HALF:
                groups.append((kt, qh, q0))
    NU = 2 * len(groups)
    with ExitStack() as ctx:
        def sb(name, shape, dt=F32):
            return ctx.enter_context(nc.sbuf_tensor(f"a{layer}_{name}", shape, dt))

        sem = Semaphores(nc, ctx, f"a{layer}_")

        SC, PR = 3, 4
        q_st = [sb(f"q_st{n}", [P, G // 2, T], BF16) for n in range(2)]
        k_st = [sb(f"k_st{n}", [P, G // 2, T], BF16) for n in range(2)]
        v_st = [sb(f"v_st{n}", [P, BT, G, VW]) for n in range(2)]
        probs = [sb(f"probs{n}", [P, G, HALF]) for n in range(PR)]
        o_sb = [sb(f"o_sb{n}", [P, 2, HALF]) for n in range(2)]
        scores = [ctx.enter_context(nc.psum_tensor(f"a{layer}_sc{n}", [P, 2, HALF], F32)) for n in range(SC)]
        o_ps = ctx.enter_context(nc.psum_tensor(f"a{layer}_o", [P, 2, HALF], F32))
        if not causal:
            mem = [sb(f"mem{n}", [P, 2, C]) for n in range(2)]
            count = sb("count", [P, 2, C])
        staged = [sem(f"staged{n}") for n in range(2)]
        scored = sem("scored")
        exp_done = [sem(f"exp_done{n}") for n in range(SC)]
        pv_done = [sem(f"pv_done{n}") for n in range(PR)]
        o_done = [sem(f"o_done{n}") for n in range(2)]
        o_free, o_clear, spikes = sem("o_free"), sem("o_clear"), sem("spikes")
        o_in = [sem(f"o_in{n}") for n in range(2)]
        stored = [sem(f"stored{n}") for n in range(2)]

        def sc_slot(n, u):
            return (n * NU + u) % SC, (n * NU + u) // SC

        def sc_uses(slot):
            return len(range(slot, 2 * NU, SC))

        LAST = len(groups) - 1

        def wait_probs_free(act, n, j, trip):
            at = n * (LAST + 1) + j
            before_n, before_j = divmod((at - PR) % NU, LAST + 1)
            if before_j == LAST:
                act.wait_ge(o_done[before_n], trip + (1 if at >= PR else 0))
            else:
                uses = [x for x in range(at % PR, NU, PR) if x % (LAST + 1) != LAST]
                act.wait_ge(pv_done[at % PR], len(uses) * trip + len([x for x in uses if x < at]))

        with nc.Block() as block:
            def store_sums(sp, at, n):
                sp.dma_start(sums[bass.ds(at, 1)].rearrange("o p t -> p (o t)"),
                             o_sb[n][:, :, :].rearrange("p k t -> p (k t)")).then_inc(stored[n], 16)

            @block.sync
            def _(sp):
                sp.wait_ge(o_clear, 2)
                with sp.Fori(0, B) as b:
                    with sp.Fori(0, NG // 2) as gg:
                        trip = 2 * b + gg
                        for n in range(2):
                            sp.wait_ge(o_in[n], 2 * trip)
                            store_sums(sp, 2 * trip + n, n)
                            sp.wait_ge(o_done[n], trip)
                            load_stacks(sp, q_rows, k_rows, q_st[n], k_st[n], b, 2 * gg + n, staged[n])
                            sp.dma_start(v_st[n][:, :, :, :],
                                         s["v"][:, bass.ds(BT * b, BT), bass.ds(G * (2 * gg + n), G), :]).then_inc(staged[n], 16)
                for n in range(2):
                    sp.wait_ge(o_in[n], B * NG)
                    store_sums(sp, B * NG + n, n)
                for n in range(2):
                    sp.wait_ge(stored[n], 16 * (B * NG // 2 + 1))

            @block.scalar
            def _(act):
                with act.Fori(0, B) as b:
                    with act.Fori(0, NG // 2) as gg:
                        trip = 2 * b + gg
                        for n in range(2):
                            for u in range(NU):
                                j, pair = u // 2, u % 2
                                kt, qh, q0 = groups[j]
                                slot, _ = sc_slot(n, u)
                                p_slot = (n * (LAST + 1) + j) % PR
                                act.wait_ge(scored, 2 * NU * trip + n * NU + u + 1)
                                if pair == 0:
                                    wait_probs_free(act, n, j, trip)
                                nc.scalar.activation(probs[p_slot][:, 2 * pair:2 * pair + 2, 0:HALF - q0],
                                                     scores[slot][:, :, 0:HALF - q0], ACT.Exp).then_inc(exp_done[slot], 1)

            @block.vector
            def _(dve):
                for n in range(2):
                    ins = nc.vector.memset(o_sb[n][:, :, :], 0.0)
                nc.vector.memset(o_ps[:, :, :], 0.0).then_inc(o_clear, 2)
                dve.wait_ge(o_clear, 2)
                with dve.Fori(0, B) as b:
                    with dve.Fori(0, NG // 2) as gg:
                        trip = 2 * b + gg
                        for n in range(2):
                            if not causal:
                                spike(nc, dve, s["y"][:, bass.ds(BT * b + 4 * gg + 2 * n, 2), :], mem, count, spikes,
                                      2 * (3 * (STEPS - 1) + 1) * trip + (3 * (STEPS - 1) + 1) * n)
                            dve.wait_ge(o_done[n], trip + 1)
                            dve.wait_ge(stored[n], 16 * trip + 16)
                            for qh in range(2):
                                nc.vector.tensor_copy(o_sb[n][:, qh, :], o_ps[:, qh, :]).then_inc(o_in[n], 1)

            @block.tensor
            def _(pe):
                pe.wait_ge(o_clear, 2)

                def score(n, u, trip):
                    kt, qh, q0 = groups[u // 2]
                    pair = u % 2
                    slot, use = sc_slot(n, u)
                    pe.wait_ge(exp_done[slot], sc_uses(slot) * trip + use)
                    diagonal = causal and kt // HT == qh
                    for i in range(2):
                        part = slice(64 * i, 64 * i + ROWS)
                        ins = nc.tensor.matmul(scores[slot][:, i, 0:HALF - q0], k_st[n][part, pair, kt * P:(kt + 1) * P],
                                               q_st[n][part, pair, qh * HALF + q0:(qh + 1) * HALF],
                                               start=True, stop=not diagonal)
                    if diagonal:
                        for i in range(2):
                            ins = nc.tensor.matmul(scores[slot][:, i, 0:P], s["ident_bf"][:, :], s["mask_kq"][:, :],
                                                   start=False, stop=True)
                    ins.then_inc(scored, 1)

                def product(n, j, trip):
                    kt, qh, q0 = groups[j]
                    slot, use = sc_slot(n, 2 * j + 1)
                    pe.wait_ge(exp_done[slot], sc_uses(slot) * trip + use + 1)
                    if kt == 0:
                        pe.wait_ge(o_in[1 - n], 2 * trip + 2 * n)
                    last_kt = HT * (qh + 1) - 1 if causal else BT - 1
                    p_slot = (n * (LAST + 1) + j) % PR
                    for h in range(G):
                        ins = nc.tensor.matmul(o_ps[32 * h:32 * h + VW, qh, q0:HALF], v_st[n][:, kt, h, :],
                                               probs[p_slot][:, h, 0:HALF - q0], start=kt == 0, stop=kt == last_kt,
                                               tile_position=(0, 32 * h))
                    ins.then_inc(o_done[n] if j == LAST else pv_done[p_slot], 1)

                with pe.Fori(0, B) as b:
                    with pe.Fori(0, NG // 2) as gg:
                        trip = 2 * b + gg
                        for n in range(2):
                            pe.wait_ge(staged[n], 80 * trip + 80)
                            score(n, 0, trip)
                            score(n, 1, trip)
                            for j in range(len(groups)):
                                if j + 1 < len(groups):
                                    score(n, 2 * j + 2, trip)
                                    score(n, 2 * j + 3, trip)
                                product(n, j, trip)
        sem.wiped()


def spike(nc, dve, y, mem, count, sem, base):
    ch = Chain(dve, sem, base)
    m0 = y
    ch.after(nc.vector.tensor_scalar(count[:, :, :], y, 1.0, None, ALU.is_gt))
    for step in range(1, STEPS):
        m1 = mem[step % 2]
        ch.after(nc.vector.scalar_tensor_tensor(m1[:, :, :], m0, BETA, y, ALU.mult, ALU.add))
        ch.after(nc.vector.scalar_tensor_tensor(m1[:, :, :], m0, 1.0, m1[:, :, :], ALU.is_gt, ALU.subtract, reverse1=True))
        last = step == STEPS - 1
        ch.after(nc.vector.scalar_tensor_tensor(y if last else count[:, :, :], m1[:, :, :], 1.0, count[:, :, :],
                                                ALU.is_gt, ALU.add))
        m0 = m1[:, :, :]


def combine(nc, a, s, layer, sums, out_t):
    first = layer == 0
    gate_in, gate_scale = (s["y"], 1.0 / STEPS) if first else (s["xn"], 1.0)
    with ExitStack() as ctx:
        def sb(name, shape, dt=F32):
            return ctx.enter_context(nc.sbuf_tensor(f"c{layer}_{name}", shape, dt))

        sem = Semaphores(nc, ctx, f"c{layer}_")

        heads = [sb(f"heads{n}", [P, NG, T]) for n in range(2)]
        gate = [sb(f"gate{n}", [P, BT, C]) for n in range(2)]
        skip = [sb(f"skip{n}", [P, BT, C]) for n in range(2)]
        recip = [sb(f"recip{n}", [P, H]) for n in range(2)]
        tok = [sb(f"tok{n}", [P, C]) for n in range(2)]
        chan = [sb(f"chan{n}", [P, P]) for n in range(2)]
        mix = [sb(f"mix{n}", [P, C]) for n in range(2)]
        turn = [ctx.enter_context(nc.psum_tensor(f"c{layer}_turn{n}", [P, NG, P], F32)) for n in range(2)]
        back = [ctx.enter_context(nc.psum_tensor(f"c{layer}_back{n}", [P, HALF], F32)) for n in range(2)]
        proj = [ctx.enter_context(nc.psum_tensor(f"c{layer}_proj{n}", [P, HALF], F32)) for n in range(2)]
        loaded, turned, gated, exped, skipped, stored = (sem.pair(x) for x in (
            "loaded", "turned", "gated", "exped", "skipped", "stored"))
        tok_rdy, back_rdy, chan_rdy, proj_rdy, mixed = (sem.pair(x) for x in ("tok_rdy", "back_rdy", "chan_rdy", "proj_rdy", "mixed"))
        link = sem("link")
        glink = sem("glink")
        TILE_STEPS = 3
        per_trip = BT

        with nc.Block() as block:
            @block.sync
            def _(sp):
                with sp.Fori(0, B // 2) as i:
                    for n in range(2):
                        last_trip(sp, turned, i, n, BT)
                        sp.dma_start(heads[n][:, :, :], sums[bass.ds(NG * (2 * i + n) + 2, NG)].rearrange("g p t -> p g t")).then_inc(loaded[n], 16)
                if not first:
                    with sp.Fori(0, B // 2) as i:
                        for n in range(2):
                            now(sp, mixed, i, n, BT)
                            tiles = bass.ds(BT * (2 * i + n), BT)
                            sp.dma_start(out_t[:, tiles, :], s["x"][:, tiles, :]).then_inc(stored[n], 16)
                    for n in range(2):
                        sp.wait_ge(stored[n], 16 * B // 2)

            @block.gpsimd
            def _(pool):
                if not first:
                    return
                with pool.Fori(0, B // 2) as i:
                    for n in range(2):
                        last_trip(pool, mixed, i, n, BT)
                        for t in range(BT):
                            tile = bass.ds(BT * (2 * i + n) + t, 1)
                            ins = pool.tensor_tensor(skip[n][:, t:t + 1, :], s["xn"][:, tile, :],
                                                     s["bo"][:, 0:1, :], ALU.add)
                        ins.then_inc(skipped[n], 1)

            @block.scalar
            def _(act):
                with act.Fori(0, B // 2) as i:
                    for n in range(2):
                        last_trip(act, mixed, i, n, BT)
                        nc.scalar.activation(gate[n][:, :, :], gate_in[:, bass.ds(BT * (2 * i + n), BT), :], ACT.Exp,
                                             scale=-gate_scale).then_inc(exped[n], 1)
                        for t in range(BT):
                            k = t % 2
                            act.wait_ge(back_rdy[k], per_trip * i + BT // 2 * n + t // 2 + 1)
                            act.wait_ge(proj_rdy[k], per_trip * i + BT // 2 * n + t // 2)
                            nc.scalar.copy(chan[k][:, :], back[k][:, 0:P]).then_inc(chan_rdy[k], 1)

            @block.vector
            def _(dve):
                with dve.Fori(0, B // 2) as i:
                    for n in range(2):
                        gl = Chain(dve, glink, 4 * i + 2 * n)
                        now(dve, exped, i, n)
                        gl.after(nc.vector.tensor_scalar_add(gate[n][:, :, :], gate[n][:, :, :], 1.0))
                        gl.after(nc.vector.reciprocal(gate[n][:, :, :], gate[n][:, :, :]))
                        nc.vector.scalar_tensor_tensor(gate[n][:, :, :], gate_in[:, bass.ds(BT * (2 * i + n), BT), :],
                                                       gate_scale, gate[n][:, :, :], ALU.mult, ALU.mult).then_inc(gated[n], 1)
                        now(dve, gated, i, n)
                        if first:
                            now(dve, skipped, i, n)
                        ch = Chain(dve, link, 2 * TILE_STEPS * BT * i + TILE_STEPS * BT * n)

                        def normalize(t):
                            k = t % 2
                            dve.wait_ge(turned[n], BT * i + t + 1)
                            heads_of = turn[k][:, :, :].rearrange("p g (h w) -> p (g h) w", w=32)
                            ch.after(nc.vector.reciprocal(recip[k][:, :], heads_of[:, :, D]))
                            dve.wait_ge(back_rdy[k], per_trip * i + BT // 2 * n + t // 2)
                            nc.vector.tensor_tensor(tok[k][:, :].rearrange("p (h d) -> p h d", d=D), heads_of[:, :, 0:D],
                                                    recip[k][:, :].rearrange("p (h o) -> p h o", o=1).broadcast_to([P, H, D]),
                                                    ALU.mult).then_inc(tok_rdy[k], 1)

                        def add(t):
                            k = t % 2
                            tile = bass.ds(BT * (2 * i + n) + t, 1)
                            x = s["x"][:, tile, :].rearrange("p o c -> p (o c)")
                            dve.wait_ge(proj_rdy[k], per_trip * i + BT // 2 * n + t // 2 + 1)
                            ch.after(nc.vector.tensor_tensor(mix[k][:, :], proj[k][:, 0:C], skip[n][:, t, :] if first else s["bo"][:, 1, :], ALU.add))
                            ch.after(nc.vector.tensor_tensor(mix[k][:, :], mix[k][:, :], gate[n][:, t, :], ALU.mult))
                            nc.vector.tensor_tensor(x, x, mix[k][:, :], ALU.add).then_inc(mixed[n], 1)

                        for t in range(BT + 1):
                            if t < BT:
                                normalize(t)
                            if t >= 1:
                                add(t - 1)

            @block.tensor
            def _(pe):
                with pe.Fori(0, B // 2) as i:
                    for n in range(2):
                        now(pe, loaded, i, n, 16)

                        def so_far(t):
                            return per_trip * i + BT // 2 * n + t // 2

                        for t in range(BT + 2):
                            if t < BT:
                                k = t % 2
                                pe.wait_ge(tok_rdy[k], so_far(t))
                                for g in range(NG):
                                    ins = nc.tensor.transpose(turn[k][:, g, :], heads[n][:, g, t * P:(t + 1) * P], s["ident"][:, :])
                                ins.then_inc(turned[n], 1)
                            if 1 <= t <= BT:
                                k = (t - 1) % 2
                                pe.wait_ge(tok_rdy[k], so_far(t - 1) + 1)
                                pe.wait_ge(chan_rdy[k], so_far(t - 1))
                                nc.tensor.transpose(back[k][:, 0:P], tok[k][:, :], s["ident"][:, :]).then_inc(back_rdy[k], 1)
                            if t >= 2:
                                k = t % 2
                                pe.wait_ge(chan_rdy[k], so_far(t - 2) + 1)
                                u = t - 2
                                if u >= 2:
                                    pe.wait_ge(mixed[n], BT * i + u - 1)
                                elif n == 1:
                                    pe.wait_ge(mixed[0], BT * i + BT - 1 + u)
                                else:
                                    pe.wait_ge(mixed[1], BT * i)
                                nc.tensor.matmul(proj[k][:, 0:C], chan[k][:, :], s["wo"][:, layer, :], start=True,
                                                 stop=True).then_inc(proj_rdy[k], 1)
        sem.wiped()


def coupling(nc, a, s):
    with ExitStack() as ctx:
        def sb(name, shape, dt=F32):
            return ctx.enter_context(nc.sbuf_tensor(f"n_{name}", shape, dt))

        sem = Semaphores(nc, ctx, f"n_")

        H1, H2 = C // 2, C // 4
        Q = P // 4
        w1, w2, w3, w4 = sb("w1", [C, C]), sb("w2", [C, H1]), sb("w3", [H1, P]), sb("w4", [H2, 1])
        g1, g2, g3 = sb("g1", [C, H1]), sb("g2", [H1, H2]), sb("g3", [H2, 1])
        w4_all, g3_all = sb("w4_all", [H2, P]), sb("g3_all", [H2, P])
        b1, b2, b3 = sb("b1", [C, 1]), sb("b2", [H1, 1]), sb("b3", [H2, 1])
        gb1, gb2 = sb("gb1", [H1, 1]), sb("gb2", [H2, 1])
        scalars = sb("scalars", [1, 4])
        ones = sb("ones", [1, P])
        col = sb("col", [P, 8])
        twist = sb("twist", [P, P])
        mean = sb("mean", [P, B])
        u1, u2 = sb("gu1", [H1, B]), sb("gu2", [H2, B])
        gf = sb("gf", [P, B])
        offset = sb("offset", [P, B])
        state = [sb(f"state{hf}", [P, HALF]) for hf in range(2)]
        h1 = [sb(f"h1_{hf}", [C, HALF]) for hf in range(2)]
        h2 = [sb(f"h2_{hf}", [H1, HALF]) for hf in range(2)]
        h3 = [sb(f"h3_{hf}", [H2, HALF]) for hf in range(2)]
        th = [sb(f"th{hf}", [P, HALF]) for hf in range(2)]
        ps = [[ctx.enter_context(nc.psum_tensor(f"n_ps{k}_{hf}", [P, HALF], F32)) for k in range(4)] for hf in range(2)]
        load, const, gps, gact, chain, gready = (sem(x) for x in ("load", "const", "gps", "gact", "chain", "gready"))
        start, l1, l2, l3, l4, tw = (sem.pair(x) for x in ("start", "l1", "l2", "l3", "l4", "tw"))
        a1, a2, a3, a4, upd, link, turned, kept = (sem.pair(x) for x in ("a1", "a2", "a3", "a4", "upd", "link", "turned", "kept"))
        xt = s["y"][:, :, :].rearrange("p t c -> p (t c)")

        def column(name):
            return a[name].rearrange("(c o) -> c o", o=1)

        with nc.Block() as block:
            @block.sync
            def _(sp):
                pairs = [(w1[:, :], a["L1_ffn_cn_w1"]), (w2[:, :], a["L1_ffn_cn_w2"]), (w3[:, 0:H2], a["L1_ffn_cn_w3"]),
                         (w4[:, :], a["L1_ffn_cn_w4"]), (g1[:, :], a["L1_ffn_gc_w1"]), (g2[:, :], a["L1_ffn_gc_w2"]),
                         (g3[:, :], a["L1_ffn_gc_w3"]), (b1[:, :], column("L1_ffn_cn_b1")), (b2[:, :], column("L1_ffn_cn_b2")),
                         (b3[:, :], column("L1_ffn_cn_b3")), (gb1[:, :], column("L1_ffn_gc_b1")),
                         (gb2[:, :], column("L1_ffn_gc_b2")), (scalars[:, 0:1], column("L1_ffn_cn_b4")),
                         (scalars[:, 1:2], column("L1_ffn_gc_b3")), (scalars[:, 2:3], column("L1_ffn_adaptive_range"))]
                for dst, src in pairs:
                    sp.dma_start(dst, src).then_inc(load, 16)

            @block.gpsimd
            def _(pool):
                with pool.Fori(0, B) as i:
                    for hf in range(2):
                        last_trip(pool, turned, i, hf)
                        pool.tensor_copy(state[hf][:, :], xt[:, bass.ds(T * i + HALF * hf, HALF)]).then_inc(start[hf], 1)

            @block.scalar
            def _(act):
                act.wait_ge(gps, 1)
                nc.scalar.activation(u1[:, :], ps[0][0][0:H1, 0:B], ACT.Gelu, bias=gb1[:, :]).then_inc(gact, 1)
                act.wait_ge(gps, 2)
                nc.scalar.activation(u2[:, :], ps[0][1][0:H2, 0:B], ACT.Gelu, bias=gb2[:, :]).then_inc(gact, 1)
                act.wait_ge(gps, 3)
                act.wait_ge(gready, 1)
                nc.scalar.activation(gf[:, :], ps[0][2][:, 0:B], ACT.Tanh, bias=col[:, 1:2], scale=0.5).then_inc(gact, 1)
                with act.Fori(0, B) as i:
                    for c in range(CYCLES):
                        for hf in range(2):
                            act.wait_ge(l1[hf], CYCLES * i + c + 1)
                            nc.scalar.activation(h1[hf][:, :], ps[hf][0][:, :], ACT.Gelu, bias=b1[:, :]).then_inc(a1[hf], 1)
                        for hf in range(2):
                            act.wait_ge(l2[hf], CYCLES * i + c + 1)
                            nc.scalar.activation(h2[hf][:, :], ps[hf][1][0:H1, :], ACT.Gelu, bias=b2[:, :]).then_inc(a2[hf], 1)
                        for hf in range(2):
                            act.wait_ge(l3[hf], CYCLES * i + c + 1)
                            nc.scalar.activation(h3[hf][:, :], ps[hf][0][0:H2, :], ACT.Gelu, bias=b3[:, :]).then_inc(a3[hf], 1)
                        for hf in range(2):
                            act.wait_ge(l4[hf], CYCLES * i + c + 1)
                            nc.scalar.activation(th[hf][:, :], ps[hf][1][:, :], ACT.Tanh, bias=col[:, 0:1],
                                                 scale=0.5).then_inc(a4[hf], 1)
                    for hf in range(2):
                        now(act, turned, i, hf)
                        nc.scalar.copy(s["xn"][:, bass.ds(BT * i + HT * hf, HT), :],
                                       ps[hf][3][:, :].rearrange("p (t c) -> p t c", c=C)).then_inc(kept[hf], 1)

            @block.vector
            def _(dve):
                ch = Chain(dve, chain)
                nc.vector.memset(w3[:, H2:P], 0.0)
                nc.vector.memset(ones[:, :], 1.0).then_inc(const, 1)
                ch.after(nc.vector.memset(twist[:, :], 0.0))
                for dst, src, sign in ((0, 2, 1.0), (1, 3, -1.0), (2, 0, -1.0), (3, 1, 1.0)):
                    r = slice(Q * src, Q * src + Q)
                    ch.mark(nc.vector.tensor_scalar_mul(twist[r, Q * dst:Q * dst + Q], s["ident"][r, r], sign))
                ins = nc.vector.reduce_sum(mean[:, :], xt.rearrange("p (b t) -> p b t", b=B), axis=AX.X)
                ch.after(ins)
                ch.mark(nc.vector.tensor_scalar_mul(mean[:, :], mean[:, :], 1.0 / T))
                dve.wait_ge(load, 16 * 15)
                ch.mark(nc.vector.tensor_copy(w4_all[:, :], w4[:, :].broadcast_to([H2, P])))
                nc.vector.tensor_copy(g3_all[:, :], g3[:, :].broadcast_to([H2, P])).then_inc(const, 1)
                dve.wait_ge(gps, 3)
                ch.after(nc.vector.tensor_copy(col[:, 2:5], ps[0][3][:, 0:3]))
                ch.mark(nc.vector.tensor_scalar_mul(col[:, 0:2], col[:, 2:4], 0.5))
                ch.mark(nc.vector.tensor_scalar_mul(col[:, 5:6], col[:, 4:5], 0.3))
                nc.vector.tensor_scalar_mul(col[:, 6:7], col[:, 4:5], 2.0).then_inc(gready, 1)
                dve.wait_ge(gready, 1)
                ch.wait()
                dve.wait_ge(gact, 3)
                ch.after(nc.vector.tensor_scalar(offset[:, :], gf[:, :], 0.35, col[:, 6:7], ALU.mult, ALU.mult))
                ch.after(nc.vector.tensor_scalar_add(offset[:, :], offset[:, :], 0.1))
                with dve.Fori(0, B) as i:
                    for c in range(CYCLES):
                        for hf in range(2):
                            ln = Chain(dve, link[hf], 2 * CYCLES * i + 2 * c)
                            if c == 0:
                                now(dve, start, i, hf)
                            dve.wait_ge(a4[hf], CYCLES * i + c + 1)
                            ln.after(nc.vector.tensor_scalar(th[hf][:, :], th[hf][:, :], col[:, 5:6],
                                                             offset[:, bass.ds(i, 1)], ALU.mult, ALU.add))
                            dve.wait_ge(tw[hf], CYCLES * i + c + 1)
                            ln.after(nc.vector.tensor_tensor(th[hf][:, :], th[hf][:, :], ps[hf][2][:, :], ALU.mult))
                            nc.vector.tensor_tensor(state[hf][:, :], state[hf][:, :], th[hf][:, :], ALU.add).then_inc(upd[hf], 1)

            @block.tensor
            def _(pe):
                pe.wait_ge(const, 2)
                pe.wait_ge(chain, 7)
                nc.tensor.matmul(ps[0][0][0:H1, 0:B], g1[:, :], mean[:, :], start=True, stop=True).then_inc(gps, 1)
                nc.tensor.matmul(ps[0][3][:, 0:3], ones[:, :], scalars[:, 0:3], start=True, stop=True)
                pe.wait_ge(gact, 1)
                nc.tensor.matmul(ps[0][1][0:H2, 0:B], g2[:, :], u1[:, :], start=True, stop=True).then_inc(gps, 1)
                pe.wait_ge(gact, 2)
                nc.tensor.matmul(ps[0][2][:, 0:B], g3_all[:, :], u2[:, :], start=True, stop=True).then_inc(gps, 1)
                pe.wait_ge(gact, 3)
                pe.wait_ge(gready, 1)
                with pe.Fori(0, B) as i:
                    for c in range(CYCLES):
                        k = CYCLES * i + c
                        for hf in range(2):
                            if c == 0:
                                now(pe, start, i, hf)
                                last_trip(pe, kept, i, hf)
                            pe.wait_ge(upd[hf], k)
                            pe.wait_ge(a3[hf], k)
                            nc.tensor.matmul(ps[hf][0][:, :], w1[:, :], state[hf][:, :], start=True, stop=True).then_inc(l1[hf], 1)
                            nc.tensor.matmul(ps[hf][2][:, :], twist[:, :], state[hf][:, :], start=True, stop=True).then_inc(tw[hf], 1)
                        for hf in range(2):
                            pe.wait_ge(a1[hf], k + 1)
                            pe.wait_ge(a4[hf], k)
                            nc.tensor.matmul(ps[hf][1][0:H1, :], w2[:, :], h1[hf][:, :], start=True, stop=True).then_inc(l2[hf], 1)
                        for hf in range(2):
                            pe.wait_ge(a2[hf], k + 1)
                            nc.tensor.matmul(ps[hf][0][:, :], w3[:, :], h2[hf][:, :], start=True, stop=True).then_inc(l3[hf], 1)
                        for hf in range(2):
                            pe.wait_ge(a3[hf], k + 1)
                            nc.tensor.matmul(ps[hf][1][:, :], w4_all[:, :], h3[hf][:, :], start=True, stop=True).then_inc(l4[hf], 1)
                    for hf in range(2):
                        pe.wait_ge(upd[hf], CYCLES * i + CYCLES)
                        for t in range(HT):
                            ins = nc.tensor.transpose(ps[hf][3][:, t * P:(t + 1) * P], state[hf][:, t * P:(t + 1) * P], s["ident"][:, :])
                        ins.then_inc(turned[hf], 1)
        sem.wiped()


_INS = ["L0_attn_x", "L0_attn_ln_gamma", "L0_attn_ln_beta", "L0_attn_w_qkv", "L0_attn_b_qkv", "L0_attn_w_out",
        "L0_attn_b_out", "L0_ffn_W_fc", "L0_ffn_W_proj", "L1_attn_Wq", "L1_attn_bq", "L1_attn_Wk", "L1_attn_bk",
        "L1_attn_Wv", "L1_attn_bv", "L1_attn_Wo", "L1_attn_bo", "L1_ffn_cn_w1", "L1_ffn_cn_b1", "L1_ffn_cn_w2",
        "L1_ffn_cn_b2", "L1_ffn_cn_w3", "L1_ffn_cn_b3", "L1_ffn_cn_w4", "L1_ffn_cn_b4", "L1_ffn_gc_w1", "L1_ffn_gc_b1",
        "L1_ffn_gc_w2", "L1_ffn_gc_b2", "L1_ffn_gc_w3", "L1_ffn_gc_b3", "L1_ffn_adaptive_range"]


def position_rows():
    slopes = 2.0 ** (-8.0 * (np.arange(H) + 1) / H)
    shift = (slopes.astype(np.float32)[:, None] * (T - 1 - np.arange(T, dtype=np.float32))).astype(np.float32)
    q = np.zeros((2, ROWS - SPLIT_ROWS, H, T), np.uint16)
    k = np.zeros((2, ROWS - SPLIT_ROWS, H, T), np.uint16)
    q[:, 3:6], k[:, :3] = 0x3F80, 0x3F80
    rest = shift.copy()
    for n in range(3):
        part = rest.view(np.uint32) & np.uint32(0xFFFF0000)
        q[1, n], k[1, 3 + n] = part >> 16, (part >> 16) | (part != 0) * 0x8000
        rest = rest - part.view(np.float32)
    base = np.zeros((2, P, BT, H), np.float32)
    base[1] = shift.reshape(H, BT, P).transpose(2, 1, 0)
    return {"q_extra": q, "k_extra": k, "q_shift": base}


def kernel(**inputs):
    import concourse.bacc as _bacc
    from concourse.bass_utils import run_bass_kernel_spmd as _run

    nc = _bacc.Bacc("TRN2", target_bir_lowering=False, num_devices=1)
    arrays, args = {}, {}
    for name, value in [(n, inputs[n]) for n in _INS] + list(position_rows().items()):
        x = np.ascontiguousarray(value)
        arrays[f"in_{name}_dram"] = x
        args[name] = nc.dram_tensor(f"in_{name}_dram", x.shape, mybir.dt.from_np(x.dtype), kind="ExternalInput").ap()
    args["out"] = nc.dram_tensor("out_0_dram", (B, T, C), F32, kind="ExternalOutput").ap()
    build(nc, args)
    r = _run(nc, [arrays], core_ids=[0])
    return r.results[0]["out_0_dram"]
```

```python
from contextlib import ExitStack

import numpy as np

import concourse.bass as bass
from concourse import mybir

F32 = mybir.dt.float32
BF16 = mybir.dt.bfloat16
I32 = mybir.dt.int32
ALU = mybir.AluOpType
ACT = mybir.ActivationFunctionType
AX = mybir.AxisListType

P = 128
B, T, C = 4, 1024, 128
H, D = 16, 8
N = B * T
NT = N // P
BT = T // P
HALF = 512
HT = HALF // P
G = 4
NG = H // G
FF = 512
FC = FF // P
SCALE = float(D) ** -0.5
EPS = 1e-5
Q_PARTS = (0, 0, 0, 1, 1, 2)
K_PARTS = (0, 1, 2, 0, 1, 0)
SPLIT_ROWS = D * len(Q_PARTS)
ROWS = 64
VW = 16
BOUND = 60.0
STEPS = 5
BETA = 0.9
MASK = -1.0e30
CYCLES = 3


class Semaphores:

    def __init__(self, nc, ctx, prefix):
        self.nc, self.ctx, self.prefix, self.all = nc, ctx, prefix, []

    def __call__(self, name):
        self.all.append(self.ctx.enter_context(self.nc.semaphore(f"{self.prefix}{name}")))
        return self.all[-1]

    def pair(self, name):
        return self.many(name, 2)

    def many(self, name, n):
        return [self(f"{name}{k}") for k in range(n)]

    def wiped(self):
        ids = sorted(h.num for h in self.all)
        firsts = [n for n in ids if n - 1 not in ids]
        with self.nc.Block() as block:
            @block.sync
            def _(sp):
                for n in firsts:
                    end = next(m for m in range(n, n + len(ids) + 1) if m not in ids)
                    sp.sem_clear(range(n, end))


def now(eng, sem, i, hf, m=1):
    eng.wait_ge(sem[hf], m * i + m)


def before(eng, sem, i, hf, m=1):
    eng.wait_ge(sem[1 - hf], m * i + m * hf)


def last_trip(eng, sem, i, hf, m=1):
    eng.wait_ge(sem[hf], m * i)


def reached(eng, sem, count):
    if not (isinstance(count, int) and count <= 0):
        eng.wait_ge(sem, count)


def after_first(eng, count, body):
    body(0)
    with eng.Fori(1, count) as i:
        body(i)


def trips(eng, body):
    body(0, True, False)
    with eng.Fori(1, B) as b:
        body(b, True, True)
    body(B, False, True)


class Chain:

    def __init__(self, eng, sem, base=0):
        self.eng, self.sem, self.base, self.n = eng, sem, base, 0

    def mark(self, ins):
        self.n += 1
        ins.then_inc(self.sem, 1)

    def wait(self):
        self.eng.wait_ge(self.sem, self.base + self.n)

    def after(self, ins):
        self.mark(ins)
        self.wait()


def build(nc, a):
    x_t = a["L0_attn_x"].rearrange("b (t p) c -> p (b t) c", p=P)
    out_t = a["out"].rearrange("b (t p) c -> p (b t) c", p=P)
    q_rows = [nc.dram_tensor(f"q_rows{n}", [ROWS, H, N], BF16).ap() for n in range(2)]
    k_rows = [nc.dram_tensor(f"k_rows{n}", [ROWS, H, N], BF16).ap() for n in range(2)]

    with ExitStack() as ctx:
        def sb(name, shape, dt=F32):
            return ctx.enter_context(nc.sbuf_tensor(name, shape, dt))

        s = {
            "ident": sb("ident", [P, P]), "ident_bf": sb("ident_bf", [P, P], BF16),
            "mask_kq": sb("mask_kq", [P, P], BF16),
            "mask_qk": sb("mask_qk", [P, P], BF16),
            "x": sb("x", [P, NT, C]),
            "xn": sb("xn", [P, NT, C]),
            "y": sb("y", [P, NT, C]),
            "v": sb("v", [P, NT, H, VW]),
            "mean": sb("mean", [P, NT]), "rstd": sb("rstd", [P, NT]),
            "flag": sb("flag", [1, 1], I32),
            "wo": sb("wo", [P, 2, C]),
            "bo": sb("bo", [P, 2, C]),
        }
        setup(nc, a, s, q_rows, k_rows)
        layernorm(nc, s, "outer", s["x"], x_t, True)
        layernorm(nc, s, "inner", s["xn"], None, False)
        prepare(nc, a, s, 0, q_rows[0], k_rows[0])
        row_maxima(nc, a, s, 0, q_rows[0], k_rows[0])
        attention(nc, a, s, 0, q_rows[0], k_rows[0], None)
        layernorm(nc, s, "second", s["x"], None, False)
        prepare(nc, a, s, 1, q_rows[1], k_rows[1])
        coupling(nc, a, s)
        row_maxima(nc, a, s, 1, q_rows[1], k_rows[1])
        attention(nc, a, s, 1, q_rows[1], k_rows[1], out_t)


def setup(nc, a, s, q_rows, k_rows):
    with ExitStack() as ctx:
        bo_row = ctx.enter_context(nc.sbuf_tensor("bo_row", [1, 2, C], F32))
        ones = ctx.enter_context(nc.sbuf_tensor("su_ones", [1, P], F32))
        ps = ctx.enter_context(nc.psum_tensor("su_ps", [P, 2, C], F32))
        sem = Semaphores(nc, ctx, "su_")
        zero = sem("zero")
        idn = sem("ident")
        load = sem("load")
        rows = sem("rows")
        done = sem("bcast")
        vec = sem("vec")
        with nc.Block() as block:
            @block.sync
            def _(sp):
                sp.dma_start(bo_row[:, 0, :], a["L0_attn_b_out"].rearrange("(o c) -> o c", o=1)).then_inc(load, 16)
                sp.dma_start(bo_row[:, 1, :], a["L1_attn_bo"].rearrange("(o c) -> o c", o=1)).then_inc(load, 16)
                sp.dma_start(s["wo"][:, 0, :], a["L0_attn_w_out"]).then_inc(load, 16)
                sp.dma_start(s["wo"][:, 1, :], a["L1_attn_Wo"]).then_inc(load, 16)
                for n in range(2):
                    for b in range(B):
                        tok = slice(b * T, (b + 1) * T)
                        sp.dma_start(q_rows[n][SPLIT_ROWS:ROWS, :, tok], a["q_extra"][n].bitcast(BF16)).then_inc(rows, 16)
                        sp.dma_start(k_rows[n][SPLIT_ROWS:ROWS, :, tok], a["k_extra"][n].bitcast(BF16)).then_inc(rows, 16)
                sp.wait_ge(load, 64)
                sp.wait_ge(rows, 16 * 2 * B * 2)

            @block.gpsimd
            def _(pool):
                pool.memset(s["ident"][:, :], 0.0).then_inc(zero, 1)
                pool.wait_ge(zero, 1)
                pool.affine_select(out=s["ident"][:, :], in_=s["ident"][:, :], compare_op=ALU.not_equal, fill=1.0,
                                   base=0, pattern=[[-1, P]], channel_multiplier=1).then_inc(idn, 1)
                pool.wait_ge(idn, 1)
                pool.tensor_copy(s["ident_bf"][:, :], s["ident"][:, :]).then_inc(idn, 1)
                for mask, sign in ((s["mask_kq"], 1), (s["mask_qk"], -1)):
                    pool.memset(mask[:, :], 0.0).then_inc(zero, 1)
                pool.wait_ge(zero, 3)
                for mask, sign in ((s["mask_kq"], 1), (s["mask_qk"], -1)):
                    pool.affine_select(out=mask[:, :], in_=mask[:, :], compare_op=ALU.is_ge, fill=MASK, base=0,
                                       pattern=[[sign, P]], channel_multiplier=-sign).then_inc(idn, 1)

            @block.vector
            def _(dve):
                nc.vector.memset(ones[:, :], 1.0).then_inc(vec, 1)
                nc.vector.memset(s["v"][:, :, :, D + 1:VW], 0.0)
                nc.vector.memset(s["v"][:, :, :, D:D + 1], 1.0)
                dve.wait_ge(done, 1)
                nc.vector.tensor_copy(s["bo"][:, :, :], ps[:, :, :]).then_inc(vec, 1)

            @block.tensor
            def _(pe):
                pe.wait_ge(load, 64)
                pe.wait_ge(vec, 1)
                nc.tensor.matmul(ps[:, :, :], ones[:, :], bo_row[:, :, :], start=True, stop=True).then_inc(done, 1)
        sem.wiped()


def layernorm(nc, s, tag, src, x_t, apply):
    with ExitStack() as ctx:
        st = ctx.enter_context(nc.sbuf_tensor(f"{tag}_st", [P, NT, 6], F32))
        mv = ctx.enter_context(nc.sbuf_tensor(f"{tag}_mv", [P, NT, 2], F32))
        tmp = [ctx.enter_context(nc.sbuf_tensor(f"{tag}_t{k}", [P, NT], F32)) for k in range(3)]
        sem = Semaphores(nc, ctx, f"{tag}_")
        load = sem.many("load", B)
        var, root, step = sem("var"), sem("root"), sem("step")
        with nc.Block() as block:
            @block.sync
            def _(sp):
                if x_t is not None:
                    for b in range(B):
                        sp.dma_start(src[:, b * BT:(b + 1) * BT, :], x_t[:, b * BT:(b + 1) * BT, :]).then_inc(load[b], 16)

            @block.scalar
            def _(act):
                act.wait_ge(var, 1)
                nc.scalar.activation(tmp[1][:, :], tmp[0][:, :], ACT.Sqrt).then_inc(root, 1)

            @block.vector
            def _(dve):
                ch = Chain(dve, step)
                for b in range(B):
                    if x_t is not None:
                        dve.wait_ge(load[b], 16)
                    for t in range(b * BT, (b + 1) * BT):
                        ch.mark(nc.vector.bn_stats(st[:, t, :], src[:, t, :]))
                ch.wait()
                for t in range(NT):
                    ch.mark(nc.vector.bn_aggr(mv[:, t, :], st[:, t, :]))
                ch.wait()
                ch.mark(nc.vector.tensor_copy(s["mean"][:, :], mv[:, :, 0]))
                nc.vector.tensor_scalar_add(tmp[0][:, :], mv[:, :, 1], EPS).then_inc(var, 1)
                dve.wait_ge(root, 1)
                ch.after(nc.vector.reciprocal(tmp[1][:, :], tmp[1][:, :]))
                ch.after(nc.vector.tensor_tensor(tmp[2][:, :], tmp[1][:, :], tmp[1][:, :], ALU.mult))
                ch.after(nc.vector.tensor_tensor(tmp[2][:, :], tmp[2][:, :], tmp[0][:, :], ALU.mult))
                ch.after(nc.vector.tensor_scalar(tmp[2][:, :], tmp[2][:, :], -0.5, 1.5, ALU.mult, ALU.add))
                ch.after(nc.vector.tensor_tensor(s["rstd"][:, :], tmp[1][:, :], tmp[2][:, :], ALU.mult))
                if apply:
                    for t in range(NT):
                        ch.mark(nc.vector.tensor_scalar(s["xn"][:, t, :], src[:, t, :], s["mean"][:, t:t + 1],
                                                        s["rstd"][:, t:t + 1], ALU.subtract, ALU.mult))
        sem.wiped()


def prepare(nc, a, s, layer, q_rows, k_rows):
    first = layer == 0
    with ExitStack() as ctx:
        def sb(name, shape, dt=F32):
            return ctx.enter_context(nc.sbuf_tensor(f"p{layer}_{name}", shape, dt))

        def ps(name, shape=(P, HALF)):
            return ctx.enter_context(nc.psum_tensor(f"p{layer}_{name}", list(shape), F32))

        sem = Semaphores(nc, ctx, f"p{layer}_")

        w = sb("w", [P, 3, C])
        wqk = sb("wqk", [P, 2, C])
        b_row = sb("b_row", [1, 3, C])
        bqk_row = sb("bqk_row", [1, 2, C])
        b_col = sb("b_col", [P, 2])
        bv = sb("bv", [P, HT, C])
        norm_col = sb("norm_col", [P, 2])
        ones = sb("ones", [1, P])
        head_of = sb("head_of", [P, H], BF16)
        xs = [sb(f"xs{hf}", [P, HT, C]) for hf in range(2)]
        hs = [sb(f"hs{hf}", [P, HT, C]) for hf in range(2)] if first else xs
        x_ch = [sb(f"x_ch{hf}", [P, HALF]) for hf in range(2)]
        h_ch = [sb(f"h_ch{hf}", [P, HALF]) for hf in range(2)] if first else x_ch
        qk = [sb(f"qk{hf}", [P, 2, HALF]) for hf in range(2)]
        rest = sb("rest", [P, 2, HALF])
        parts = [sb(f"parts{hf}", [P, 2, 3, HALF], BF16) for hf in range(2)]
        square = [sb(f"square{hf}", [P, 2, HALF], BF16) for hf in range(2)]
        norms = sb("norms", [H, 2, 2 * B])
        top = sb("top", [H, 4])
        peak = sb("peak", [1, 1])
        if first:
            fc = sb("fc", [P, FC, C])
            proj = sb("proj", [P, FF])
            fc_t = sb("fc_t", [P, FC, P])
            proj_t = sb("proj_t", [P, FC, C])
            relu = sb("relu", [P, FC, HALF])
            hidden = sb("hidden", [P, FC, HALF])

        tr_x, tr_h, pq, pk, pv = ps("tr_x"), ps("tr_h"), ps("pq"), ps("pk"), ps("pv")
        pf = [ps("pf0"), ps("pf1")]
        py = ps("py")

        w_in, ffn_in, const, perm, bias_ps, wt_ps, wt_in = (sem(x) for x in (
            "w_in", "ffn_in", "const", "perm", "bias_ps", "wt_ps", "wt_in"))
        bias_in, tail, tail_ps, chain = sem("bias_in"), sem("tail"), sem("tail_ps"), sem("chain")
        xs_rdy, hs_rdy, trx_rdy, trh_rdy, xch_rdy, hch_rdy = (sem.pair(x) for x in (
            "xs_rdy", "hs_rdy", "trx_rdy", "trh_rdy", "xch_rdy", "hch_rdy"))
        q_rdy, k_rdy, v_rdy, qk_in, v_in, parts_rdy, stored = (sem.pair(x) for x in (
            "q_rdy", "k_rdy", "v_rdy", "qk_in", "v_in", "parts_rdy", "stored"))
        sq_rdy, norm_ps, norm_in, f_rdy, relu_in, hid_rdy, y_rdy, y_in = (sem.pair(x) for x in (
            "sq_rdy", "norm_ps", "norm_in", "f_rdy", "relu_in", "hid_rdy", "y_rdy", "y_in"))
        if not first:
            hs_rdy, trh_rdy, hch_rdy = xs_rdy, trx_rdy, xch_rdy
        HALF_STEPS = 4

        with nc.Block() as block:
            @block.sync
            def _(sp):
                if first:
                    sp.dma_start(w[:, :, :], a["L0_attn_w_qkv"].rearrange("k (n c) -> k n c", n=3)).then_inc(w_in, 16)
                    sp.dma_start(b_row[:, :, :], a["L0_attn_b_qkv"].rearrange("(o n c) -> o n c", o=1, n=3)).then_inc(w_in, 16)
                    sp.dma_start(norm_col[:, 0:1], a["L0_attn_ln_gamma"].rearrange("(c o) -> c o", o=1)).then_inc(w_in, 16)
                    sp.dma_start(norm_col[:, 1:2], a["L0_attn_ln_beta"].rearrange("(c o) -> c o", o=1)).then_inc(w_in, 16)
                    sp.dma_start(fc[:, :, :], a["L0_ffn_W_fc"].rearrange("(n f) c -> f n c", f=P)).then_inc(ffn_in, 16)
                    sp.dma_start(proj[:, :], a["L0_ffn_W_proj"]).then_inc(ffn_in, 16)
                else:
                    for n, name in enumerate("qkv"):
                        sp.dma_start(w[:, n, :], a[f"L1_attn_W{name}"]).then_inc(w_in, 16)
                        sp.dma_start(b_row[:, n, :], a[f"L1_attn_b{name}"].rearrange("(o c) -> o c", o=1)).then_inc(w_in, 16)
                with sp.Fori(0, B) as i:
                    for hf in range(2):
                        now(sp, parts_rdy, i, hf)
                        tok = bass.ds(T * i + HALF * hf, HALF)
                        for r in range(len(Q_PARTS)):
                            rows = slice(D * r, D * r + D)
                            sp.dma_start(q_rows[rows, :, tok].rearrange("d h t -> (d h) t"),
                                         parts[hf][:, 0, Q_PARTS[r], :]).then_inc(stored[hf], 16)
                            sp.dma_start(k_rows[rows, :, tok].rearrange("d h t -> (d h) t"),
                                         parts[hf][:, 1, K_PARTS[r], :]).then_inc(stored[hf], 16)
                for hf in range(2):
                    sp.wait_ge(stored[hf], 192 * B)

            @block.gpsimd
            def _(pool):
                pool.wait_ge(const, 1)
                for d in range(D):
                    pool.affine_select(out=head_of[:, :], in_=head_of[:, :], compare_op=ALU.not_equal, fill=1.0,
                                       base=-H * d, pattern=[[-1, H]], channel_multiplier=1).then_inc(perm, 1)
                    pool.wait_ge(perm, d + 1)
                with pool.Fori(0, B) as i:
                    for hf in range(2):
                        if first:
                            last_trip(pool, trx_rdy, i, hf)
                            pool.tensor_copy(xs[hf][:, :, :], s["xn"][:, bass.ds(BT * i + HT * hf, HT), :]).then_inc(xs_rdy[hf], 1)
                            last_trip(pool, y_rdy, i, hf)
                            before(pool, y_rdy, i, hf)
                            for f in range(FC):
                                pool.wait_ge(relu_in[hf], FC * i + f + 1)
                                pool.tensor_tensor(hidden[:, f, :], relu[:, f, :], relu[:, f, :], ALU.mult).then_inc(hid_rdy[hf], 1)
                        else:
                            now(pool, xch_rdy, i, hf)
                            pool.tensor_copy(s["y"][:, bass.ds(BT * i + HT * hf, HT), :],
                                             x_ch[hf][:, :].rearrange("p (t c) -> p t c", c=C)).then_inc(y_in[hf], 1)

            @block.scalar
            def _(act):
                with act.Fori(0, B) as i:
                    for hf in range(2):
                        now(act, trx_rdy, i, hf)
                        last_trip(act, v_rdy, i, hf)
                        if first:
                            last_trip(act, f_rdy, i, hf, FC)
                        else:
                            last_trip(act, y_in, i, hf)
                        nc.scalar.copy(x_ch[hf][:, :], tr_x[:, :]).then_inc(xch_rdy[hf], 1)
                        if first:
                            now(act, trh_rdy, i, hf)
                            nc.scalar.activation(h_ch[hf][:, :], tr_h[:, :], ACT.Identity, bias=norm_col[:, 1:2],
                                                 scale=norm_col[:, 0:1]).then_inc(hch_rdy[hf], 1)
                        now(act, q_rdy, i, hf)
                        act.wait_ge(bias_in, 1)
                        last_trip(act, parts_rdy, i, hf)
                        nc.scalar.activation(qk[hf][:, 0, :], pq[:, :], ACT.Identity, bias=b_col[:, 0:1],
                                             scale=SCALE).then_inc(qk_in[hf], 1)
                        now(act, k_rdy, i, hf)
                        nc.scalar.activation(qk[hf][:, 1, :], pk[:, :], ACT.Identity, bias=b_col[:, 1:2]).then_inc(qk_in[hf], 1)
                        last_trip(act, norm_ps, i, hf)
                        now(act, qk_in, i, hf, 2)
                        nc.scalar.activation(square[hf][:, :, :], qk[hf][:, :, :], ACT.Square).then_inc(sq_rdy[hf], 1)
                        if first:
                            for f in range(FC):
                                act.wait_ge(f_rdy[hf], FC * i + f + 1)
                                before(act, hid_rdy, i, hf, FC)
                                nc.scalar.activation(relu[:, f, :], pf[f % 2][:, :], ACT.Relu).then_inc(relu_in[hf], 1)
                            now(act, y_rdy, i, hf)
                            nc.scalar.copy(s["y"][:, bass.ds(BT * i + HT * hf, HT), :],
                                           py[:, :].rearrange("p (t c) -> p t c", c=C)).then_inc(y_in[hf], 1)

            @block.vector
            def _(dve):
                nc.vector.memset(head_of[:, :], 0.0).then_inc(const, 1)
                nc.vector.memset(ones[:, :], 1.0).then_inc(const, 1)
                dve.wait_ge(w_in, 64 if first else 96)
                nc.vector.tensor_copy(wqk[:, :, :].rearrange("p n (d h) -> p n d h", h=H),
                                      w[:, 0:2, :].rearrange("p n (h d) -> p n d h", d=D))
                nc.vector.tensor_copy(bqk_row[:, :, :].rearrange("p n (d h) -> p n d h", h=H),
                                      b_row[:, 0:2, :].rearrange("p n (h d) -> p n d h", d=D)).then_inc(const, 1)
                dve.wait_ge(bias_ps, 1)
                for t in range(HT):
                    nc.vector.tensor_copy(bv[:, t, :], pv[:, 0:C])
                nc.vector.tensor_scalar_mul(b_col[:, 0:1], pq[:, 0:1], SCALE)
                nc.vector.tensor_copy(b_col[:, 1:2], pq[:, 1:2]).then_inc(bias_in, 1)
                if first:
                    dve.wait_ge(wt_ps, 1)
                    nc.vector.tensor_copy(fc_t[:, :, :], pf[0][:, :].rearrange("p (n f) -> p n f", n=FC))
                    nc.vector.tensor_copy(proj_t[:, :, :], pf[1][:, :].rearrange("p (n f) -> p n f", n=FC)).then_inc(wt_in, 1)
                with dve.Fori(0, B) as i:
                    for hf in range(2):
                        ch = Chain(dve, chain, 2 * HALF_STEPS * i + HALF_STEPS * hf)
                        last_trip(dve, trh_rdy, i, hf)
                        src = s["xn"] if first else s["x"]
                        for t in range(HT):
                            tile = bass.ds(BT * i + HT * hf + t, 1)
                            ins = nc.vector.tensor_scalar(
                                hs[hf][:, t, :], src[:, tile, :].rearrange("p o c -> p (o c)"), s["mean"][:, tile],
                                s["rstd"][:, tile], ALU.subtract, ALU.mult)
                        ins.then_inc(hs_rdy[hf], 1)
                        now(dve, qk_in, i, hf, 2)
                        last_trip(dve, stored, i, hf, 192)
                        part = [parts[hf][:, :, n, :] for n in range(3)]
                        ch.after(nc.vector.tensor_copy(part[0], qk[hf][:, :, :]))
                        ch.after(nc.vector.tensor_tensor(rest[:, :, :], qk[hf][:, :, :], part[0], ALU.subtract))
                        ch.after(nc.vector.tensor_copy(part[1], rest[:, :, :]))
                        nc.vector.tensor_tensor(part[2], rest[:, :, :], part[1], ALU.subtract).then_inc(parts_rdy[hf], 1)
                        now(dve, v_rdy, i, hf)
                        nc.vector.tensor_tensor(s["v"][:, bass.ds(BT * i + HT * hf, HT), :, 0:D],
                                                pv[:, :].rearrange("p (t h d) -> p t h d", t=HT, d=D),
                                                bv[:, :, :].rearrange("p t (h d) -> p t h d", d=D), ALU.add).then_inc(v_in[hf], 1)
                        now(dve, norm_ps, i, hf)
                        ch.mark(nc.vector.reduce_max(norms[:, 0, bass.ds(2 * i + hf, 1)], pq[0:H, :], axis=AX.X))
                        nc.vector.reduce_max(norms[:, 1, bass.ds(2 * i + hf, 1)], pk[0:H, :], axis=AX.X).then_inc(norm_in[hf], 1)
                ch = Chain(dve, tail)
                dve.wait_ge(norm_in[0], B)
                dve.wait_ge(norm_in[1], B)
                ch.after(nc.vector.reduce_max(top[:, 0:2], norms[:, :, :], axis=AX.X))
                ch.after(nc.vector.tensor_tensor(top[:, 2:3], top[:, 0:1], top[:, 1:2], ALU.mult))
                dve.wait_ge(tail_ps, 1)
                ch.after(nc.vector.reduce_max(peak[:, :], tr_x[0:1, 0:H], axis=AX.X))
                ch.after(nc.vector.tensor_scalar(s["flag"][:, :], peak[:, :], BOUND * BOUND, None, ALU.is_gt))

            @block.tensor
            def _(pe):
                pe.wait_ge(const, 3)
                for n in range(2):
                    nc.tensor.matmul(pq[:, n:n + 1], bqk_row[:, n, :], ones[:, 0:1], start=True, stop=True)
                nc.tensor.matmul(pv[:, 0:C], ones[:, :], b_row[:, 2, :], start=True, stop=True).then_inc(bias_ps, 1)
                if first:
                    pe.wait_ge(ffn_in, 32)
                    for n in range(FC):
                        nc.tensor.transpose(pf[0][:, n * P:(n + 1) * P], fc[:, n, :], s["ident"][:, :])
                    for n in range(FC):
                        ins = nc.tensor.transpose(pf[1][:, n * P:(n + 1) * P], proj[:, n * P:(n + 1) * P], s["ident"][:, :])
                    ins.then_inc(wt_ps, 1)
                    pe.wait_ge(wt_in, 1)
                pe.wait_ge(bias_in, 1)
                pe.wait_ge(perm, D)
                with pe.Fori(0, B) as i:
                    for hf in range(2):
                        now(pe, xs_rdy, i, hf)
                        before(pe, xch_rdy, i, hf)
                        for t in range(HT):
                            ins = nc.tensor.transpose(tr_x[:, t * P:(t + 1) * P], xs[hf][:, t, :], s["ident"][:, :])
                        ins.then_inc(trx_rdy[hf], 1)
                        if first:
                            now(pe, hs_rdy, i, hf)
                            before(pe, hch_rdy, i, hf)
                            for t in range(HT):
                                ins = nc.tensor.transpose(tr_h[:, t * P:(t + 1) * P], hs[hf][:, t, :], s["ident"][:, :])
                            ins.then_inc(trh_rdy[hf], 1)
                            now(pe, xch_rdy, i, hf)
                            for f in range(2):
                                before(pe, relu_in, i, hf, FC)
                                nc.tensor.matmul(pf[f][:, :], fc_t[:, f, :], x_ch[hf][:, :], start=True, stop=True).then_inc(f_rdy[hf], 1)
                        now(pe, hch_rdy, i, hf)
                        before(pe, norm_in, i, hf)
                        nc.tensor.matmul(pq[:, :], wqk[:, 0, :], h_ch[hf][:, :], start=True, stop=True).then_inc(q_rdy[hf], 1)
                        nc.tensor.matmul(pk[:, :], wqk[:, 1, :], h_ch[hf][:, :], start=True, stop=True).then_inc(k_rdy[hf], 1)
                        before(pe, v_in, i, hf)
                        for t in range(HT):
                            ins = nc.tensor.matmul(pv[:, t * C:(t + 1) * C], h_ch[hf][:, t * P:(t + 1) * P], w[:, 2, :],
                                                   start=True, stop=True)
                        ins.then_inc(v_rdy[hf], 1)
                        if first:
                            for f in range(2, FC):
                                pe.wait_ge(relu_in[hf], FC * i + f - 1)
                                nc.tensor.matmul(pf[f % 2][:, :], fc_t[:, f, :], x_ch[hf][:, :], start=True, stop=True).then_inc(f_rdy[hf], 1)
                        now(pe, sq_rdy, i, hf)
                        nc.tensor.matmul(pq[0:H, :], head_of[:, :], square[hf][:, 0, :], start=True, stop=True)
                        nc.tensor.matmul(pk[0:H, :], head_of[:, :], square[hf][:, 1, :], start=True, stop=True).then_inc(norm_ps[hf], 1)
                        if first:
                            now(pe, hid_rdy, i, hf, FC)
                            before(pe, y_in, i, hf)
                            for t in range(HT):
                                for f in range(FC):
                                    ins = nc.tensor.matmul(py[:, t * C:(t + 1) * C], hidden[:, f, t * P:(t + 1) * P],
                                                           proj_t[:, f, :], start=f == 0, stop=f == FC - 1)
                            ins.then_inc(y_rdy[hf], 1)
                pe.wait_ge(tail, 2)
                nc.tensor.matmul(tr_x[0:1, 0:H], top[:, 2:3], s["ident"][0:H, 0:H], start=True, stop=True).then_inc(tail_ps, 1)
        sem.wiped()


def load_stacks(sp, q_rows, k_rows, q_st, k_st, b, g, sem):
    for rows, st in ((q_rows, q_st), (k_rows, k_st)):
        by_head = rows.rearrange("r (g j i) t -> r g j i t", j=G // 2, i=2)
        for i in range(2):
            sp.dma_start(st[64 * i:64 * i + ROWS, :, :],
                         by_head[:, bass.ds(g, 1), :, i, bass.ds(T * b, T)].rearrange("r o j t -> r (o j) t")).then_inc(sem, 16)


def row_maxima(nc, a, s, layer, q_rows, k_rows):
    causal = layer == 1
    with ExitStack() as ctx:
        def sb(name, shape, dt=F32):
            return ctx.enter_context(nc.sbuf_tensor(f"m{layer}_{name}", shape, dt))

        sem = Semaphores(nc, ctx, f"m{layer}_")

        SLOTS = 4
        UNITS = BT * G
        q_st = [sb(f"q_st{n}", [P, G // 2, T], BF16) for n in range(2)]
        k_st = [sb(f"k_st{n}", [P, G // 2, T], BF16) for n in range(2)]
        maxima = sb("maxima", [P, NT, H])
        base = sb("base", [P, BT, H])
        parts = sb("parts", [P, NT, P // H, H], BF16)
        rows = sb("rows", [3 * H, N], BF16)
        sc = [ctx.enter_context(nc.psum_tensor(f"m{layer}_sc{n}", [P, T], F32)) for n in range(SLOTS)]
        staged = [sem(f"staged{n}") for n in range(2)]
        used = [sem(f"used{n}") for n in range(2)]
        scored, base_in, split, turned, row_in, out = (sem(x) for x in (
            "scored", "base_in", "split", "turned", "row_in", "out"))
        reduced = [sem(f"reduced{n}") for n in range(SLOTS)]

        with nc.Block() as block:
            @block.sync
            def _(sp):
                with sp.If(sp.value_load(s["flag"][0:1, 0:1], min_val=0, max_val=1) > 0):
                    sp.dma_start(base[:, :, :], a["q_shift"][layer]).then_inc(base_in, 16)
                    with sp.Fori(0, B) as b:
                        with sp.Fori(0, NG // 2) as gg:
                            for n in range(2):
                                sp.wait_ge(used[n], 2 * b + gg)
                                load_stacks(sp, q_rows, k_rows, q_st[n], k_st[n], b, 2 * gg + n, staged[n])
                    sp.wait_ge(row_in, NT)
                    sp.dma_start(q_rows[SPLIT_ROWS:SPLIT_ROWS + 3, :, :].rearrange("r h t -> (r h) t"),
                                 rows[:, :]).then_inc(out, 16)
                    sp.wait_ge(out, 16)
                with sp.Else():
                    sp.nop()

            @block.tensor
            def _(pe):
                with pe.If(pe.value_load(s["flag"][0:1, 0:1], min_val=0, max_val=1) > 0):
                    with pe.Fori(0, B) as b:
                        with pe.Fori(0, NG // 2) as gg:
                            trip = 2 * b + gg
                            for n in range(2):
                                pe.wait_ge(staged[n], 64 * trip + 64)
                                for u in range(UNITS):
                                    qt, pair, i = u // G, u % G // 2, u % 2
                                    width = (qt + 1) * P if causal else T
                                    slot = u % SLOTS
                                    per_trip = 2 * UNITS // SLOTS
                                    pe.wait_ge(reduced[slot], per_trip * trip + (n * UNITS + u) // SLOTS)
                                    part = slice(64 * i, 64 * i + ROWS)
                                    for k0 in range(0, width, HALF):
                                        k1 = min(width, k0 + HALF)
                                        diagonal = causal and k1 == width
                                        ins = nc.tensor.matmul(sc[slot][:, k0:k1], q_st[n][part, pair, qt * P:(qt + 1) * P],
                                                               k_st[n][part, pair, k0:k1], start=True, stop=not diagonal)
                                        if diagonal:
                                            ins = nc.tensor.matmul(sc[slot][:, k1 - P:k1], s["ident_bf"][:, :],
                                                                   s["mask_qk"][:, :], start=False, stop=True)
                                    if u == UNITS - 1:
                                        ins.then_inc(used[n], 1)
                                        pe.wait_ge(used[n], trip + 1)
                                        pe.sem_inc(scored, 1)
                                    else:
                                        ins.then_inc(scored, 1)
                    with pe.Fori(0, NT) as t:
                        pe.wait_ge(split, 6)
                        pe.wait_ge(row_in, t)
                        nc.tensor.transpose(sc[0][:, 0:P // 2].bitcast(BF16),
                                            parts[:, bass.ds(t, 1), :, :].rearrange("p o r h -> p (o r h)"),
                                            s["ident_bf"][:, :]).then_inc(turned, 1)
                with pe.Else():
                    pe.nop()

            @block.vector
            def _(dve):
                with dve.If(dve.value_load(s["flag"][0:1, 0:1], min_val=0, max_val=1) > 0):
                    with dve.Fori(0, B) as b:
                        with dve.Fori(0, NG // 2) as gg:
                            for n in range(2):
                                for u in range(UNITS):
                                    qt, head = u // G, u % G
                                    width = (qt + 1) * P if causal else T
                                    dve.wait_ge(scored, 2 * UNITS * (2 * b + gg) + n * UNITS + u + 1)
                                    nc.vector.reduce_max(
                                        maxima[:, bass.ds(BT * b + qt, 1), bass.ds(2 * G * gg + G * n + head, 1)],
                                        sc[u % SLOTS][:, 0:width], axis=AX.X).then_inc(reduced[u % SLOTS], 1)
                    dve.wait_ge(base_in, 16)
                    for n in range(SLOTS):
                        dve.wait_ge(reduced[n], B * NG * UNITS // SLOTS)
                    ch = Chain(dve, split)
                    ch.mark(nc.vector.memset(parts[:, :, 3:, :], 0.0))
                    for b in range(B):
                        tiles = slice(b * BT, (b + 1) * BT)
                        ins = nc.vector.tensor_tensor(maxima[:, tiles, :], base[:, :, :], maxima[:, tiles, :], ALU.subtract)
                    ch.after(ins)
                    ch.after(nc.vector.tensor_copy(parts[:, :, 0, :], maxima[:, :, :]))
                    ch.after(nc.vector.tensor_tensor(maxima[:, :, :], maxima[:, :, :], parts[:, :, 0, :], ALU.subtract))
                    ch.after(nc.vector.tensor_copy(parts[:, :, 1, :], maxima[:, :, :]))
                    ch.after(nc.vector.tensor_tensor(parts[:, :, 2, :], maxima[:, :, :], parts[:, :, 1, :], ALU.subtract))
                    with dve.Fori(0, NT) as t:
                        dve.wait_ge(turned, t + 1)
                        nc.vector.tensor_copy(rows[:, bass.ds(P * t, P)], sc[0][0:3 * H, 0:P // 2].bitcast(BF16)).then_inc(row_in, 1)
                with dve.Else():
                    dve.nop()
        sem.wiped()


def attention(nc, a, s, layer, q_rows, k_rows, out_t):
    causal = layer == 1
    first = layer == 0
    LAG = 2
    halves = [[(kt, max(kt * P - qh * HALF, 0) if causal else 0) for kt in range(BT)] for qh in range(2)]
    halves = [[(kt, q0) for kt, q0 in half if q0 < HALF] for half in halves]
    groups = [(qh, kt, q0, kt == half[0][0], kt == half[-1][0]) for qh, half in enumerate(halves) for kt, q0 in half]
    L = len(groups)
    S = NG * L
    ends = [g * L + j for g in range(NG) for j in range(L) if groups[j][4]]
    ENDS = len(ends)
    jobs = []
    for k, end in enumerate(ends):
        jobs.append((end + LAG + 2, "turn", k))
        if k >= ENDS - 2:
            jobs.append((end + LAG + 3, "back", k - (ENDS - 2)))
            jobs.append((end + LAG + 4, "mix", k - (ENDS - 2)))
    JOBS = len(jobs)
    TAIL = jobs[-1][0] - S + 1
    GATE_ENDS = [ends[2], ends[4]]
    LINKS = ENDS + 4
    SPIKE_STEPS = 3 * (STEPS - 1) + 1

    def turn_index(k):
        return next(i for i, (_, kind, n) in enumerate(jobs) if (kind, n) == ("turn", k))

    def jobs_at(step):
        return [(index, kind, k) for index, (at, kind, k) in enumerate(jobs) if at == step]

    with ExitStack() as ctx:
        def sb(name, shape, dt=F32):
            return ctx.enter_context(nc.sbuf_tensor(f"a{layer}_{name}", shape, dt))

        sem = Semaphores(nc, ctx, f"a{layer}_")

        SC, PR = 3, 4
        q_st = [sb(f"q_st{n}", [P, G // 2, T], BF16) for n in range(2)]
        k_st = [sb(f"k_st{n}", [P, G // 2, T], BF16) for n in range(2)]
        v_st = [sb(f"v_st{n}", [P, BT, G, VW]) for n in range(2)]
        probs = [sb(f"probs{n}", [P, G, HALF]) for n in range(PR)]
        o_sb = [sb(f"o_sb{n}", [P, HALF]) for n in range(2)]
        recip = sb("recip", [P, HT, G])
        tok = sb("tok", [P, BT, C])
        chan = sb("chan", [P, HALF])
        gate = sb("gate", [P, BT, C])
        mix = [sb(f"mix{n}", [P, HT, C]) for n in range(2)]
        scores = [ctx.enter_context(nc.psum_tensor(f"a{layer}_sc{n}", [P, 2, HALF], F32)) for n in range(SC)]
        o_ps = ctx.enter_context(nc.psum_tensor(f"a{layer}_o", [P, HALF], F32))
        job_ps = ctx.enter_context(nc.psum_tensor(f"a{layer}_job", [P, HALF], F32))
        if first:
            mem = [sb(f"mem{n}", [P, 2, C]) for n in range(2)]
            count = sb("count", [P, 2, C])
        gate_in, gate_scale = (s["y"], 1.0 / STEPS) if first else (s["xn"], 1.0)
        staged = sem.pair("staged")
        scored = sem("scored")
        exp_done = sem.many("exp_done", SC)
        pv_done = sem.many("pv_done", PR)
        o_clear = sem("o_clear")
        o_in = sem("o_in")
        job_rdy, job_read = sem("job_rdy"), sem("job_read")
        spikes, exped, glink, gated = (sem(x) for x in ("spikes", "exped", "glink", "gated"))
        skipped, scaled, updated = (sem(x) for x in ("skipped", "scaled", "updated"))
        stored = sem.pair("stored")

        UNITS = 2 * S

        def exp_count(unit, b):
            return len(range(unit % SC, UNITS, SC)) * b + unit // SC + 1

        def pv_count(group, b):
            return S // PR * b + group // PR + 1

        with nc.Block() as block:
            @block.sync
            def _(sp):
                def load(b, g):
                    n = g % 2
                    group = ((g - 2) * L + L - 1) % S
                    reached(sp, pv_done[group % PR], pv_count(group, b) - (S // PR if g < 2 else 0))
                    load_stacks(sp, q_rows, k_rows, q_st[n], k_st[n], b, g, staged[n])
                    sp.dma_start(v_st[n][:, :, :, :], s["v"][:, bass.ds(BT * b, BT), G * g:G * g + G, :]).then_inc(staged[n], 16)

                def trip(b, own, late):
                    if own:
                        load(b, 0)
                        load(b, 1)
                    if late and not first:
                        for hf in range(2):
                            sp.wait_ge(updated, 2 * b - 1 + hf)
                            tiles = bass.ds(BT * b + HT * hf - BT, HT)
                            sp.dma_start(out_t[:, tiles, :], s["x"][:, tiles, :]).then_inc(stored[hf], 16)
                    if own:
                        load(b, 2)
                        load(b, 3)

                trips(sp, trip)
                if not first:
                    for hf in range(2):
                        sp.wait_ge(stored[hf], 16 * B)

            @block.scalar
            def _(act):
                def trip(b, own, late):
                    if not own:
                        return
                    for j in range(S):
                        qh, kt, q0, _, _ = groups[j % L]
                        reached(act, pv_done[j % PR], pv_count(j, b) - 1)
                        for pair in range(2):
                            unit = 2 * j + pair
                            act.wait_ge(scored, UNITS * b + unit + 1)
                            nc.scalar.activation(probs[j % PR][:, 2 * pair:2 * pair + 2, 0:HALF - q0],
                                                 scores[unit % SC][:, :, 0:HALF - q0], ACT.Exp).then_inc(exp_done[unit % SC], 1)
                        if j in GATE_ENDS:
                            hf = GATE_ENDS.index(j)
                            if first:
                                act.wait_ge(spikes, NG * SPIKE_STEPS * b + NG // 2 * SPIKE_STEPS * (hf + 1))
                            reached(act, updated, 2 * b)
                            nc.scalar.activation(gate[:, HT * hf:HT * hf + HT, :], gate_in[:, bass.ds(BT * b + HT * hf, HT), :],
                                                 ACT.Exp, scale=-gate_scale).then_inc(exped, 1)

                trips(act, trip)

            @block.gpsimd
            def _(pool):
                if first:
                    for b in range(B):
                        tiles = slice(BT * b, BT * b + BT)
                        pool.tensor_tensor(s["xn"][:, tiles, :], s["xn"][:, tiles, :],
                                           s["bo"][:, 0:1, :].broadcast_to([P, BT, C]), ALU.add).then_inc(skipped, 1)

                def update(b, hf):
                    index = next(i for i, (_, kind, k) in enumerate(jobs) if (kind, k) == ("mix", hf))
                    pool.wait_ge(job_read, JOBS * b + index + 1)
                    pool.wait_ge(gated, 2 * b + hf + 1)
                    pool.tensor_tensor(mix[hf][:, :, :], mix[hf][:, :, :], gate[:, HT * hf:HT * hf + HT, :],
                                       ALU.mult).then_inc(scaled, 1)
                    pool.wait_ge(scaled, 2 * b + hf + 1)
                    x = s["x"][:, bass.ds(BT * b + HT * hf, HT), :]
                    pool.tensor_tensor(x, x, mix[hf][:, :, :], ALU.add).then_inc(updated, 1)

                def trip(b, own, late):
                    if late:
                        update(b - 1, 1)
                    if own:
                        update(b, 0)

                trips(pool, trip)

            @block.vector
            def _(dve):
                nc.vector.memset(o_ps[:, :], 0.0).then_inc(o_clear, 1)
                if first:
                    dve.wait_ge(skipped, B)

                def finish_gate(b, hf):
                    part = gate[:, HT * hf:HT * hf + HT, :]
                    done = LINKS * b + (2 if hf == 0 else 6)
                    dve.wait_ge(exped, 2 * b + hf + 1)
                    nc.vector.tensor_scalar_add(part, part, 1.0).then_inc(glink, 1)
                    dve.wait_ge(glink, done + 1)
                    nc.vector.reciprocal(part, part).then_inc(glink, 1)
                    dve.wait_ge(glink, done + 2)
                    nc.vector.scalar_tensor_tensor(part, gate_in[:, bass.ds(BT * b + HT * hf, HT), :], gate_scale, part,
                                                   ALU.mult, ALU.mult).then_inc(gated, 1)

                def step(b, at):
                    for k, end in enumerate(ends):
                        if at == end + LAG:
                            dve.wait_ge(pv_done[end % PR], pv_count(end, b))
                            if k >= 2:
                                dve.wait_ge(job_rdy, JOBS * b + turn_index(k - 2) + 1)
                            else:
                                reached(dve, job_rdy, JOBS * b + turn_index(ENDS + k - 2) + 1 - JOBS)
                            nc.vector.tensor_copy(o_sb[k % 2][:, :], o_ps[:, :]).then_inc(o_in, 1)
                            if end in GATE_ENDS:
                                finish_gate(b, GATE_ENDS.index(end))
                    for index, kind, k in jobs_at(at):
                        dve.wait_ge(job_rdy, JOBS * b + index + 1)
                        if kind == "turn":
                            g, qh = k // 2, k % 2
                            heads = job_ps[:, :].rearrange("p (t h w) -> p t h w", t=HT, w=32)
                            nc.vector.reciprocal(recip[:, :, :], heads[:, :, :, D]).then_inc(glink, 1)
                            dve.wait_ge(glink, LINKS * b + k + 1 + 2 * (k >= 2) + 2 * (k >= 4))
                            nc.vector.tensor_tensor(
                                tok[:, HT * qh:HT * qh + HT, G * D * g:G * D * g + G * D].rearrange("p t (h d) -> p t h d", d=D),
                                heads[:, :, :, 0:D],
                                recip[:, :, :].rearrange("p t (h o) -> p t h o", o=1).broadcast_to([P, HT, G, D]),
                                ALU.mult).then_inc(job_read, 1)
                            if first and k < NG:
                                spike(nc, dve, s["y"][:, bass.ds(BT * b + 2 * k, 2), :], mem, count, spikes,
                                      SPIKE_STEPS * (NG * b + k))
                        elif kind == "back":
                            nc.vector.tensor_copy(chan[:, :], job_ps[:, :]).then_inc(job_read, 1)
                        else:
                            reached(dve, updated, 2 * b + k - 1)
                            skip = (s["xn"][:, bass.ds(BT * b + HT * k, HT), :] if first
                                    else s["bo"][:, 1:2, :].broadcast_to([P, HT, C]))
                            nc.vector.tensor_tensor(mix[k][:, :, :], job_ps[:, :].rearrange("p (t c) -> p t c", c=C),
                                                    skip, ALU.add).then_inc(job_read, 1)

                def trip(b, own, late):
                    for at in range(S if own else TAIL):
                        if late:
                            step(b - 1, at + S)
                        if own:
                            step(b, at)

                trips(dve, trip)

            @block.tensor
            def _(pe):
                pe.wait_ge(o_clear, 1)

                def score(b, j):
                    g, n = j // L, j // L % 2
                    qh, kt, q0, _, _ = groups[j % L]
                    if j % L == 0:
                        pe.wait_ge(staged[n], 160 * b + 80 * (g // 2) + 80)
                    diagonal = causal and kt // HT == qh
                    for pair in range(2):
                        unit = 2 * j + pair
                        slot = unit % SC
                        reached(pe, exp_done[slot], exp_count(unit, b) - 1)
                        for i in range(2):
                            part = slice(64 * i, 64 * i + ROWS)
                            ins = nc.tensor.matmul(scores[slot][:, i, 0:HALF - q0], k_st[n][part, pair, kt * P:(kt + 1) * P],
                                                   q_st[n][part, pair, qh * HALF + q0:(qh + 1) * HALF],
                                                   start=True, stop=not diagonal)
                        if diagonal:
                            for i in range(2):
                                ins = nc.tensor.matmul(scores[slot][:, i, 0:P], s["ident_bf"][:, :], s["mask_kq"][:, :],
                                                       start=False, stop=True)
                        ins.then_inc(scored, 1)

                def product(b, j):
                    n = j // L % 2
                    qh, kt, q0, opens, closes = groups[j % L]
                    pe.wait_ge(exp_done[(2 * j + 1) % SC], exp_count(2 * j + 1, b))
                    if opens:
                        reached(pe, o_in, ENDS * b + 2 * (j // L) + qh)
                    for h in range(G):
                        ins = nc.tensor.matmul(o_ps[32 * h:32 * h + VW, q0:HALF], v_st[n][:, kt, h, :],
                                               probs[j % PR][:, h, 0:HALF - q0], start=opens, stop=closes,
                                               tile_position=(0, 32 * h))
                    ins.then_inc(pv_done[j % PR], 1)

                def job(b, index, kind, k):
                    reached(pe, job_read, JOBS * b + index)
                    if kind == "turn":
                        pe.wait_ge(o_in, ENDS * b + k + 1)
                    for t in range(HT):
                        tile = slice(t * P, (t + 1) * P)
                        if kind == "turn":
                            ins = nc.tensor.transpose(job_ps[:, tile], o_sb[k % 2][:, tile], s["ident"][:, :])
                        elif kind == "back":
                            ins = nc.tensor.transpose(job_ps[:, tile], tok[:, HT * k + t, :], s["ident"][:, :])
                        else:
                            ins = nc.tensor.matmul(job_ps[:, tile], chan[:, tile], s["wo"][:, layer, :], start=True, stop=True)
                    ins.then_inc(job_rdy, 1)

                def trip(b, own, late):
                    for at in range(S if own else TAIL):
                        if own:
                            score(b, at)
                        if at >= LAG and own:
                            product(b, at - LAG)
                        if at < LAG and late:
                            product(b - 1, at - LAG + S)
                        if late:
                            for one in jobs_at(at + S):
                                job(b - 1, *one)
                        if own:
                            for one in jobs_at(at):
                                job(b, *one)

                trips(pe, trip)
        sem.wiped()


def spike(nc, dve, y, mem, count, sem, base):
    ch = Chain(dve, sem, base)
    m0 = y
    ch.after(nc.vector.tensor_scalar(count[:, :, :], y, 1.0, None, ALU.is_gt))
    for step in range(1, STEPS):
        m1 = mem[step % 2]
        ch.after(nc.vector.scalar_tensor_tensor(m1[:, :, :], m0, BETA, y, ALU.mult, ALU.add))
        ch.after(nc.vector.scalar_tensor_tensor(m1[:, :, :], m0, 1.0, m1[:, :, :], ALU.is_gt, ALU.subtract, reverse1=True))
        last = step == STEPS - 1
        ch.after(nc.vector.scalar_tensor_tensor(y if last else count[:, :, :], m1[:, :, :], 1.0, count[:, :, :],
                                                ALU.is_gt, ALU.add))
        m0 = m1[:, :, :]


def coupling(nc, a, s):
    with ExitStack() as ctx:
        def sb(name, shape, dt=F32):
            return ctx.enter_context(nc.sbuf_tensor(f"n_{name}", shape, dt))

        sem = Semaphores(nc, ctx, f"n_")

        H1, H2 = C // 2, C // 4
        Q = P // 4
        w1, w2, w3, w4 = sb("w1", [C, C]), sb("w2", [C, H1]), sb("w3", [2 * H1, 2 * H2]), sb("w4", [2 * H2, 2])
        g1, g2, g3 = sb("g1", [C, H1]), sb("g2", [H1, H2]), sb("g3", [H2, 1])
        w4_all, g3_all = sb("w4_all", [2 * H2, 2, P]), sb("g3_all", [H2, P])
        b1, b2, b3 = sb("b1", [C, 1]), sb("b2", [2 * H1, 1]), sb("b3", [2 * H2, 1])
        gb1, gb2 = sb("gb1", [H1, 1]), sb("gb2", [H2, 1])
        scalars = sb("scalars", [1, 4])
        ones = sb("ones", [1, P])
        col = sb("col", [P, 8])
        twist = sb("twist", [P, P])
        mean = sb("mean", [P, B])
        u1, u2 = sb("gu1", [H1, B]), sb("gu2", [H2, B])
        gf = sb("gf", [P, B])
        offset = sb("offset", [P, B])
        h1 = [[sb(f"h1_{z}{hf}", [C, HALF]) for hf in range(2)] for z in range(2)]
        h2 = [sb(f"h2_{z}", [2 * H1, HALF]) for z in range(2)]
        h3 = [sb(f"h3_{z}", [2 * H2, HALF]) for z in range(2)]
        th = [[sb(f"th{z}{hf}", [P, HALF]) for hf in range(2)] for z in range(2)]
        ps = [[ctx.enter_context(nc.psum_tensor(f"n_ps{z}_{k}", [P, HALF], F32)) for k in range(4)] for z in range(2)]
        load, wide, const, gps, gact, chain, gready = (sem(x) for x in (
            "load", "wide", "const", "gps", "gact", "chain", "gready"))
        layered, squashed = sem("layered"), sem("squashed")
        twisted, link, updated = sem("twisted"), sem("link"), sem("updated")
        turned, kept = sem("turned"), sem("kept")
        xt = s["y"][:, :, :].rearrange("p t c -> p (t c)")
        LAYERED, TWISTED = 12, 4
        PAIRS = B // 2
        LOADS = 19

        def layer_index(layer, z, hf=0):
            return {1: 2 * z + hf, 2: 4 + z, 3: 6 + z, 4: 8 + 2 * z + hf}[layer]

        def layer_count(c, pair, index):
            return LAYERED * PAIRS * c + LAYERED * pair + index + 1

        def twist_count(c, pair, z, hf):
            return TWISTED * PAIRS * c + TWISTED * pair + 2 * z + hf + 1

        def state(pair, z, hf):
            at = (2 * pair + z) * T + HALF * hf
            return xt[:, at:at + HALF]

        def column(name):
            return a[name].rearrange("(c o) -> c o", o=1)

        with nc.Block() as block:
            @block.sync
            def _(sp):
                sp.wait_ge(wide, 1)
                pairs = [(g1[:, :], a["L1_ffn_gc_w1"]), (g2[:, :], a["L1_ffn_gc_w2"]),
                         (g3[:, :], a["L1_ffn_gc_w3"]), (gb1[:, :], column("L1_ffn_gc_b1")),
                         (gb2[:, :], column("L1_ffn_gc_b2")), (scalars[:, 0:1], column("L1_ffn_cn_b4")),
                         (scalars[:, 1:2], column("L1_ffn_gc_b3")), (scalars[:, 2:3], column("L1_ffn_adaptive_range")),
                         (w1[:, :], a["L1_ffn_cn_w1"]), (w2[:, :], a["L1_ffn_cn_w2"]), (b1[:, :], column("L1_ffn_cn_b1"))]
                for hf in range(2):
                    wide_of, narrow_of = slice(H1 * hf, H1 * hf + H1), slice(H2 * hf, H2 * hf + H2)
                    pairs += [(w3[wide_of, narrow_of], a["L1_ffn_cn_w3"]), (w4[narrow_of, hf:hf + 1], a["L1_ffn_cn_w4"]),
                              (b2[wide_of, :], column("L1_ffn_cn_b2")), (b3[narrow_of, :], column("L1_ffn_cn_b3"))]
                assert len(pairs) == LOADS
                for dst, src in pairs:
                    sp.dma_start(dst, src).then_inc(load, 16)

            @block.scalar
            def _(act):
                act.wait_ge(gps, 1)
                nc.scalar.activation(u1[:, :], ps[0][0][0:H1, 0:B], ACT.Gelu, bias=gb1[:, :]).then_inc(gact, 1)
                act.wait_ge(gps, 2)
                nc.scalar.activation(u2[:, :], ps[0][1][0:H2, 0:B], ACT.Gelu, bias=gb2[:, :]).then_inc(gact, 1)
                act.wait_ge(gps, 3)
                act.wait_ge(gready, 1)
                nc.scalar.activation(gf[:, :], ps[0][2][:, 0:B], ACT.Tanh, bias=col[:, 1:2], scale=0.5).then_inc(gact, 1)

                def cycle(c):
                    for pair in range(PAIRS):
                        for z in range(2):
                            for hf in range(2):
                                act.wait_ge(layered, layer_count(c, pair, layer_index(1, z, hf)))
                                nc.scalar.activation(h1[z][hf][:, :], ps[z][hf][:, :], ACT.Gelu, bias=b1[:, :]).then_inc(squashed, 1)
                        for z in range(2):
                            act.wait_ge(layered, layer_count(c, pair, layer_index(2, z)))
                            nc.scalar.activation(h2[z][:, :], ps[z][2][:, :], ACT.Gelu, bias=b2[:, :]).then_inc(squashed, 1)
                        for z in range(2):
                            act.wait_ge(layered, layer_count(c, pair, layer_index(3, z)))
                            nc.scalar.activation(h3[z][:, :], ps[z][3][0:2 * H2, :], ACT.Gelu, bias=b3[:, :]).then_inc(squashed, 1)
                        for z in range(2):
                            for hf in range(2):
                                act.wait_ge(layered, layer_count(c, pair, layer_index(4, z, hf)))
                                reached(act, updated, twist_count(c, pair, z, hf) - TWISTED)
                                nc.scalar.activation(th[z][hf][:, :], ps[z][hf][:, :], ACT.Tanh, bias=col[:, 0:1],
                                                     scale=0.5).then_inc(squashed, 1)

                after_first(act, CYCLES, cycle)
                for k in range(2 * B):
                    act.wait_ge(turned, k + 1)
                    nc.scalar.copy(s["xn"][:, HT * k:HT * k + HT, :],
                                   ps[k % 2][k // 2 % 2][:, :].rearrange("p (t c) -> p t c", c=C)).then_inc(kept, 1)

            @block.vector
            def _(dve):
                ch = Chain(dve, chain)
                nc.vector.memset(w3[:, :], 0.0)
                nc.vector.memset(w4[:, :], 0.0).then_inc(wide, 1)
                nc.vector.memset(ones[:, :], 1.0).then_inc(const, 1)
                ch.after(nc.vector.memset(twist[:, :], 0.0))
                for dst, src, sign in ((0, 2, 1.0), (1, 3, -1.0), (2, 0, -1.0), (3, 1, 1.0)):
                    r = slice(Q * src, Q * src + Q)
                    ch.mark(nc.vector.tensor_scalar_mul(twist[r, Q * dst:Q * dst + Q], s["ident"][r, r], sign))
                ch.after(nc.vector.reduce_sum(mean[:, :], xt.rearrange("p (b t) -> p b t", b=B), axis=AX.X))
                ch.mark(nc.vector.tensor_scalar_mul(mean[:, :], mean[:, :], 1.0 / T))
                dve.wait_ge(load, 16 * LOADS)
                for hf in range(2):
                    ch.mark(nc.vector.tensor_copy(w4_all[:, hf, :], w4[:, hf:hf + 1].broadcast_to([2 * H2, P])))
                nc.vector.tensor_copy(g3_all[:, :], g3[:, :].broadcast_to([H2, P])).then_inc(const, 1)
                dve.wait_ge(gps, 3)
                ch.after(nc.vector.tensor_copy(col[:, 2:5], ps[0][3][:, 0:3]))
                ch.mark(nc.vector.tensor_scalar_mul(col[:, 0:2], col[:, 2:4], 0.5))
                ch.mark(nc.vector.tensor_scalar_mul(col[:, 5:6], col[:, 4:5], 0.3))
                nc.vector.tensor_scalar_mul(col[:, 6:7], col[:, 4:5], 2.0).then_inc(gready, 1)
                dve.wait_ge(gready, 1)
                ch.wait()
                dve.wait_ge(gact, 3)
                ch.after(nc.vector.tensor_scalar(offset[:, :], gf[:, :], 0.35, col[:, 6:7], ALU.mult, ALU.mult))
                ch.after(nc.vector.tensor_scalar_add(offset[:, :], offset[:, :], 0.1))

                def cycle(c):
                    for pair in range(PAIRS):
                        for z in range(2):
                            for hf in range(2):
                                done = 2 * (twist_count(c, pair, z, hf) - 1)
                                t = th[z][hf][:, :]
                                b = 2 * pair + z
                                dve.wait_ge(squashed, layer_count(c, pair, layer_index(4, z, hf)))
                                nc.vector.tensor_scalar(t, t, col[:, 5:6], offset[:, b:b + 1], ALU.mult, ALU.add).then_inc(link, 1)
                                dve.wait_ge(link, done + 1)
                                dve.wait_ge(twisted, twist_count(c, pair, z, hf))
                                nc.vector.tensor_tensor(t, t, ps[z][2 + hf][:, :], ALU.mult).then_inc(link, 1)
                                dve.wait_ge(link, done + 2)
                                out = state(pair, z, hf)
                                nc.vector.tensor_tensor(out, out, t, ALU.add).then_inc(updated, 1)

                after_first(dve, CYCLES, cycle)

            @block.tensor
            def _(pe):
                pe.wait_ge(const, 2)
                pe.wait_ge(chain, 9)
                nc.tensor.matmul(ps[0][0][0:H1, 0:B], g1[:, :], mean[:, :], start=True, stop=True).then_inc(gps, 1)
                nc.tensor.matmul(ps[0][3][:, 0:3], ones[:, :], scalars[:, 0:3], start=True, stop=True)
                pe.wait_ge(gact, 1)
                nc.tensor.matmul(ps[0][1][0:H2, 0:B], g2[:, :], u1[:, :], start=True, stop=True).then_inc(gps, 1)
                pe.wait_ge(gact, 2)
                nc.tensor.matmul(ps[0][2][:, 0:B], g3_all[:, :], u2[:, :], start=True, stop=True).then_inc(gps, 1)
                pe.wait_ge(gact, 3)
                pe.wait_ge(gready, 1)

                def cycle(c):
                    for pair in range(PAIRS):
                        for z in range(2):
                            for hf in range(2):
                                reached(pe, squashed, layer_count(c, pair, layer_index(4, z, hf)) - LAYERED)
                                reached(pe, updated, twist_count(c, pair, z, hf) - TWISTED * PAIRS)
                                nc.tensor.matmul(ps[z][hf][:, :], w1[:, :], state(pair, z, hf), start=True, stop=True).then_inc(layered, 1)
                        for z in range(2):
                            pe.wait_ge(squashed, layer_count(c, pair, layer_index(1, z, 1)))
                            reached(pe, updated, twist_count(c, pair, z, 0) - TWISTED)
                            for hf in range(2):
                                ins = nc.tensor.matmul(ps[z][2][H1 * hf:H1 * hf + H1, :], w2[:, :], h1[z][hf][:, :],
                                                       start=True, stop=True, tile_position=(0, H1 * hf))
                            ins.then_inc(layered, 1)
                        for z in range(2):
                            pe.wait_ge(squashed, layer_count(c, pair, layer_index(2, z)))
                            reached(pe, updated, twist_count(c, pair, z, 1) - TWISTED)
                            nc.tensor.matmul(ps[z][3][0:2 * H2, :], w3[:, :], h2[z][:, :], start=True, stop=True).then_inc(layered, 1)
                        for z in range(2):
                            pe.wait_ge(squashed, layer_count(c, pair, layer_index(3, z)))
                            for hf in range(2):
                                nc.tensor.matmul(ps[z][hf][:, :], w4_all[:, hf, :], h3[z][:, :], start=True, stop=True).then_inc(layered, 1)
                            for hf in range(2):
                                nc.tensor.matmul(ps[z][2 + hf][:, :], twist[:, :], state(pair, z, hf), start=True,
                                                 stop=True).then_inc(twisted, 1)

                after_first(pe, CYCLES, cycle)
                for k in range(2 * B):
                    if k >= 4:
                        pe.wait_ge(kept, k - 3)
                    else:
                        pe.wait_ge(updated, TWISTED * PAIRS * CYCLES - 4 + 2 * (k % 2) + k // 2 + 1)
                    pe.wait_ge(updated, TWISTED * PAIRS * (CYCLES - 1) + k + 1)
                    for t in range(HT):
                        ins = nc.tensor.transpose(ps[k % 2][k // 2 % 2][:, t * P:(t + 1) * P],
                                                  s["y"][:, HT * k + t, :], s["ident"][:, :])
                    ins.then_inc(turned, 1)
        sem.wiped()


_INS = ["L0_attn_x", "L0_attn_ln_gamma", "L0_attn_ln_beta", "L0_attn_w_qkv", "L0_attn_b_qkv", "L0_attn_w_out",
        "L0_attn_b_out", "L0_ffn_W_fc", "L0_ffn_W_proj", "L1_attn_Wq", "L1_attn_bq", "L1_attn_Wk", "L1_attn_bk",
        "L1_attn_Wv", "L1_attn_bv", "L1_attn_Wo", "L1_attn_bo", "L1_ffn_cn_w1", "L1_ffn_cn_b1", "L1_ffn_cn_w2",
        "L1_ffn_cn_b2", "L1_ffn_cn_w3", "L1_ffn_cn_b3", "L1_ffn_cn_w4", "L1_ffn_cn_b4", "L1_ffn_gc_w1", "L1_ffn_gc_b1",
        "L1_ffn_gc_w2", "L1_ffn_gc_b2", "L1_ffn_gc_w3", "L1_ffn_gc_b3", "L1_ffn_adaptive_range"]


def position_rows():
    slopes = 2.0 ** (-8.0 * (np.arange(H) + 1) / H)
    shift = (slopes.astype(np.float32)[:, None] * (T - 1 - np.arange(T, dtype=np.float32))).astype(np.float32)
    q = np.zeros((2, ROWS - SPLIT_ROWS, H, T), np.uint16)
    k = np.zeros((2, ROWS - SPLIT_ROWS, H, T), np.uint16)
    q[:, 3:6], k[:, :3] = 0x3F80, 0x3F80
    rest = shift.copy()
    for n in range(3):
        part = rest.view(np.uint32) & np.uint32(0xFFFF0000)
        q[1, n], k[1, 3 + n] = part >> 16, (part >> 16) | (part != 0) * 0x8000
        rest = rest - part.view(np.float32)
    base = np.zeros((2, P, BT, H), np.float32)
    base[1] = shift.reshape(H, BT, P).transpose(2, 1, 0)
    return {"q_extra": q, "k_extra": k, "q_shift": base}


def kernel(**inputs):
    import concourse.bacc as _bacc
    from concourse.bass_utils import run_bass_kernel_spmd as _run

    nc = _bacc.Bacc("TRN2", target_bir_lowering=False, num_devices=1)
    arrays, args = {}, {}
    for name, value in [(n, inputs[n]) for n in _INS] + list(position_rows().items()):
        x = np.ascontiguousarray(value)
        arrays[f"in_{name}_dram"] = x
        args[name] = nc.dram_tensor(f"in_{name}_dram", x.shape, mybir.dt.from_np(x.dtype), kind="ExternalInput").ap()
    args["out"] = nc.dram_tensor("out_0_dram", (B, T, C), F32, kind="ExternalOutput").ap()
    build(nc, args)
    r = _run(nc, [arrays], core_ids=[0])
    return r.results[0]["out_0_dram"]
```

```python
from contextlib import ExitStack

import numpy as np

import concourse.bass as bass
from concourse import mybir

F32 = mybir.dt.float32
BF16 = mybir.dt.bfloat16
I32 = mybir.dt.int32
ALU = mybir.AluOpType
ACT = mybir.ActivationFunctionType
AX = mybir.AxisListType

P = 128
B, T, C = 4, 1024, 128
H, D = 16, 8
N = B * T
NT = N // P
BT = T // P
HALF = 512
HT = HALF // P
G = 4
NG = H // G
FF = 512
FC = FF // P
SCALE = float(D) ** -0.5
EPS = 1e-5
RUNS = ((0, 3), (3, 2), (5, 1))
SPLIT_ROWS = D * 6
ROWS = 64
VW = 16
BOUND = 60.0
STEPS = 5
BETA = 0.9
MASK = -1.0e30
CYCLES = 3
ROOT_GUESS = 0x5F3759DF


H1, H2 = C // 2, C // 4
COUPLING_WEIGHTS = {
    "w1": [C, C], "w2": [C, H1], "w3": [2 * H1, 2 * H2], "w4": [2 * H2, 2], "b1": [C, 1], "b2": [2 * H1, 1],
    "b3": [2 * H2, 1], "g1": [C, H1], "g2": [H1, H2], "g3": [H2, 1], "gb1": [H1, 1], "gb2": [H2, 1],
    "scalars": [1, 4],
}
COUPLING_LOADS = 19


class Semaphores:

    def __init__(self, nc, ctx, prefix):
        self.nc, self.ctx, self.prefix, self.all = nc, ctx, prefix, []

    def __call__(self, name):
        self.all.append(self.ctx.enter_context(self.nc.semaphore(f"{self.prefix}{name}")))
        return self.all[-1]

    def pair(self, name):
        return self.many(name, 2)

    def many(self, name, n):
        return [self(f"{name}{k}") for k in range(n)]

    def wiped(self):
        ids = sorted(h.num for h in self.all)
        firsts = [n for n in ids if n - 1 not in ids]
        with self.nc.Block() as block:
            @block.sync
            def _(sp):
                for n in firsts:
                    end = next(m for m in range(n, n + len(ids) + 1) if m not in ids)
                    sp.sem_clear(range(n, end))


def reached(eng, sem, count):
    if not (isinstance(count, int) and count <= 0):
        eng.wait_ge(sem, count)


def after_first(eng, count, body):
    body(0)
    with eng.Fori(1, count) as i:
        body(i)


def trips(eng, body, runs_ahead=False):
    loop_end = B - 1 if runs_ahead else B
    body(0, True, False)
    with eng.Fori(1, loop_end) as b:
        body(b, True, True)
    if runs_ahead:
        body(B - 1, True, True)
    body(B, False, True)


class Chain:

    def __init__(self, eng, sem, base=0):
        self.eng, self.sem, self.base, self.n = eng, sem, base, 0

    def mark(self, ins):
        self.n += 1
        ins.then_inc(self.sem, 1)

    def wait(self):
        self.eng.wait_ge(self.sem, self.base + self.n)

    def after(self, ins):
        self.mark(ins)
        self.wait()


def build(nc, a):
    x_t = a["L0_attn_x"].rearrange("b (t p) c -> p (b t) c", p=P)
    out_t = a["out"].rearrange("b (t p) c -> p (b t) c", p=P)
    q_rows = [nc.dram_tensor(f"q_rows{n}", [ROWS, H, N], BF16).ap() for n in range(2)]
    k_rows = [nc.dram_tensor(f"k_rows{n}", [ROWS, H, N], BF16).ap() for n in range(2)]

    with ExitStack() as ctx:
        def sb(name, shape, dt=F32):
            return ctx.enter_context(nc.sbuf_tensor(name, shape, dt))

        s = {
            "ident": sb("ident", [P, P]), "ident_bf": sb("ident_bf", [P, P], BF16),
            "mask_kq": sb("mask_kq", [P, P], BF16),
            "mask_qk": sb("mask_qk", [P, P], BF16),
            "x": sb("x", [P, NT, C]),
            "xn": sb("xn", [P, NT, C]),
            "y": sb("y", [P, NT, C]),
            "v": sb("v", [P, NT, H, VW]),
            "flag": sb("flag", [1, 1], I32),
            "mean": sb("mean", [P, NT]), "rstd": sb("rstd", [P, NT]),
            "xn_sums": sb("xn_sums", [P, 2 * B]),
            "wo": sb("wo", [P, 2, C]),
            "bo": sb("bo", [P, 2, C]),
        }
        s["cn"] = {name: sb(f"cn_{name}", shape) for name, shape in COUPLING_WEIGHTS.items()}
        s["parts"] = [sb(f"parts{hf}", [P, 2, 3, HALF], BF16) for hf in range(2)]
        s["ctx"] = ctx
        for name in ("x_first", "x_rest", "cn_zeroed", "cn_in", "zeroed", "made", "stored00", "stored01", "stored10",
                     "stored11"):
            s[name] = ctx.enter_context(nc.semaphore(name))
        prepare(nc, a, s, 0, q_rows[0], k_rows[0], x_t)
        row_maxima(nc, a, s, 0, q_rows[0], k_rows[0])
        attention(nc, a, s, 0, q_rows[0], k_rows[0], None)
        prepare(nc, a, s, 1, q_rows[1], k_rows[1], None)
        coupling(nc, a, s)
        row_maxima(nc, a, s, 1, q_rows[1], k_rows[1])
        attention(nc, a, s, 1, q_rows[1], k_rows[1], out_t)


def constants_on_pool(nc, pool, s):
    zero, made = s["zeroed"], s["made"]
    pool.memset(s["ident"][:, :], 0.0).then_inc(zero, 1)
    pool.wait_ge(zero, 1)
    pool.affine_select(out=s["ident"][:, :], in_=s["ident"][:, :], compare_op=ALU.not_equal, fill=1.0,
                       base=0, pattern=[[-1, P]], channel_multiplier=1).then_inc(made, 1)
    pool.wait_ge(made, 1)
    pool.tensor_copy(s["ident_bf"][:, :], s["ident"][:, :])
    pool.memset(s["mask_kq"][:, :], 0.0)
    pool.memset(s["mask_qk"][:, :], 0.0).then_inc(zero, 1)
    pool.wait_ge(zero, 2)
    for mask, sign in ((s["mask_kq"], 1), (s["mask_qk"], -1)):
        pool.affine_select(out=mask[:, :], in_=mask[:, :], compare_op=ALU.is_ge, fill=MASK, base=0,
                           pattern=[[sign, P]], channel_multiplier=-sign)


NEWTON = 3
MOMENT_STEPS = 5 + 3 * NEWTON


def moment_tiles(sb, n):
    return {"stats": sb("stats", [P, n, 6]), "moments": sb("moments", [P, n, 2]), "var": sb("var", [P, n]),
            "fix": sb("fix", [P, n]), "root": sb("root", [P, n])}


def token_moments(nc, dve, sources, work, rstd, sem, base):
    some = len(sources)
    stats, moments = work["stats"], work["moments"]
    v, f, r = (work[x][:, 0:some] for x in ("var", "fix", "root"))
    for n, (src, t) in enumerate(sources):
        nc.vector.bn_stats(stats[:, n, :], src(t)).then_inc(sem, 1)
    at = base + some
    dve.wait_ge(sem, at)
    dve.sem_inc(sem, 1)
    for n in range(some):
        ins = nc.vector.bn_aggr(moments[:, n, :], stats[:, n, :])
    ins.then_inc(sem, 1)
    dve.wait_ge(sem, at + 2)
    nc.vector.tensor_scalar_add(v, moments[:, 0:some, 1], EPS).then_inc(sem, 1)
    dve.wait_ge(sem, at + 3)
    nc.vector.tensor_scalar(r.bitcast(I32), v.bitcast(I32), 1, None, ALU.logical_shift_right).then_inc(sem, 1)
    dve.wait_ge(sem, at + 4)
    nc.vector.tensor_scalar(r.bitcast(I32), r.bitcast(I32), -1, ROOT_GUESS, ALU.mult, ALU.add).then_inc(sem, 1)
    dve.wait_ge(sem, at + 5)
    for n in range(NEWTON):
        nc.vector.scalar_tensor_tensor(f, r, -0.5, r, ALU.mult, ALU.mult).then_inc(sem, 1)
        dve.wait_ge(sem, at + 5 + 3 * n + 1)
        nc.vector.tensor_tensor(f, f, v, ALU.mult).then_inc(sem, 1)
        dve.wait_ge(sem, at + 5 + 3 * n + 2)
        nc.vector.scalar_tensor_tensor(rstd if n == NEWTON - 1 else r, f, 1.5, r, ALU.add, ALU.mult).then_inc(sem, 1)
        dve.wait_ge(sem, at + 5 + 3 * n + 3)


def prepare(nc, a, s, layer, q_rows, k_rows, x_t):
    first = layer == 0
    with ExitStack() as ctx:
        def sb(name, shape, dt=F32):
            return ctx.enter_context(nc.sbuf_tensor(f"p{layer}_{name}", shape, dt))

        def ps(name, shape=(P, HALF)):
            return ctx.enter_context(nc.psum_tensor(f"p{layer}_{name}", list(shape), F32))

        sem = Semaphores(nc, ctx if first else s["ctx"], f"p{layer}_")

        KN = 32
        w = sb("w", [P, 3, C])
        wqk = sb("wqk", [P, 2, C])
        b_row = sb("b_row", [1, 3, C])
        bqk_row = sb("bqk_row", [1, 2, C])
        b_col = sb("b_col", [P, 2])
        bv = sb("bv", [P, HT, C])
        norm_col = sb("norm_col", [P, 2])
        ones = sb("ones", [P, P])
        head_of = sb("head_of", [P, KN], BF16)
        if first:
            work = moment_tiles(sb, 2 * HT)
            rstd = sb("rstd", [P, 2 * HT])
        xs = [sb(f"xs{hf}", [P, HT, C]) for hf in range(2)]
        hs = [sb(f"hs{hf}", [P, HT, C]) for hf in range(2)] if first else xs
        x_ch = [sb(f"x_ch{hf}", [P, HALF]) for hf in range(2)]
        h_ch = [sb(f"h_ch{hf}", [P, HALF]) for hf in range(2)] if first else x_ch
        qk = [sb(f"qk{hf}", [P, 2, HALF]) for hf in range(2)]
        rest = sb("rest", [P, 2, HALF])
        parts = s["parts"]
        square = [sb(f"square{hf}", [P, 2, HALF], BF16) for hf in range(2)]
        norms = sb("norms", [2 * KN, 2 * B])
        top = sb("top", [2 * KN, 1])
        peak = sb("peak", [1, 2 * KN])
        if first:
            bo_row = sb("bo_row", [1, 2, C])
            fc = sb("fc", [P, FC, C])
            proj = sb("proj", [P, FF])
            fc_t = sb("fc_t", [P, FC, P])
            proj_t = sb("proj_t", [P, FC, C])
            relu = sb("relu", [P, FC, HALF])
            hidden = sb("hidden", [P, FC, HALF])

        tr_x, tr_h, pq, pk, pv = ps("tr_x"), ps("tr_h"), ps("pq"), ps("pk"), ps("pv")
        pf = [ps("pf0"), ps("pf1")]
        py = ps("py")
        pn = pq if first else pf[0]

        headed = sem("headed")
        w_in, ffn_in, const, perm, bias_ps, wt_ps, wt_in = (sem(x) for x in (
            "w_in", "ffn_in", "const", "perm", "bias_ps", "wt_ps", "wt_in"))
        bias_in, tail, tail_ps, ln = sem("bias_in"), sem("tail"), sem("tail_ps"), sem("ln")
        xs_rdy, hs_rdy, trx_rdy, trh_rdy, xch_rdy, hch_rdy = (sem(x) for x in (
            "xs_rdy", "hs_rdy", "trx_rdy", "trh_rdy", "xch_rdy", "hch_rdy"))
        qk_ps, qk_in, part0_rdy, rest_rdy, part1_rdy, parts_rdy = (sem(x) for x in (
            "qk_ps", "qk_in", "part0_rdy", "rest_rdy", "part1_rdy", "parts_rdy"))
        v_ps, v_in, sq_rdy, norm_ps, norm_in = (sem(x) for x in ("v_ps", "v_in", "sq_rdy", "norm_ps", "norm_in"))
        f_ps, relu_in, hid_rdy, y_ps, y_in, xn_in = (sem(x) for x in (
            "f_ps", "relu_in", "hid_rdy", "y_ps", "y_in", "xn_in"))
        mean_ps, mean_in, rows_in, bo_in = sem("mean_ps"), sem("mean_in"), sem("rows_in"), sem("bo_in")
        stored = [s[f"stored{layer}{hf}"] for hf in range(2)]
        if not first:
            hs_rdy, trh_rdy, hch_rdy = xs_rdy, trx_rdy, xch_rdy

        def steps(body):
            def trip(b, own, late):
                for hf in range(2 if own else 1):
                    body(2 * b + hf, hf, BT * b + HT * hf, own, late or hf == 1)
            return trip

        with nc.Block() as block:
            @block.sync
            def _(sp):
                if first:
                    sp.dma_start(s["x"][:, 0:BT, :], x_t[:, 0:BT, :]).then_inc(s["x_first"], 16)
                    sp.dma_start(w[:, :, :], a["L0_attn_w_qkv"].rearrange("k (n c) -> k n c", n=3)).then_inc(w_in, 16)
                    sp.dma_start(b_row[:, :, :], a["L0_attn_b_qkv"].rearrange("(o n c) -> o n c", o=1, n=3)).then_inc(w_in, 16)
                    sp.dma_start(norm_col[:, 0:1], a["L0_attn_ln_gamma"].rearrange("(c o) -> c o", o=1)).then_inc(w_in, 16)
                    sp.dma_start(norm_col[:, 1:2], a["L0_attn_ln_beta"].rearrange("(c o) -> c o", o=1)).then_inc(w_in, 16)
                    sp.dma_start(fc[:, :, :], a["L0_ffn_W_fc"].rearrange("(n f) c -> f n c", f=P)).then_inc(ffn_in, 16)
                    sp.dma_start(proj[:, :], a["L0_ffn_W_proj"]).then_inc(ffn_in, 16)
                else:
                    for n, name in enumerate("qkv"):
                        sp.dma_start(w[:, n, :], a[f"L1_attn_W{name}"]).then_inc(w_in, 16)
                        sp.dma_start(b_row[:, n, :], a[f"L1_attn_b{name}"].rearrange("(o c) -> o c", o=1)).then_inc(w_in, 16)
                if first:
                    sp.dma_start(bo_row[:, 0, :], a["L0_attn_b_out"].rearrange("(o c) -> o c", o=1)).then_inc(bo_in, 16)
                    sp.dma_start(bo_row[:, 1, :], a["L1_attn_bo"].rearrange("(o c) -> o c", o=1)).then_inc(bo_in, 16)
                    for b in range(1, B):
                        later = slice(b * BT, (b + 1) * BT)
                        sp.dma_start(s["x"][:, later, :], x_t[:, later, :]).then_inc(s["x_rest"], 16)
                    sp.dma_start(s["wo"][:, 0, :], a["L0_attn_w_out"]).then_inc(rows_in, 16)
                    sp.dma_start(s["wo"][:, 1, :], a["L1_attn_Wo"]).then_inc(rows_in, 16)

                for b in range(B):
                    tok = slice(b * T, (b + 1) * T)
                    sp.dma_start(q_rows[SPLIT_ROWS:ROWS, :, tok], a["q_extra"][layer].bitcast(BF16)).then_inc(rows_in, 16)
                    sp.dma_start(k_rows[SPLIT_ROWS:ROWS, :, tok], a["k_extra"][layer].bitcast(BF16)).then_inc(rows_in, 16)

                if first:
                    sp.wait_ge(s["cn_zeroed"], 1)
                    load_coupling_weights(sp, a, s)

                def store(b):
                    for hf in range(2):
                        sp.wait_ge(parts_rdy, 2 * b + hf + 1)
                        tok = bass.ds(T * b + HALF * hf, HALF)
                        for part, (r, n) in enumerate(RUNS):
                            def blocks(rows):
                                return rows[D * r:D * r + D * n, :, tok].rearrange("(r d) h t -> (d h) r t", d=D)

                            same = parts[hf][:, 0, part:part + 1, :]
                            sp.dma_start(blocks(q_rows), same.broadcast_to([P, n, HALF])).then_inc(stored[hf], 16)
                            sp.dma_start(blocks(k_rows), parts[hf][:, 1, 0:n, :]).then_inc(stored[hf], 16)

                after_first(sp, B, store)
                sp.wait_ge(rows_in, 16 * (2 * B + 2 * first))

            @block.gpsimd
            def _(pool):
                if first:
                    constants_on_pool(nc, pool, s)
                pool.wait_ge(headed, 1)
                for d in range(D):
                    pool.affine_select(out=head_of[:, 0:H], in_=head_of[:, 0:H], compare_op=ALU.not_equal, fill=1.0,
                                       base=-H * d, pattern=[[-1, H]], channel_multiplier=1).then_inc(perm, 1)
                    pool.wait_ge(perm, d + 1)
                if first:
                    pool.memset(s["v"][:, :, :, D + 1:VW], 0.0)
                    pool.memset(s["v"][:, :, :, D:D + 1], 1.0)

                def step(b):
                    for hf in range(2):
                        m, tiles = 2 * b + hf, bass.ds(BT * b + HT * hf, HT)
                        if first:
                            pool.wait_ge(bias_in, 1)
                            pool.wait_ge(xs_rdy, m + 1)
                            pool.tensor_tensor(s["xn"][:, tiles, :], xs[hf][:, :, :],
                                               s["bo"][:, 0:1, :].broadcast_to([P, HT, C]), ALU.add).then_inc(xn_in, 1)
                            reached(pool, y_ps, m)
                            for f in range(FC):
                                pool.wait_ge(relu_in, FC * m + f + 1)
                                pool.tensor_tensor(hidden[:, f, :], relu[:, f, :], relu[:, f, :], ALU.mult).then_inc(hid_rdy, 1)
                        else:
                            pool.wait_ge(xch_rdy, m + 1)
                            pool.tensor_copy(s["y"][:, tiles, :],
                                             x_ch[hf][:, :].rearrange("p (t c) -> p t c", c=C)).then_inc(y_in, 1)

                after_first(pool, B, step)

            @block.scalar
            def _(act):
                act.wait_ge(w_in, 64 if first else 96)

                def step(m, hf, tiles, own, late):
                    def relus(fs):
                        for f in fs:
                            act.wait_ge(f_ps, FC * m + f + 1)
                            reached(act, hid_rdy, FC * m)
                            nc.scalar.activation(relu[:, f, :], pf[f % 2][:, :], ACT.Relu).then_inc(relu_in, 1)

                    if own:
                        act.wait_ge(trx_rdy, m + 1)
                        reached(act, v_ps, m - 1)
                        if first:
                            reached(act, f_ps, FC * (m - 1))
                        else:
                            reached(act, y_in, m - 1)
                        nc.scalar.copy(x_ch[hf][:, :], tr_x[:, :]).then_inc(xch_rdy, 1)
                        if first:
                            act.wait_ge(trh_rdy, m + 1)
                            nc.scalar.activation(h_ch[hf][:, :], tr_h[:, :], ACT.Identity, bias=norm_col[:, 1:2],
                                                 scale=norm_col[:, 0:1]).then_inc(hch_rdy, 1)
                    if late:
                        act.wait_ge(rest_rdy, m)
                        nc.scalar.copy(parts[1 - hf][:, :, 1, :], rest[:, :, :]).then_inc(part1_rdy, 1)
                    if own:
                        if first:
                            relus((0, 1))
                        act.wait_ge(qk_ps, 2 * m + 1)
                        act.wait_ge(bias_in, 1)
                        reached(act, parts_rdy, m - 1)
                        nc.scalar.activation(qk[hf][:, 0, :], pq[:, :], ACT.Identity, bias=b_col[:, 0:1],
                                             scale=SCALE).then_inc(qk_in, 1)
                        act.wait_ge(qk_ps, 2 * m + 2)
                        nc.scalar.activation(qk[hf][:, 1, :], pk[:, :], ACT.Identity, bias=b_col[:, 1:2]).then_inc(qk_in, 1)
                        act.wait_ge(qk_in, 2 * m + 2)
                        reached(act, stored[hf], 48 * (m - hf))
                        nc.scalar.copy(parts[hf][:, :, 0, :], qk[hf][:, :, :]).then_inc(part0_rdy, 1)
                        reached(act, norm_ps, m - 1)
                        nc.scalar.activation(square[hf][:, :, :], qk[hf][:, :, :], ACT.Square).then_inc(sq_rdy, 1)
                    if late and first:
                        act.wait_ge(y_ps, m)
                        last = tiles - HT
                        nc.scalar.copy(s["y"][:, bass.ds(last, HT), :],
                                       py[:, :].rearrange("p (t c) -> p t c", c=C)).then_inc(y_in, 1)
                    if own and first:
                        relus((2, 3))

                trips(act, steps(step))

            @block.vector
            def _(dve):
                nc.vector.memset(head_of[:, :], 0.0).then_inc(headed, 1)
                nc.vector.memset(ones[:, :], 1.0).then_inc(const, 1)
                if first:
                    nc.vector.memset(s["cn"]["w3"][:, :], 0.0)
                    nc.vector.memset(s["cn"]["w4"][:, :], 0.0).then_inc(s["cn_zeroed"], 1)
                dve.wait_ge(w_in, 64 if first else 96)
                nc.vector.tensor_copy(wqk[:, :, :].rearrange("p n (d h) -> p n d h", h=H),
                                      w[:, 0:2, :].rearrange("p n (h d) -> p n d h", d=D))
                nc.vector.tensor_copy(bqk_row[:, :, :].rearrange("p n (d h) -> p n d h", h=H),
                                      b_row[:, 0:2, :].rearrange("p n (h d) -> p n d h", d=D)).then_inc(const, 1)
                def layernorm(norms_of, base):
                    sources = [(src, t) for src, _, _ in norms_of for t in range(HT)]
                    r = rstd[:, 0:len(sources)]
                    token_moments(nc, dve, sources, work, r, ln, base)
                    for n, (src, dst, rdy) in enumerate(norms_of):
                        for t in range(HT):
                            k = HT * n + t
                            ins = nc.vector.tensor_scalar(dst[:, t, :], src(t), work["moments"][:, k, 0:1], rstd[:, k:k + 1],
                                                          ALU.subtract, ALU.mult)
                        ins.then_inc(rdy, 1)

                def norm_of_x(tiles, hf):
                    return (lambda t: s["x"][:, bass.ds(tiles + t, 1), :].rearrange("p o c -> p (o c)"), xs[hf], xs_rdy)

                def norm_of_xs(hf):
                    return (lambda t: xs[hf][:, t, :], hs[hf], hs_rdy)

                if first:
                    dve.wait_ge(s["x_first"], 16)
                    layernorm([norm_of_x(0, 0)], 0)
                AHEAD = HT + MOMENT_STEPS
                A_STEP = 2 * HT + MOMENT_STEPS

                def step(m, hf, tiles, own, late):
                    ahead = not (isinstance(m, int) and m >= 2 * B - 1)
                    if own and first:
                        dve.wait_ge(xs_rdy, m + 1)
                        reached(dve, trh_rdy, m - 1)
                        todo = [norm_of_xs(hf)]
                        if ahead:
                            reached(dve, trx_rdy, m)
                            reached(dve, xn_in, m)
                            if hf == 1:
                                dve.wait_ge(s["x_rest"], 16 * (B - 1))
                            todo.append(norm_of_x(tiles + HT, 1 - hf))
                        layernorm(todo, AHEAD + A_STEP * m)
                    elif own:
                        reached(dve, mean_ps, m - 1)
                        for t in range(HT):
                            tile = bass.ds(tiles + t, 1)
                            ins = nc.vector.tensor_scalar(
                                xs[hf][:, t, :], s["x"][:, tile, :].rearrange("p o c -> p (o c)"), s["mean"][:, tile],
                                s["rstd"][:, tile], ALU.subtract, ALU.mult)
                        ins.then_inc(xs_rdy, 1)
                    if isinstance(m, int) and m == 0:
                        weights()
                    if late:
                        l, n = m - 1, 1 - hf
                        part = [parts[n][:, :, z, :] for z in range(3)]
                        dve.wait_ge(part0_rdy, l + 1)
                        reached(dve, parts_rdy, l)
                        nc.vector.tensor_tensor(rest[:, :, :], qk[n][:, :, :], part[0], ALU.subtract).then_inc(rest_rdy, 1)
                        dve.wait_ge(v_ps, l + 1)
                        nc.vector.tensor_tensor(s["v"][:, bass.ds(tiles - HT, HT), :, 0:D],
                                                pv[:, :].rearrange("p (t h d) -> p t h d", t=HT, d=D),
                                                bv[:, :, :].rearrange("p t (h d) -> p t h d", d=D), ALU.add).then_inc(v_in, 1)
                        if not first:
                            dve.wait_ge(mean_ps, l + 1)
                            nc.vector.tensor_copy(s["xn_sums"][:, bass.ds(l, 1)], (py, tr_h)[n][:, 0:1]).then_inc(mean_in, 1)
                        dve.wait_ge(norm_ps, l + 1)
                        nc.vector.reduce_max(norms[:, bass.ds(l, 1)], pn[0:2 * KN, :], axis=AX.X).then_inc(norm_in, 1)
                        dve.wait_ge(part1_rdy, l + 1)
                        nc.vector.tensor_tensor(part[2], rest[:, :, :], part[1], ALU.subtract).then_inc(parts_rdy, 1)

                def weights():
                    dve.wait_ge(bias_ps, 1)
                    if first:
                        nc.vector.tensor_copy(s["bo"][:, :, :], py[:, 0:2 * C].rearrange("p (n c) -> p n c", n=2))
                    for t in range(HT):
                        nc.vector.tensor_copy(bv[:, t, :], pv[:, 0:C])
                    nc.vector.tensor_scalar_mul(b_col[:, 0:1], pq[:, 0:1], SCALE)
                    nc.vector.tensor_copy(b_col[:, 1:2], pq[:, 1:2]).then_inc(bias_in, 1)
                    if first:
                        dve.wait_ge(wt_ps, 1)
                        nc.vector.tensor_copy(fc_t[:, :, :], pf[0][:, :].rearrange("p (n f) -> p n f", n=FC))
                        nc.vector.tensor_copy(proj_t[:, :, :], pf[1][:, :].rearrange("p (n f) -> p n f", n=FC)).then_inc(wt_in, 1)

                trips(dve, steps(step), runs_ahead=first)
                ch = Chain(dve, tail)
                dve.wait_ge(norm_in, 2 * B)
                ch.after(nc.vector.reduce_max(top[:, :], norms[:, :], axis=AX.X))
                dve.wait_ge(tail_ps, 1)
                ch.after(nc.vector.tensor_copy(peak[:, :], tr_x[0:1, 0:2 * KN]))
                ch.after(nc.vector.tensor_tensor(peak[:, 0:H], peak[:, 0:H], peak[:, KN:KN + H], ALU.mult))
                ch.after(nc.vector.reduce_max(peak[:, H:H + 1], peak[:, 0:H], axis=AX.X))
                ch.after(nc.vector.tensor_scalar(s["flag"][:, :], peak[:, H:H + 1], BOUND * BOUND, None, ALU.is_gt))

            @block.tensor
            def _(pe):
                pe.wait_ge(const, 2)
                for n in range(2):
                    nc.tensor.matmul(pq[:, n:n + 1], bqk_row[:, n, :], ones[0:1, 0:1], start=True, stop=True)
                if first:
                    pe.wait_ge(bo_in, 32)
                    nc.tensor.matmul(py[:, 0:2 * C], ones[0:1, :], bo_row[:, :, :].rearrange("o n c -> o (n c)"), start=True, stop=True)
                nc.tensor.matmul(pv[:, 0:C], ones[0:1, :], b_row[:, 2, :], start=True, stop=True).then_inc(bias_ps, 1)
                if first:
                    pe.wait_ge(s["made"], 1)
                    pe.wait_ge(ffn_in, 32)
                    for n in range(FC):
                        nc.tensor.transpose(pf[0][:, n * P:(n + 1) * P], fc[:, n, :], s["ident"][:, :])
                    for n in range(FC):
                        ins = nc.tensor.transpose(pf[1][:, n * P:(n + 1) * P], proj[:, n * P:(n + 1) * P], s["ident"][:, :])
                    ins.then_inc(wt_ps, 1)

                def step(m, hf, tiles, own, late):
                    def chunks(fs):
                        for f in fs:
                            reached(pe, relu_in, FC * m + f - 1)
                            nc.tensor.matmul(pf[f % 2][:, :], fc_t[:, f, :], x_ch[hf][:, :], start=True, stop=True).then_inc(f_ps, 1)

                    if own:
                        pe.wait_ge(xs_rdy, m + 1)
                        reached(pe, xch_rdy, m)
                        for t in range(HT):
                            ins = nc.tensor.transpose(tr_x[:, t * P:(t + 1) * P], xs[hf][:, t, :], s["ident"][:, :])
                        ins.then_inc(trx_rdy, 1)
                        if not first:
                            reached(pe, mean_in, m - 1)
                            for t in range(HT):
                                ins = nc.tensor.matmul((py, tr_h)[hf][:, 0:1], xs[hf][:, t, :], ones[:, 0:1], start=t == 0,
                                                       stop=t == HT - 1)
                            ins.then_inc(mean_ps, 1)
                        if first:
                            pe.wait_ge(hs_rdy, m + 1)
                            reached(pe, hch_rdy, m)
                            for t in range(HT):
                                ins = nc.tensor.transpose(tr_h[:, t * P:(t + 1) * P], hs[hf][:, t, :], s["ident"][:, :])
                            ins.then_inc(trh_rdy, 1)
                    if isinstance(m, int) and m == 0:
                        pe.wait_ge(bias_in, 1)
                        pe.wait_ge(perm, D)
                        if first:
                            pe.wait_ge(wt_in, 1)
                    if late:
                        l, n = m - 1, 1 - hf
                        pe.wait_ge(sq_rdy, l + 1)
                        if not first:
                            reached(pe, norm_in, l)
                        for z in range(2):
                            ins = nc.tensor.matmul(pn[KN * z:KN * z + KN, :], head_of[:, :], square[n][:, z, :],
                                                   start=True, stop=True, tile_position=(0, KN * z))
                        ins.then_inc(norm_ps, 1)
                    if own:
                        if first:
                            pe.wait_ge(xch_rdy, m + 1)
                            chunks((0, 1))
                        pe.wait_ge(hch_rdy, m + 1)
                        if first:
                            reached(pe, norm_in, m)
                        nc.tensor.matmul(pq[:, :], wqk[:, 0, :], h_ch[hf][:, :], start=True, stop=True).then_inc(qk_ps, 1)
                        nc.tensor.matmul(pk[:, :], wqk[:, 1, :], h_ch[hf][:, :], start=True, stop=True).then_inc(qk_ps, 1)
                        reached(pe, v_in, m)
                        for t in range(HT):
                            ins = nc.tensor.matmul(pv[:, t * C:(t + 1) * C], h_ch[hf][:, t * P:(t + 1) * P], w[:, 2, :],
                                                   start=True, stop=True)
                        ins.then_inc(v_ps, 1)
                    if late and first:
                        l = m - 1
                        pe.wait_ge(hid_rdy, FC * l + FC)
                        reached(pe, y_in, l)
                        for t in range(HT):
                            for f in range(FC):
                                ins = nc.tensor.matmul(py[:, t * C:(t + 1) * C], hidden[:, f, t * P:(t + 1) * P],
                                                       proj_t[:, f, :], start=f == 0, stop=f == FC - 1)
                        ins.then_inc(y_ps, 1)
                    if own and first:
                        chunks((2, 3))

                trips(pe, steps(step))
                pe.wait_ge(tail, 1)
                nc.tensor.matmul(tr_x[0:1, 0:2 * KN], top[:, :], s["ident"][0:2 * KN, 0:2 * KN], start=True,
                                 stop=True).then_inc(tail_ps, 1)
        if first:
            sem.wiped()


def load_stacks(sp, q_rows, k_rows, q_st, k_st, b, g, sem):
    for rows, st in ((q_rows, q_st), (k_rows, k_st)):
        by_head = rows.rearrange("r (g j i) t -> r g j i t", j=G // 2, i=2)
        for i in range(2):
            sp.dma_start(st[64 * i:64 * i + ROWS, :, :],
                         by_head[:, bass.ds(g, 1), :, i, bass.ds(T * b, T)].rearrange("r o j t -> r (o j) t")).then_inc(sem, 16)


def row_maxima(nc, a, s, layer, q_rows, k_rows):
    causal = layer == 1
    with ExitStack() as ctx:
        def sb(name, shape, dt=F32):
            return ctx.enter_context(nc.sbuf_tensor(f"m{layer}_{name}", shape, dt))

        sem = Semaphores(nc, s["ctx"], f"m{layer}_")

        START = 1
        SLOTS = 4
        UNITS = BT * G
        q_st = [sb(f"q_st{n}", [P, G // 2, T], BF16) for n in range(2)]
        k_st = [sb(f"k_st{n}", [P, G // 2, T], BF16) for n in range(2)]
        maxima = sb("maxima", [P, NT, H])
        base = sb("base", [P, BT, H])
        parts = sb("parts", [P, NT, P // H, H], BF16)
        rows = sb("rows", [3 * H, N], BF16)
        sc = [ctx.enter_context(nc.psum_tensor(f"m{layer}_sc{n}", [P, T], F32)) for n in range(SLOTS)]
        staged = [sem(f"staged{n}") for n in range(2)]
        used = [sem(f"used{n}") for n in range(2)]
        scored, base_in, split, turned, row_in, out = (sem(x) for x in (
            "scored", "base_in", "split", "turned", "row_in", "out"))
        reduced = [sem(f"reduced{n}") for n in range(SLOTS)]

        with nc.Block() as block:
            @block.sync
            def _(sp):
                for hf in range(2):
                    sp.wait_ge(s[f"stored{layer}{hf}"], 96 * B)
                with sp.If(sp.value_load(s["flag"][0:1, 0:1], min_val=0, max_val=1) > 0):
                    sp.dma_start(base[:, :, :], a["q_shift"][layer]).then_inc(base_in, 16)
                    with sp.Fori(0, B) as b:
                        with sp.Fori(0, NG // 2) as gg:
                            for n in range(2):
                                sp.wait_ge(used[n], START + 2 * b + gg)
                                load_stacks(sp, q_rows, k_rows, q_st[n], k_st[n], b, 2 * gg + n, staged[n])
                    sp.wait_ge(row_in, START + NT)
                    sp.dma_start(q_rows[SPLIT_ROWS:SPLIT_ROWS + 3, :, :].rearrange("r h t -> (r h) t"),
                                 rows[:, :]).then_inc(out, 16)
                    sp.wait_ge(out, 16)
                with sp.Else():
                    sp.nop()

            @block.tensor
            def _(pe):
                with pe.If(pe.value_load(s["flag"][0:1, 0:1], min_val=0, max_val=1) > 0):
                    for n in range(2):
                        pe.sem_inc(used[n], START)
                    with pe.Fori(0, B) as b:
                        with pe.Fori(0, NG // 2) as gg:
                            trip = 2 * b + gg
                            for n in range(2):
                                pe.wait_ge(staged[n], 64 * trip + 64)
                                for u in range(UNITS):
                                    qt, pair, i = u // G, u % G // 2, u % 2
                                    width = (qt + 1) * P if causal else T
                                    slot = u % SLOTS
                                    per_trip = 2 * UNITS // SLOTS
                                    pe.wait_ge(reduced[slot], START + per_trip * trip + (n * UNITS + u) // SLOTS)
                                    part = slice(64 * i, 64 * i + ROWS)
                                    for k0 in range(0, width, HALF):
                                        k1 = min(width, k0 + HALF)
                                        diagonal = causal and k1 == width
                                        ins = nc.tensor.matmul(sc[slot][:, k0:k1], q_st[n][part, pair, qt * P:(qt + 1) * P],
                                                               k_st[n][part, pair, k0:k1], start=True, stop=not diagonal)
                                        if diagonal:
                                            ins = nc.tensor.matmul(sc[slot][:, k1 - P:k1], s["ident_bf"][:, :],
                                                                   s["mask_qk"][:, :], start=False, stop=True)
                                    if u == UNITS - 1:
                                        ins.then_inc(used[n], 1)
                                        pe.wait_ge(used[n], START + trip + 1)
                                        pe.sem_inc(scored, 1)
                                    else:
                                        ins.then_inc(scored, 1)
                    with pe.Fori(0, NT) as t:
                        pe.wait_ge(split, 6)
                        pe.wait_ge(row_in, START + t)
                        nc.tensor.transpose(sc[0][:, 0:P // 2].bitcast(BF16),
                                            parts[:, bass.ds(t, 1), :, :].rearrange("p o r h -> p (o r h)"),
                                            s["ident_bf"][:, :]).then_inc(turned, 1)
                with pe.Else():
                    pe.nop()

            @block.vector
            def _(dve):
                with dve.If(dve.value_load(s["flag"][0:1, 0:1], min_val=0, max_val=1) > 0):
                    dve.sem_inc(row_in, START)
                    for n in range(SLOTS):
                        dve.sem_inc(reduced[n], START)
                    with dve.Fori(0, B) as b:
                        with dve.Fori(0, NG // 2) as gg:
                            for n in range(2):
                                for u in range(UNITS):
                                    qt, head = u // G, u % G
                                    width = (qt + 1) * P if causal else T
                                    dve.wait_ge(scored, 2 * UNITS * (2 * b + gg) + n * UNITS + u + 1)
                                    nc.vector.reduce_max(
                                        maxima[:, bass.ds(BT * b + qt, 1), bass.ds(2 * G * gg + G * n + head, 1)],
                                        sc[u % SLOTS][:, 0:width], axis=AX.X).then_inc(reduced[u % SLOTS], 1)
                    dve.wait_ge(base_in, 16)
                    for n in range(SLOTS):
                        dve.wait_ge(reduced[n], START + B * NG * UNITS // SLOTS)
                    ch = Chain(dve, split)
                    ch.mark(nc.vector.memset(parts[:, :, 3:, :], 0.0))
                    for b in range(B):
                        tiles = slice(b * BT, (b + 1) * BT)
                        ins = nc.vector.tensor_tensor(maxima[:, tiles, :], base[:, :, :], maxima[:, tiles, :], ALU.subtract)
                    ch.after(ins)
                    ch.after(nc.vector.tensor_copy(parts[:, :, 0, :], maxima[:, :, :]))
                    ch.after(nc.vector.tensor_tensor(maxima[:, :, :], maxima[:, :, :], parts[:, :, 0, :], ALU.subtract))
                    ch.after(nc.vector.tensor_copy(parts[:, :, 1, :], maxima[:, :, :]))
                    ch.after(nc.vector.tensor_tensor(parts[:, :, 2, :], maxima[:, :, :], parts[:, :, 1, :], ALU.subtract))
                    with dve.Fori(0, NT) as t:
                        dve.wait_ge(turned, t + 1)
                        nc.vector.tensor_copy(rows[:, bass.ds(P * t, P)], sc[0][0:3 * H, 0:P // 2].bitcast(BF16)).then_inc(row_in, 1)
                with dve.Else():
                    dve.nop()


def attention(nc, a, s, layer, q_rows, k_rows, out_t):
    causal = layer == 1
    first = layer == 0
    LAG = 2 if first else 4
    WARM_UP = 6
    halves = [[(kt, max(kt * P - qh * HALF, 0) if causal else 0) for kt in range(BT)] for qh in range(2)]
    halves = [[(kt, q0) for kt, q0 in half if q0 < HALF] for half in halves]
    groups = [(qh, kt, q0, kt == half[0][0], kt == half[-1][0]) for qh, half in enumerate(halves) for kt, q0 in half]
    L = len(groups)
    S = NG * L
    ends = [g * L + j for g in range(NG) for j in range(L) if groups[j][4]]
    ENDS = len(ends)
    jobs = []
    for k, end in enumerate(ends):
        jobs.append((end + LAG + 2, "turn", k))
        if k >= ENDS - 2:
            jobs.append((end + LAG + 3, "back", k - (ENDS - 2)))
            jobs.append((end + LAG + 4, "mix", k - (ENDS - 2)))
    JOBS = len(jobs)
    norm_steps = [at + 3 for at, kind, _ in jobs if kind == "mix"] if first else []
    TAIL = max([jobs[-1][0]] + norm_steps) - S + 1
    GATE_ENDS = [ends[2], ends[4]]
    LINKS = ENDS + 4
    SPIKE_STEPS = 3 * (STEPS - 1) + 1

    def turn_index(k):
        return next(i for i, (_, kind, n) in enumerate(jobs) if (kind, n) == ("turn", k))

    def jobs_at(step):
        return [(index, kind, k) for index, (at, kind, k) in enumerate(jobs) if at == step]

    with ExitStack() as ctx:
        def sb(name, shape, dt=F32):
            return ctx.enter_context(nc.sbuf_tensor(f"a{layer}_{name}", shape, dt))

        sem = Semaphores(nc, s["ctx"], f"a{layer}_")

        SC, PR = 3, 2 * LAG
        q_st = [sb(f"q_st{n}", [P, G // 2, T], BF16) for n in range(2)]
        k_st = [sb(f"k_st{n}", [P, G // 2, T], BF16) for n in range(2)]
        v_st = [sb(f"v_st{n}", [P, BT, G, VW]) for n in range(2)]
        probs = [sb(f"probs{n}", [P, G, HALF]) for n in range(PR)]
        o_sb = [sb(f"o_sb{n}", [P, HALF]) for n in range(2)]
        recip = sb("recip", [P, HT, G])
        tok = sb("tok", [P, BT, C])
        chan = sb("chan", [P, HALF])
        gate = sb("gate", [P, BT, C])
        mix = [sb(f"mix{n}", [P, HT, C]) for n in range(2)]
        scores = [ctx.enter_context(nc.psum_tensor(f"a{layer}_sc{n}", [P, 2, HALF], F32)) for n in range(SC)]
        o_ps = ctx.enter_context(nc.psum_tensor(f"a{layer}_o", [P, HALF], F32))
        job_ps = ctx.enter_context(nc.psum_tensor(f"a{layer}_job", [P, HALF], F32))
        if first:
            mem = [sb(f"mem{n}", [P, 2, C]) for n in range(2)]
            count = sb("count", [P, 2, C])
            work = moment_tiles(sb, HT)
        gate_in, gate_scale = (s["y"], 1.0 / STEPS) if first else (s["xn"], 1.0)
        staged = sem.pair("staged")
        scored = sem("scored")
        exp_done = sem.many("exp_done", SC)
        pv_done = sem.many("pv_done", PR)
        o_clear = sem("o_clear")
        o_in = sem("o_in")
        job_rdy, job_read = sem("job_rdy"), sem("job_read")
        spikes, exped, glink, gated = (sem(x) for x in ("spikes", "exped", "glink", "gated"))
        scaled, updated, moment = sem("scaled"), sem("updated"), sem("moment")
        stored = sem.pair("stored")

        UNITS = 2 * S

        def exp_count(unit, b):
            return len(range(unit % SC, UNITS, SC)) * b + unit // SC + 1

        def pv_count(group, b):
            return S // PR * b + group // PR + 1

        with nc.Block() as block:
            @block.sync
            def _(sp):
                def load(b, g):
                    n = g % 2
                    group = ((g - 2) * L + L - 1) % S
                    reached(sp, pv_done[group % PR], pv_count(group, b) - (S // PR if g < 2 else 0))
                    load_stacks(sp, q_rows, k_rows, q_st[n], k_st[n], b, g, staged[n])
                    sp.dma_start(v_st[n][:, :, :, :], s["v"][:, bass.ds(BT * b, BT), G * g:G * g + G, :]).then_inc(staged[n], 16)

                def trip(b, own, late):
                    if own:
                        load(b, 0)
                        load(b, 1)
                    if late and not first:
                        for hf in range(2):
                            sp.wait_ge(updated, 2 * b - 1 + hf)
                            tiles = bass.ds(BT * b + HT * hf - BT, HT)
                            sp.dma_start(out_t[:, tiles, :], s["x"][:, tiles, :]).then_inc(stored[hf], 16)
                    if own:
                        load(b, 2)
                        load(b, 3)

                trips(sp, trip)
                if not first:
                    for hf in range(2):
                        sp.wait_ge(stored[hf], 16 * B)

            @block.scalar
            def _(act):
                def trip(b, own, late):
                    if not own:
                        return
                    for j in range(S):
                        qh, kt, q0, _, _ = groups[j % L]
                        reached(act, pv_done[j % PR], pv_count(j, b) - 1)
                        for pair in range(2):
                            unit = 2 * j + pair
                            act.wait_ge(scored, UNITS * b + unit + 1)
                            nc.scalar.activation(probs[j % PR][:, 2 * pair:2 * pair + 2, 0:HALF - q0],
                                                 scores[unit % SC][:, :, 0:HALF - q0], ACT.Exp).then_inc(exp_done[unit % SC], 1)
                        if j in GATE_ENDS:
                            hf = GATE_ENDS.index(j)
                            if first:
                                act.wait_ge(spikes, NG * SPIKE_STEPS * b + NG // 2 * SPIKE_STEPS * (hf + 1))
                            reached(act, updated, 2 * b)
                            nc.scalar.activation(gate[:, HT * hf:HT * hf + HT, :], gate_in[:, bass.ds(BT * b + HT * hf, HT), :],
                                                 ACT.Exp, scale=-gate_scale).then_inc(exped, 1)

                trips(act, trip)

            @block.gpsimd
            def _(pool):
                def update(b, hf):
                    index = next(i for i, (_, kind, k) in enumerate(jobs) if (kind, k) == ("mix", hf))
                    pool.wait_ge(job_read, JOBS * b + index + 1)
                    pool.wait_ge(gated, 2 * b + hf + 1)
                    pool.tensor_tensor(mix[hf][:, :, :], mix[hf][:, :, :], gate[:, HT * hf:HT * hf + HT, :],
                                       ALU.mult).then_inc(scaled, 1)
                    pool.wait_ge(scaled, 2 * b + hf + 1)
                    x = s["x"][:, bass.ds(BT * b + HT * hf, HT), :]
                    pool.tensor_tensor(x, x, mix[hf][:, :, :], ALU.add).then_inc(updated, 1)

                def trip(b, own, late):
                    if late:
                        update(b - 1, 1)
                    if own:
                        update(b, 0)

                trips(pool, trip)

            @block.vector
            def _(dve):
                nc.vector.memset(o_ps[:, :], 0.0).then_inc(o_clear, 1)

                def finish_gate(b, hf):
                    part = gate[:, HT * hf:HT * hf + HT, :]
                    done = LINKS * b + (2 if hf == 0 else 6)
                    dve.wait_ge(exped, 2 * b + hf + 1)
                    nc.vector.tensor_scalar_add(part, part, 1.0).then_inc(glink, 1)
                    dve.wait_ge(glink, done + 1)
                    nc.vector.reciprocal(part, part).then_inc(glink, 1)
                    dve.wait_ge(glink, done + 2)
                    nc.vector.scalar_tensor_tensor(part, gate_in[:, bass.ds(BT * b + HT * hf, HT), :], gate_scale, part,
                                                   ALU.mult, ALU.mult).then_inc(gated, 1)

                def step(b, at):
                    for k, end in enumerate(ends):
                        if at == end + LAG:
                            dve.wait_ge(pv_done[end % PR], pv_count(end, b))
                            if k >= 2:
                                dve.wait_ge(job_rdy, JOBS * b + turn_index(k - 2) + 1)
                            else:
                                reached(dve, job_rdy, JOBS * b + turn_index(ENDS + k - 2) + 1 - JOBS)
                            nc.vector.tensor_copy(o_sb[k % 2][:, :], o_ps[:, :]).then_inc(o_in, 1)
                            if end in GATE_ENDS:
                                finish_gate(b, GATE_ENDS.index(end))
                    for index, kind, k in jobs_at(at):
                        dve.wait_ge(job_rdy, JOBS * b + index + 1)
                        if kind == "turn":
                            g, qh = k // 2, k % 2
                            heads = job_ps[:, :].rearrange("p (t h w) -> p t h w", t=HT, w=32)
                            nc.vector.reciprocal(recip[:, :, :], heads[:, :, :, D]).then_inc(glink, 1)
                            dve.wait_ge(glink, LINKS * b + k + 1 + 2 * (k >= 2) + 2 * (k >= 4))
                            nc.vector.tensor_tensor(
                                tok[:, HT * qh:HT * qh + HT, G * D * g:G * D * g + G * D].rearrange("p t (h d) -> p t h d", d=D),
                                heads[:, :, :, 0:D],
                                recip[:, :, :].rearrange("p t (h o) -> p t h o", o=1).broadcast_to([P, HT, G, D]),
                                ALU.mult).then_inc(job_read, 1)
                            if first and k < NG:
                                spike(nc, dve, s["y"][:, bass.ds(BT * b + 2 * k, 2), :], mem, count, spikes,
                                      SPIKE_STEPS * (NG * b + k))
                        elif kind == "back":
                            nc.vector.tensor_copy(chan[:, :], job_ps[:, :]).then_inc(job_read, 1)
                        else:
                            reached(dve, updated, 2 * b + k - 1)
                            skip = (s["xn"][:, bass.ds(BT * b + HT * k, HT), :] if first
                                    else s["bo"][:, 1:2, :].broadcast_to([P, HT, C]))
                            nc.vector.tensor_tensor(mix[k][:, :, :], job_ps[:, :].rearrange("p (t c) -> p t c", c=C),
                                                    skip, ALU.add).then_inc(job_read, 1)
                    if at in norm_steps:
                        hf = norm_steps.index(at)
                        dve.wait_ge(updated, 2 * b + hf + 1)
                        tiles = BT * b + HT * hf
                        token_moments(nc, dve, [(lambda t: s["x"][:, bass.ds(tiles + t, 1), :].rearrange("p o c -> p (o c)"), t)
                                                for t in range(HT)],
                                      work, s["rstd"][:, bass.ds(tiles, HT)], moment, (HT + MOMENT_STEPS) * (2 * b + hf))
                        nc.vector.tensor_copy(s["mean"][:, bass.ds(tiles, HT)], work["moments"][:, :, 0])

                def trip(b, own, late):
                    for at in range(S if own else TAIL):
                        if late:
                            step(b - 1, at + S)
                        if own:
                            step(b, at)

                trips(dve, trip)

            @block.tensor
            def _(pe):
                for _ in range(WARM_UP):
                    nc.tensor.matmul(job_ps[:, :], s["ident"][:, :], s["x"][:, 0:HT, :].rearrange("p t c -> p (t c)"),
                                     start=True, stop=True)
                pe.wait_ge(o_clear, 1)

                def score(b, j):
                    g, n = j // L, j // L % 2
                    qh, kt, q0, _, _ = groups[j % L]
                    if j % L == 0:
                        pe.wait_ge(staged[n], 160 * b + 80 * (g // 2) + 80)
                    diagonal = causal and kt // HT == qh
                    for pair in range(2):
                        unit = 2 * j + pair
                        slot = unit % SC
                        reached(pe, exp_done[slot], exp_count(unit, b) - 1)
                        for i in range(2):
                            part = slice(64 * i, 64 * i + ROWS)
                            ins = nc.tensor.matmul(scores[slot][:, i, 0:HALF - q0], k_st[n][part, pair, kt * P:(kt + 1) * P],
                                                   q_st[n][part, pair, qh * HALF + q0:(qh + 1) * HALF],
                                                   start=True, stop=not diagonal)
                        if diagonal:
                            for i in range(2):
                                ins = nc.tensor.matmul(scores[slot][:, i, 0:P], s["ident_bf"][:, :], s["mask_kq"][:, :],
                                                       start=False, stop=True)
                        ins.then_inc(scored, 1)

                def product(b, j):
                    n = j // L % 2
                    qh, kt, q0, opens, closes = groups[j % L]
                    pe.wait_ge(exp_done[(2 * j + 1) % SC], exp_count(2 * j + 1, b))
                    if opens:
                        reached(pe, o_in, ENDS * b + 2 * (j // L) + qh)
                    for h in range(G):
                        ins = nc.tensor.matmul(o_ps[32 * h:32 * h + VW, q0:HALF], v_st[n][:, kt, h, :],
                                               probs[j % PR][:, h, 0:HALF - q0], start=opens, stop=closes,
                                               tile_position=(0, 32 * h))
                    ins.then_inc(pv_done[j % PR], 1)

                def job(b, index, kind, k):
                    reached(pe, job_read, JOBS * b + index)
                    if kind == "turn":
                        pe.wait_ge(o_in, ENDS * b + k + 1)
                    for t in range(HT):
                        tile = slice(t * P, (t + 1) * P)
                        if kind == "turn":
                            ins = nc.tensor.transpose(job_ps[:, tile], o_sb[k % 2][:, tile], s["ident"][:, :])
                        elif kind == "back":
                            ins = nc.tensor.transpose(job_ps[:, tile], tok[:, HT * k + t, :], s["ident"][:, :])
                        else:
                            ins = nc.tensor.matmul(job_ps[:, tile], chan[:, tile], s["wo"][:, layer, :], start=True, stop=True)
                    ins.then_inc(job_rdy, 1)

                def trip(b, own, late):
                    for at in range(S if own else TAIL):
                        if own:
                            score(b, at)
                        if at >= LAG and own:
                            product(b, at - LAG)
                        if at < LAG and late:
                            product(b - 1, at - LAG + S)
                        if late:
                            for one in jobs_at(at + S):
                                job(b - 1, *one)
                        if own:
                            for one in jobs_at(at):
                                job(b, *one)

                trips(pe, trip)


def spike(nc, dve, y, mem, count, sem, base):
    ch = Chain(dve, sem, base)
    m0 = y
    ch.after(nc.vector.tensor_scalar(count[:, :, :], y, 1.0, None, ALU.is_gt))
    for step in range(1, STEPS):
        m1 = mem[step % 2]
        ch.after(nc.vector.scalar_tensor_tensor(m1[:, :, :], m0, BETA, y, ALU.mult, ALU.add))
        ch.after(nc.vector.scalar_tensor_tensor(m1[:, :, :], m0, 1.0, m1[:, :, :], ALU.is_gt, ALU.subtract, reverse1=True))
        last = step == STEPS - 1
        ch.after(nc.vector.scalar_tensor_tensor(y if last else count[:, :, :], m1[:, :, :], 1.0, count[:, :, :],
                                                ALU.is_gt, ALU.add))
        m0 = m1[:, :, :]


def load_coupling_weights(sp, a, s):
    cn = s["cn"]

    def column(name):
        return a[name].rearrange("(c o) -> c o", o=1)

    loads = [(cn["g1"][:, :], a["L1_ffn_gc_w1"]), (cn["g2"][:, :], a["L1_ffn_gc_w2"]),
             (cn["g3"][:, :], a["L1_ffn_gc_w3"]), (cn["gb1"][:, :], column("L1_ffn_gc_b1")),
             (cn["gb2"][:, :], column("L1_ffn_gc_b2")), (cn["scalars"][:, 0:1], column("L1_ffn_cn_b4")),
             (cn["scalars"][:, 1:2], column("L1_ffn_gc_b3")), (cn["scalars"][:, 2:3], column("L1_ffn_adaptive_range")),
             (cn["w1"][:, :], a["L1_ffn_cn_w1"]), (cn["w2"][:, :], a["L1_ffn_cn_w2"]), (cn["b1"][:, :], column("L1_ffn_cn_b1"))]
    for hf in range(2):
        wide, narrow = slice(H1 * hf, H1 * hf + H1), slice(H2 * hf, H2 * hf + H2)
        loads += [(cn["w3"][wide, narrow], a["L1_ffn_cn_w3"]), (cn["w4"][narrow, hf:hf + 1], a["L1_ffn_cn_w4"]),
                  (cn["b2"][wide, :], column("L1_ffn_cn_b2")), (cn["b3"][narrow, :], column("L1_ffn_cn_b3"))]
    assert len(loads) == COUPLING_LOADS
    for dst, src in loads:
        sp.dma_start(dst, src).then_inc(s["cn_in"], 16)


def coupling(nc, a, s):
    with ExitStack() as ctx:
        def sb(name, shape, dt=F32):
            return ctx.enter_context(nc.sbuf_tensor(f"n_{name}", shape, dt))

        sem = Semaphores(nc, s["ctx"], f"n_")

        Q = P // 4
        w1, w2, w3, w4, b1, b2, b3, g1, g2, g3, gb1, gb2, scalars = (s["cn"][name] for name in (
            "w1", "w2", "w3", "w4", "b1", "b2", "b3", "g1", "g2", "g3", "gb1", "gb2", "scalars"))
        w4_all, g3_all = sb("w4_all", [2 * H2, 2, P]), sb("g3_all", [H2, P])
        ones = sb("ones", [1, P])
        col = sb("col", [P, 8])
        mean = sb("mean", [P, B])
        u1, u2 = sb("gu1", [H1, B]), sb("gu2", [H2, B])
        gf = sb("gf", [P, B])
        offset = sb("offset", [P, B])
        h1 = [[sb(f"h1_{z}{hf}", [C, HALF]) for hf in range(2)] for z in range(2)]
        h2 = [sb(f"h2_{z}", [2 * H1, HALF]) for z in range(2)]
        h3 = [sb(f"h3_{z}", [2 * H2, HALF]) for z in range(2)]
        th = [[sb(f"th{z}{hf}", [P, HALF]) for hf in range(2)] for z in range(2)]
        change = [[sb(f"change{z}{hf}", [P, HALF]) for hf in range(2)] for z in range(2)]
        ps = [[ctx.enter_context(nc.psum_tensor(f"n_ps{z}_{k}", [P, HALF], F32)) for k in range(4)] for z in range(2)]
        const, gps, gact, chain, gready = (sem(x) for x in ("const", "gps", "gact", "chain", "gready"))
        layered, squashed = sem("layered"), sem("squashed")
        coupled, twisted, updated = sem.pair("coupled"), sem("twisted"), sem("updated")
        turned, kept = sem("turned"), sem("kept")
        xt = s["y"][:, :, :].rearrange("p t c -> p (t c)")
        LAYERED, TWISTED = 12, 4
        PAIRS = B // 2

        def layer_index(layer, z, hf=0):
            return {1: 2 * z + hf, 2: 4 + z, 3: 6 + z, 4: 8 + 2 * z + hf}[layer]

        def layer_count(c, pair, index):
            return LAYERED * PAIRS * c + LAYERED * pair + index + 1

        def twist_count(c, pair, z, hf):
            return TWISTED * PAIRS * c + TWISTED * pair + 2 * z + hf + 1

        def state(pair, z, hf):
            at = (2 * pair + z) * T + HALF * hf
            return xt[:, at:at + HALF]

        with nc.Block() as block:
            @block.gpsimd
            def _(pool):
                def cycle(c):
                    for pair in range(PAIRS):
                        for z in range(2):
                            for hf in range(2):
                                pool.wait_ge(twisted, twist_count(c, pair, z, hf))
                                out = state(pair, z, hf)
                                pool.tensor_tensor(out, out, change[z][hf][:, :], ALU.add).then_inc(updated, 1)

                after_first(pool, CYCLES, cycle)

            @block.scalar
            def _(act):
                act.wait_ge(gps, 1)
                nc.scalar.activation(u1[:, :], ps[0][0][0:H1, 0:B], ACT.Gelu, bias=gb1[:, :]).then_inc(gact, 1)
                act.wait_ge(gps, 2)
                nc.scalar.activation(u2[:, :], ps[0][1][0:H2, 0:B], ACT.Gelu, bias=gb2[:, :]).then_inc(gact, 1)
                act.wait_ge(gps, 3)
                act.wait_ge(gready, 1)
                nc.scalar.activation(gf[:, :], ps[0][2][:, 0:B], ACT.Tanh, bias=col[:, 1:2], scale=0.5).then_inc(gact, 1)

                def cycle(c):
                    for pair in range(PAIRS):
                        for z in range(2):
                            for hf in range(2):
                                act.wait_ge(layered, layer_count(c, pair, layer_index(1, z, hf)))
                                nc.scalar.activation(h1[z][hf][:, :], ps[z][hf][:, :], ACT.Gelu, bias=b1[:, :]).then_inc(squashed, 1)
                        for z in range(2):
                            act.wait_ge(layered, layer_count(c, pair, layer_index(2, z)))
                            nc.scalar.activation(h2[z][:, :], ps[z][2][:, :], ACT.Gelu, bias=b2[:, :]).then_inc(squashed, 1)
                        for z in range(2):
                            act.wait_ge(layered, layer_count(c, pair, layer_index(3, z)))
                            nc.scalar.activation(h3[z][:, :], ps[z][3][0:2 * H2, :], ACT.Gelu, bias=b3[:, :]).then_inc(squashed, 1)
                        for z in range(2):
                            for hf in range(2):
                                act.wait_ge(layered, layer_count(c, pair, layer_index(4, z, hf)))
                                reached(act, twisted, twist_count(c, pair, z, hf) - TWISTED)
                                nc.scalar.activation(th[z][hf][:, :], ps[z][hf][:, :], ACT.Tanh, bias=col[:, 0:1],
                                                     scale=0.5).then_inc(squashed, 1)
                            for hf in range(2):
                                if z == 0:
                                    act.wait_ge(squashed, layer_count(c, pair, layer_index(4, z, hf)))
                                    act.wait_ge(gready, 2)
                                    nc.scalar.activation(th[z][hf][:, :], th[z][hf][:, :], ACT.Identity,
                                                         bias=offset[:, 2 * pair:2 * pair + 1],
                                                         scale=col[:, 5:6]).then_inc(coupled[0], 1)

                after_first(act, CYCLES, cycle)
                for k in range(2 * B):
                    act.wait_ge(turned, k + 1)
                    nc.scalar.copy(s["xn"][:, HT * k:HT * k + HT, :],
                                   ps[k % 2][k // 2 % 2][:, :].rearrange("p (t c) -> p t c", c=C)).then_inc(kept, 1)

            @block.vector
            def _(dve):
                ch = Chain(dve, chain)
                nc.vector.memset(ones[:, :], 1.0).then_inc(const, 1)
                ch.after(nc.vector.reduce_sum(mean[:, :], s["xn_sums"][:, :].rearrange("p (b t) -> p b t", b=B), axis=AX.X))
                ch.mark(nc.vector.tensor_scalar_mul(mean[:, :], mean[:, :], 1.0 / T))
                dve.wait_ge(s["cn_in"], 16 * COUPLING_LOADS)
                for hf in range(2):
                    ch.mark(nc.vector.tensor_copy(w4_all[:, hf, :], w4[:, hf:hf + 1].broadcast_to([2 * H2, P])))
                nc.vector.tensor_copy(g3_all[:, :], g3[:, :].broadcast_to([H2, P])).then_inc(const, 1)
                dve.wait_ge(gps, 3)
                ch.after(nc.vector.tensor_copy(col[:, 2:5], ps[0][3][:, 0:3]))
                ch.mark(nc.vector.tensor_scalar_mul(col[:, 0:2], col[:, 2:4], 0.5))
                ch.mark(nc.vector.tensor_scalar_mul(col[:, 5:6], col[:, 4:5], 0.3))
                nc.vector.tensor_scalar_mul(col[:, 6:7], col[:, 4:5], 2.0).then_inc(gready, 1)
                dve.wait_ge(gready, 1)
                ch.wait()
                dve.wait_ge(gact, 3)
                ch.after(nc.vector.tensor_scalar(offset[:, :], gf[:, :], 0.35, col[:, 6:7], ALU.mult, ALU.mult))
                nc.vector.tensor_scalar_add(offset[:, :], offset[:, :], 0.1).then_inc(gready, 1)
                dve.wait_ge(gready, 2)

                def cycle(c):
                    for pair in range(PAIRS):
                        for z in range(2):
                            for hf in range(2):
                                t, count = th[z][hf], twist_count(c, pair, z, hf)
                                if z == 1:
                                    dve.wait_ge(squashed, layer_count(c, pair, layer_index(4, z, hf)))
                                    nc.vector.tensor_scalar(t[:, :], t[:, :], col[:, 5:6], offset[:, 2 * pair + 1:2 * pair + 2],
                                                            ALU.mult, ALU.add).then_inc(coupled[1], 1)
                                dve.wait_ge(coupled[z], 2 * PAIRS * c + 2 * pair + hf + 1)
                                reached(dve, updated, count - TWISTED)
                                for dst, src, sign in ((0, 2, 1.0), (1, 3, -1.0), (2, 0, -1.0), (3, 1, 1.0)):
                                    r = slice(Q * src, Q * src + Q)
                                    ins = nc.vector.scalar_tensor_tensor(
                                        change[z][hf][Q * dst:Q * dst + Q, :], state(pair, z, hf)[r, :], sign, t[r, :],
                                        ALU.mult, ALU.mult)
                                ins.then_inc(twisted, 1)

                after_first(dve, CYCLES, cycle)

            @block.tensor
            def _(pe):
                pe.wait_ge(const, 2)
                pe.wait_ge(chain, 4)
                nc.tensor.matmul(ps[0][0][0:H1, 0:B], g1[:, :], mean[:, :], start=True, stop=True).then_inc(gps, 1)
                nc.tensor.matmul(ps[0][3][:, 0:3], ones[:, :], scalars[:, 0:3], start=True, stop=True)
                pe.wait_ge(gact, 1)
                nc.tensor.matmul(ps[0][1][0:H2, 0:B], g2[:, :], u1[:, :], start=True, stop=True).then_inc(gps, 1)
                pe.wait_ge(gact, 2)
                nc.tensor.matmul(ps[0][2][:, 0:B], g3_all[:, :], u2[:, :], start=True, stop=True).then_inc(gps, 1)
                pe.wait_ge(gact, 3)
                pe.wait_ge(gready, 1)

                def cycle(c):
                    for pair in range(PAIRS):
                        for z in range(2):
                            for hf in range(2):
                                reached(pe, squashed, layer_count(c, pair, layer_index(4, z, hf)) - LAYERED)
                                reached(pe, updated, twist_count(c, pair, z, hf) - TWISTED * PAIRS)
                                nc.tensor.matmul(ps[z][hf][:, :], w1[:, :], state(pair, z, hf), start=True, stop=True).then_inc(layered, 1)
                        for z in range(2):
                            pe.wait_ge(squashed, layer_count(c, pair, layer_index(1, z, 1)))
                            for hf in range(2):
                                ins = nc.tensor.matmul(ps[z][2][H1 * hf:H1 * hf + H1, :], w2[:, :], h1[z][hf][:, :],
                                                       start=True, stop=True, tile_position=(0, H1 * hf))
                            ins.then_inc(layered, 1)
                        for z in range(2):
                            pe.wait_ge(squashed, layer_count(c, pair, layer_index(2, z)))
                            nc.tensor.matmul(ps[z][3][0:2 * H2, :], w3[:, :], h2[z][:, :], start=True, stop=True).then_inc(layered, 1)
                        for z in range(2):
                            pe.wait_ge(squashed, layer_count(c, pair, layer_index(3, z)))
                            for hf in range(2):
                                nc.tensor.matmul(ps[z][hf][:, :], w4_all[:, hf, :], h3[z][:, :], start=True, stop=True).then_inc(layered, 1)

                after_first(pe, CYCLES, cycle)
                for k in range(2 * B):
                    if k >= 4:
                        pe.wait_ge(kept, k - 3)
                    else:
                        pe.wait_ge(updated, TWISTED * PAIRS * CYCLES - 4 + 2 * (k % 2) + k // 2 + 1)
                    pe.wait_ge(updated, TWISTED * PAIRS * (CYCLES - 1) + k + 1)
                    for t in range(HT):
                        ins = nc.tensor.transpose(ps[k % 2][k // 2 % 2][:, t * P:(t + 1) * P],
                                                  s["y"][:, HT * k + t, :], s["ident"][:, :])
                    ins.then_inc(turned, 1)


_INS = ["L0_attn_x", "L0_attn_ln_gamma", "L0_attn_ln_beta", "L0_attn_w_qkv", "L0_attn_b_qkv", "L0_attn_w_out",
        "L0_attn_b_out", "L0_ffn_W_fc", "L0_ffn_W_proj", "L1_attn_Wq", "L1_attn_bq", "L1_attn_Wk", "L1_attn_bk",
        "L1_attn_Wv", "L1_attn_bv", "L1_attn_Wo", "L1_attn_bo", "L1_ffn_cn_w1", "L1_ffn_cn_b1", "L1_ffn_cn_w2",
        "L1_ffn_cn_b2", "L1_ffn_cn_w3", "L1_ffn_cn_b3", "L1_ffn_cn_w4", "L1_ffn_cn_b4", "L1_ffn_gc_w1", "L1_ffn_gc_b1",
        "L1_ffn_gc_w2", "L1_ffn_gc_b2", "L1_ffn_gc_w3", "L1_ffn_gc_b3", "L1_ffn_adaptive_range"]


def position_rows():
    slopes = 2.0 ** (-8.0 * (np.arange(H) + 1) / H)
    shift = (slopes.astype(np.float32)[:, None] * (T - 1 - np.arange(T, dtype=np.float32))).astype(np.float32)
    q = np.zeros((2, ROWS - SPLIT_ROWS, H, T), np.uint16)
    k = np.zeros((2, ROWS - SPLIT_ROWS, H, T), np.uint16)
    q[:, 3:6], k[:, :3] = 0x3F80, 0x3F80
    rest = shift.copy()
    for n in range(3):
        part = rest.view(np.uint32) & np.uint32(0xFFFF0000)
        q[1, n], k[1, 3 + n] = part >> 16, (part >> 16) | (part != 0) * 0x8000
        rest = rest - part.view(np.float32)
    base = np.zeros((2, P, BT, H), np.float32)
    base[1] = shift.reshape(H, BT, P).transpose(2, 1, 0)
    return {"q_extra": q, "k_extra": k, "q_shift": base}


def kernel(**inputs):
    import concourse.bacc as _bacc
    from concourse.bass_utils import run_bass_kernel_spmd as _run

    nc = _bacc.Bacc("TRN2", target_bir_lowering=False, num_devices=1)
    arrays, args = {}, {}
    for name, value in [(n, inputs[n]) for n in _INS] + list(position_rows().items()):
        x = np.ascontiguousarray(value)
        arrays[f"in_{name}_dram"] = x
        args[name] = nc.dram_tensor(f"in_{name}_dram", x.shape, mybir.dt.from_np(x.dtype), kind="ExternalInput").ap()
    args["out"] = nc.dram_tensor("out_0_dram", (B, T, C), F32, kind="ExternalOutput").ap()
    build(nc, args)
    r = _run(nc, [arrays], core_ids=[0])
    return r.results[0]["out_0_dram"]
```
